# Optimizing a Trainium2 kernel written in Bass

```python
import numpy as np
import jax
import jax.numpy as jnp

def _softmax(x, axis=-1):
    return jax.nn.softmax(x, axis=axis)

def _gelu(x):
    return jax.nn.gelu(x, approximate=True)

def _silu(x):
    return jax.nn.silu(x)

def _sigmoid(x):
    return jax.nn.sigmoid(x)

def _layernorm(x, axis=-1, eps=1e-05):
    m = jnp.mean(x, axis=axis, keepdims=True)
    v = jnp.var(x, axis=axis, keepdims=True)
    return (x - m) / jnp.sqrt(v + eps)

def _scatter_add(tgt, idx, src, axis=0):
    return tgt.at[idx].add(src)

def _segment_sum(src, seg, n):
    return jax.ops.segment_sum(src, seg, n)
kernel_name = 'mk_gnn_resnorm_d2_gnn_r64_f5c081'

def setup_inputs(seed: int=0):
    np.random.seed(seed)
    _w = jnp.asarray

    def _rec_inputs():
        import jax
        import jax.numpy as jnp
        _gk = jax.random.key(seed)
        x = -0.0003713 + 1 * jax.random.normal(jax.random.fold_in(_gk, 1), (100000, 128), jnp.float32)
        src = jax.random.randint(jax.random.fold_in(_gk, 2), (50000,), 0, 100000, jnp.int32)
        dst = jax.random.randint(jax.random.fold_in(_gk, 3), (50000,), 0, 100000, jnp.int32)
        _o = jnp.argsort(dst, stable=True)
        src = src[_o]
        dst = dst[_o]
        edge_attr_64 = 0.000189758 + 1.00013 * jax.random.normal(jax.random.fold_in(_gk, 11), (50000, 64), jnp.float32)
        return (x, src, dst, edge_attr_64)
    x, src, dst, edge_attr_64 = _rec_inputs()

    def _L0_gnn_setup():
        import jax, jax.numpy as jnp
        import numpy as np
        N = 100000
        E = 25000
        D_IN = 128
        D_OUT = 128
        BN_EPS = 1e-05
        key = jax.random.key(seed)
        ks = jax.random.split(key, 8)
        x = jax.random.normal(ks[0], (N, D_IN), dtype=jnp.float32)
        edge_index = jax.random.randint(ks[1], (2, E), 0, N, dtype=jnp.int64)
        s1 = 1.0 / np.sqrt(D_IN)
        s2 = 1.0 / np.sqrt(D_OUT)
        W1 = jax.random.uniform(ks[2], (D_OUT, D_IN), jnp.float32, -s1, s1)
        b1 = jax.random.uniform(ks[3], (D_OUT,), jnp.float32, -s1, s1)
        gamma = jnp.ones((D_OUT,), jnp.float32)
        beta = jnp.zeros((D_OUT,), jnp.float32)
        W2 = jax.random.uniform(ks[4], (D_OUT, D_OUT), jnp.float32, -s2, s2)
        b2 = jax.random.uniform(ks[5], (D_OUT,), jnp.float32, -s2, s2)
        eps = jnp.zeros((), jnp.float32)
        return {'x': x, 'edge_index': edge_index, 'W1': W1, 'b1': b1, 'gamma': gamma, 'beta': beta, 'W2': W2, 'b2': b2, 'eps': eps}
    _L0_gnn_all = _L0_gnn_setup()
    _L0_gnn_in = {k: v for k, v in _L0_gnn_all.items() if k in ('W1', 'b1', 'gamma', 'beta', 'W2', 'b2', 'eps')}
    del _L0_gnn_all

    def _L1_gnn_setup():
        import jax, jax.numpy as jnp
        import numpy as np
        N, E, D, H, ED = (50000, 12500, 128, 8, 64)
        C = D // H

        def _ln(x, g, b, eps=1e-05):
            m = jnp.mean(x, axis=-1, keepdims=True)
            v = jnp.var(x, axis=-1, keepdims=True)
            return (x - m) * jax.lax.rsqrt(v + eps) * g + b
        key = jax.random.key(seed)
        ks = jax.random.split(key, 16)
        p = lambda k, shape: jax.random.normal(k, shape, dtype=jnp.float32) * 0.05
        return {'x': jax.random.normal(ks[0], (N, D), dtype=jnp.float32), 'edge_index': jax.random.randint(ks[1], (2, E), 0, N, dtype=jnp.int64), 'edge_attr': jax.random.normal(ks[2], (E, ED), dtype=jnp.float32), 'Wq': p(ks[3], (D, D)), 'bq': jnp.zeros((D,), jnp.float32), 'Wk': p(ks[4], (D, D)), 'bk': jnp.zeros((D,), jnp.float32), 'Wv': p(ks[5], (D, D)), 'bv': jnp.zeros((D,), jnp.float32), 'We': p(ks[6], (ED, D)), 'Wskip': p(ks[7], (D, D)), 'bskip': jnp.zeros((D,), jnp.float32), 'g1': jnp.ones((D,), jnp.float32), 'b1': jnp.zeros((D,), jnp.float32), 'g2': jnp.ones((D,), jnp.float32), 'b2': jnp.zeros((D,), jnp.float32), 'Wf1': p(ks[8], (D, 4 * D)), 'bf1': jnp.zeros((4 * D,), jnp.float32), 'Wf2': p(ks[9], (4 * D, D)), 'bf2': jnp.zeros((D,), jnp.float32)}
    _L1_gnn_all = _L1_gnn_setup()
    _L1_gnn_in = {k: v for k, v in _L1_gnn_all.items() if k in ('Wq', 'bq', 'Wk', 'bk', 'Wv', 'bv', 'We', 'Wskip', 'bskip', 'g1', 'b1', 'g2', 'b2', 'Wf1', 'bf1', 'Wf2', 'bf2')}
    del _L1_gnn_all
    return {'x': x, 'src': src, 'dst': dst, 'edge_attr_64': edge_attr_64, 'L0_gnn_W1': _L0_gnn_in['W1'], 'L0_gnn_b1': _L0_gnn_in['b1'], 'L0_gnn_gamma': _L0_gnn_in['gamma'], 'L0_gnn_beta': _L0_gnn_in['beta'], 'L0_gnn_W2': _L0_gnn_in['W2'], 'L0_gnn_b2': _L0_gnn_in['b2'], 'L0_gnn_eps': _L0_gnn_in['eps'], 'L1_gnn_Wq': _L1_gnn_in['Wq'], 'L1_gnn_bq': _L1_gnn_in['bq'], 'L1_gnn_Wk': _L1_gnn_in['Wk'], 'L1_gnn_bk': _L1_gnn_in['bk'], 'L1_gnn_Wv': _L1_gnn_in['Wv'], 'L1_gnn_bv': _L1_gnn_in['bv'], 'L1_gnn_We': _L1_gnn_in['We'], 'L1_gnn_Wskip': _L1_gnn_in['Wskip'], 'L1_gnn_bskip': _L1_gnn_in['bskip'], 'L1_gnn_g1': _L1_gnn_in['g1'], 'L1_gnn_b1': _L1_gnn_in['b1'], 'L1_gnn_g2': _L1_gnn_in['g2'], 'L1_gnn_b2': _L1_gnn_in['b2'], 'L1_gnn_Wf1': _L1_gnn_in['Wf1'], 'L1_gnn_bf1': _L1_gnn_in['bf1'], 'L1_gnn_Wf2': _L1_gnn_in['Wf2'], 'L1_gnn_bf2': _L1_gnn_in['bf2']}

def reference(x, src, dst, edge_attr_64, L0_gnn_W1, L0_gnn_b1, L0_gnn_gamma, L0_gnn_beta, L0_gnn_W2, L0_gnn_b2, L0_gnn_eps, L1_gnn_Wq, L1_gnn_bq, L1_gnn_Wk, L1_gnn_bk, L1_gnn_Wv, L1_gnn_bv, L1_gnn_We, L1_gnn_Wskip, L1_gnn_bskip, L1_gnn_g1, L1_gnn_b1, L1_gnn_g2, L1_gnn_b2, L1_gnn_Wf1, L1_gnn_bf1, L1_gnn_Wf2, L1_gnn_bf2):
    import jax
    import jax.numpy as jnp

    def _L0_gnn_ref(x, edge_index, W1, b1, gamma, beta, W2, b2, eps):
        import jax, jax.numpy as jnp
        import numpy as np
        N = 100000
        E = 25000
        D_IN = 128
        D_OUT = 128
        BN_EPS = 1e-05
        src = edge_index[0]
        dst = edge_index[1]
        agg = jax.ops.segment_sum(x[src], dst, num_segments=N)
        h = (1.0 + eps) * x + agg
        h = h @ W1.T + b1
        mean = jnp.mean(h, axis=0)
        var = jnp.mean(jnp.square(h - mean), axis=0)
        h = gamma * (h - mean) * jax.lax.rsqrt(var + BN_EPS) + beta
        h = jax.nn.relu(h)
        out = h @ W2.T + b2
        return out

    def _L1_gnn_ref(x, edge_index, edge_attr, Wq, bq, Wk, bk, Wv, bv, We, Wskip, bskip, g1, b1, g2, b2, Wf1, bf1, Wf2, bf2):
        import jax, jax.numpy as jnp
        import numpy as np
        N, E, D, H, ED = (50000, 12500, 128, 8, 64)
        C = D // H

        def _ln(x, g, b, eps=1e-05):
            m = jnp.mean(x, axis=-1, keepdims=True)
            v = jnp.var(x, axis=-1, keepdims=True)
            return (x - m) * jax.lax.rsqrt(v + eps) * g + b
        n = x.shape[0]
        src, dst = (edge_index[0], edge_index[1])
        q = (x @ Wq + bq).reshape(n, H, C)
        k = (x @ Wk + bk).reshape(n, H, C)
        v = (x @ Wv + bv).reshape(n, H, C)
        e = (edge_attr @ We).reshape(-1, H, C)
        k_j = k[src] + e
        v_j = v[src] + e
        logits = jnp.sum(q[dst] * k_j, axis=-1) / np.sqrt(C)
        m = jax.ops.segment_max(logits, dst, num_segments=n)
        ex = jnp.exp(logits - m[dst])
        denom = jax.ops.segment_sum(ex, dst, num_segments=n)
        alpha = ex / denom[dst]
        agg = jax.ops.segment_sum(alpha[..., None] * v_j, dst, num_segments=n)
        conv = agg.reshape(n, D) + x @ Wskip + bskip
        h = _ln(conv + x, g1, b1)
        ffn = jax.nn.gelu(h @ Wf1 + bf1, approximate=False) @ Wf2 + bf2
        return _ln(ffn + h, g2, b2)
    edge_index = jnp.stack([src, dst])
    x = _layernorm(x + _L0_gnn_ref(x, edge_index, L0_gnn_W1, L0_gnn_b1, L0_gnn_gamma, L0_gnn_beta, L0_gnn_W2, L0_gnn_b2, L0_gnn_eps), axis=-1)
    x = _layernorm(x + _L1_gnn_ref(x, edge_index, edge_attr_64, L1_gnn_Wq, L1_gnn_bq, L1_gnn_Wk, L1_gnn_bk, L1_gnn_Wv, L1_gnn_bv, L1_gnn_We, L1_gnn_Wskip, L1_gnn_bskip, L1_gnn_g1, L1_gnn_b1, L1_gnn_g2, L1_gnn_b2, L1_gnn_Wf1, L1_gnn_bf1, L1_gnn_Wf2, L1_gnn_bf2), axis=-1)
    return x

_drawn_inputs = setup_inputs


def setup_inputs(seed=0):
    import zlib

    import numpy as np

    out = dict(_drawn_inputs(seed))
    spreads = {'L0_gnn_gamma': (1.0, 0.2),
     'L0_gnn_beta': (0.0, 0.1),
     'L1_gnn_bq': (0.0, 2.0),
     'L1_gnn_bk': (0.0, 2.0),
     'L1_gnn_bv': (0.0, 0.329),
     'L1_gnn_bskip': (0.0, 0.1),
     'L1_gnn_g1': (1.0, 0.2),
     'L1_gnn_b1': (0.0, 0.1),
     'L1_gnn_g2': (1.0, 0.2),
     'L1_gnn_b2': (0.0, 0.1),
     'L1_gnn_bf1': (0.0, 0.1),
     'L1_gnn_bf2': (0.0, 0.1)}
    factors = {'L0_gnn_b1': 64.0, 'L1_gnn_Wq': 3.393, 'L1_gnn_Wk': 4.174}
    for name, (base, spread) in spreads.items():
        noise = np.random.default_rng([zlib.crc32(name.encode()), seed]).standard_normal(out[name].shape)
        drawn = base * np.exp(spread * noise) if base else spread * noise
        out[name] = jnp.asarray(drawn.astype(out[name].dtype))
    for name, factor in factors.items():
        out[name] = (out[name] * factor).astype(out[name].dtype)
    return out
```

```python
from contextlib import ExitStack

import concourse.bass as bass
from concourse import mybir

ALU = mybir.AluOpType
ACT = mybir.ActivationFunctionType
F32 = mybir.dt.float32
BF16 = mybir.dt.bfloat16
I32 = mybir.dt.int32
U32 = mybir.dt.uint32

P = 128
D = 128
T = 4
B = T * P
H = 8
C = D // H
DE = 64
FF = 4 * D
U = 4
LN_EPS = 1e-5
BN_EPS = 1e-5
LOW = -1e30
PAD = 200000
SKIP = 1 << 20


def walk(eng, steps, lag, body):
    full = (steps - 1) // U
    if full <= 2:
        for i in range(steps + lag):
            body(i // U, i % U)
        return
    for i in range(2 * U):
        body(i // U, i % U)
    with eng.Fori(2, full) as j:
        for u in range(U):
            body(j, u)
    for i in range(full * U, steps + lag):
        body(i // U, i % U)


def back(j, u, lag):
    k = u - lag
    return j + k // U, k % U, j * U + k


def ready_values(eng, *values):
    return [v if isinstance(v, int) else eng.to_reg(v) for v in values]


def works(i, steps):
    return not isinstance(i, int) or 0 <= i < steps


def late(j, n=1):
    return not isinstance(j, int) or j >= n


def build(nc, x, src, dst, edge_attr, W1, gamma, beta, W2, b2, eps, Wq, bq, Wk, bk, Wv, bv, We, Wskip, bskip,
          g1, b1, g2, b2n, Wf1, bf1, Wf2, bf2, out):
    N = x.shape[0]
    E = src.shape[0]
    NB = -(-E // B)
    NG = -(-N // B)
    E_LAST = E - (NB - 1) * B
    N_LAST = N - (NG - 1) * B
    P_LAST = next(p for p in (128, 112, 96, 80, 64, 48, 32, 16) if N_LAST % p == 0 and N_LAST // p <= T)
    T_LAST = N_LAST // P_LAST
    NI = NB * T * 2
    CI = next(c for c in range(1, NI + 1) if NI % c == 0 and NI // c <= P)
    PI = NI // CI
    ZC = next(c for c in range(4096, 0, -1) if N % c == 0)

    agg = nc.dram_tensor("agg", [N, D], F32).ap()
    x1 = nc.dram_tensor("x1", [N, D], F32).ap()
    rows_side = nc.dram_tensor("rows_side", [2, NI, D], F32).ap()
    soft_side = nc.dram_tensor("soft_side", [NI, 2 * H], F32).ap()
    breaks = nc.dram_tensor("breaks", [NB, T, H, P + 1], F32).ap()
    keys = nc.dram_tensor("keys", [1, NI], F32).ap()
    key_rows = nc.dram_tensor("key_rows", [1, NI], I32).ap()

    def geometry(g):
        if isinstance(g, int) and g == NG - 1:
            return P_LAST, T_LAST
        return P, T

    def group(dram, g):
        p, t = geometry(g)
        rows = dram[bass.ds(g * B, p * t), :] if not isinstance(g, int) else dram[g * B:g * B + p * t, :]
        return rows.rearrange("(p t) d -> p t d", t=t)

    with ExitStack() as ctx:
        def keep(name, shape, dt=F32):
            return ctx.enter_context(nc.sbuf_tensor(name, shape, dt))

        part_sems = []

        def sem(name):
            part_sems.append(nc.alloc_semaphore(name))
            return part_sems[-1]

        def clear():
            nc.clear_and_free_semaphores(part_sems[:])
            nc.all_engine_barrier()
            part_sems.clear()

        ident = keep("ident", [P, P])
        idx_cols = keep("idx_cols", [P, NB, 3, T], I32)
        dst_cols = keep("dst_cols", [P, NB, T])
        same_item = keep("same_item", [P, NI])
        count_item = keep("count_item", [P, NI])
        row_item = keep("row_item", [PI, CI], I32)
        W1T = keep("W1T", [D, D])
        W2T = keep("W2T", [D, D])
        Wq_s = keep("Wq_s", [D, D])
        Wk_s = keep("Wk_s", [D, D])
        Wv_s = keep("Wv_s", [D, D])
        We_s = keep("We_s", [DE + 1, 2, D])
        Wskip_s = keep("Wskip_s", [D, D])
        Wf1_s = keep("Wf1_s", [D, FF])
        Wf2_s = keep("Wf2_s", [D, T, D])
        onesB = keep("onesB", [3, P], BF16)
        b2_3 = keep("b2_3", [3, T, D], BF16)
        bq_3 = keep("bq_3", [3, T, D], BF16)
        bskip_3 = keep("bskip_3", [3, T, D], BF16)
        bf2_3 = keep("bf2_3", [3, T, D], BF16)
        g1_col = keep("g1_col", [D, 1])
        b1_col = keep("b1_col", [D, 1])
        bf1_col = keep("bf1_col", [D, T])
        g1_row = keep("g1_row", [P, T, D])
        g2_row = keep("g2_row", [P, T, D])
        b2n_row = keep("b2n_row", [P, T, D])
        gamma_col = keep("gamma_col", [D, 1])
        beta_col = keep("beta_col", [D, 1])
        eps1 = keep("eps1", [P, 1])
        half = keep("half", [P, T])
        mid = keep("mid", [P, T])
        root_d = keep("root_d", [P, T])
        bn_scale = keep("bn_scale", [D, 1])
        bn_shift = keep("bn_shift", [D, 1])
        head_of = keep("head_of", [H, D])

        with ExitStack() as part:
            def sb(name, shape, dt=F32):
                return part.enter_context(nc.sbuf_tensor(name, shape, dt))

            def ps(name, shape):
                return part.enter_context(nc.psum_tensor(name, shape, F32))

            dst_i = sb("dst_i", [NB, B], I32)
            next_i = sb("next_i", [NB, B], I32)
            src_i = sb("src_i", [NB, B], I32)
            dst_f = sb("dst_f", [NB, T, P])
            next_f = sb("next_f", [NB, T, P])
            src_f = sb("src_f", [NB, T, P])
            row_f = sb("row_f", [NB, T, P])
            eq = sb("eq", [NB, T, P])
            brk = sb("brk", [NB, T, P + 1])
            ends = sb("ends", [NB, T, 2])
            key_b = sb("key_b", [P, NI])
            go_on = sb("go_on", [1, NI])
            key_skip = sb("key_skip", [1, NI])
            key_skip_i = sb("key_skip_i", [1, NI], I32)
            W1_l = sb("W1_l", [D, D])
            W2_l = sb("W2_l", [D, D])
            bias = sb("bias", [1, 5, D])
            part_b = sb("part_b", [1, 4, 3, T, D], BF16)
            rest = sb("rest", [1, 4, D])
            zeros = sb("zeros", [P, ZC])
            turn = ps("turn", [P, 4, 512])

            s_mem, s_idx, s_w, s_wb = sem("tables_cleared"), sem("indices_in"), sem("weights_in"), sem("bias_parts_in")
            s_id0, s_id, s_ho = sem("ident_zero"), sem("ident_ready"), sem("head_of_steps")
            s_f, s_eq, s_brk = sem("indices_float"), sem("row_steps"), sem("breaks_ready")
            s_ends, s_keys, s_keyb, s_item = sem("ends_ready"), sem("keys_out"), sem("keys_in"), sem("item_steps")
            s_rowo, s_rowi, s_brko = sem("item_rows_out"), sem("item_rows_in"), sem("breaks_out")
            s_turn, s_col, s_bp, s_v = sem("turned"), sem("turned_read"), sem("bias_steps"), sem("small_steps")
            s_zero = sem("agg_zeroed")
            tail = NB - 1

            with nc.Block() as block:
                @block.sync
                def _(sp):
                    sp.wait_ge(s_mem, 3)
                    for tile_, dram, off in ((dst_i, dst, 0), (next_i, dst, 1), (src_i, src, 0)):
                        if tail:
                            sp.dma_start(tile_[0:tail, :], dram[off:off + tail * B].rearrange("(b e) -> b e", e=B))\
                              .then_inc(s_idx, 16)
                        sp.dma_start(tile_[tail:NB, 0:E_LAST - off],
                                     dram[off + tail * B:E].rearrange("(b e) -> b e", b=1)).then_inc(s_idx, 16)
                    sp.wait_ge(s_ends, 1)
                    sp.dma_start(keys.rearrange("a (b i) -> (a b) i", i=2 * T),
                                 ends[:].rearrange("b t e -> b (t e)")).then_inc(s_keys, 16)
                    sp.wait_ge(s_keys, 16)
                    sp.dma_start(key_b[:], keys.to_broadcast([P, NI])).then_inc(s_keyb, 16)
                    sp.wait_ge(s_brk, 1)
                    for h in range(H):
                        sp.dma_start(breaks[:, :, h, :], brk[:]).then_inc(s_brko, 16)
                    sp.wait_ge(s_item, 6)
                    sp.dma_start(key_rows, key_skip_i[:]).then_inc(s_rowo, 16)
                    sp.wait_ge(s_rowo, 16)
                    with nc.allow_non_contiguous_dma(reason="a few hundred indices, once"):
                        sp.dma_start(row_item[:], key_rows.rearrange("a (c p) -> p (a c)", p=PI)).then_inc(s_rowi, 16)
                    sp.wait_ge(s_bp, 6)
                    for n, t in enumerate((b2_3, bq_3, bskip_3, bf2_3)):
                        for r in range(3):
                            sp.dma_start(t[r:r + 1], part_b[0:1, n, r]).then_inc(s_wb, 16)
                    sp.wait_ge(s_wb, 12 * 16)
                    sp.wait_ge(s_rowi, 16)
                    sp.wait_ge(s_brko, H * 16)

                @block.scalar
                def _(act):
                    def col(v):
                        return v.rearrange("(d a) -> d a", a=1)

                    def row(v):
                        return v.rearrange("(a d) -> a d", a=1)

                    loads = [(W1_l[:], W1), (W2_l[:], W2), (Wq_s[:], Wq), (Wk_s[:], Wk), (Wv_s[:], Wv),
                             (Wskip_s[:], Wskip), (Wf1_s[:], Wf1), (Wf2_s[:], Wf2.rearrange("(t f) d -> f t d", t=T)),
                             (We_s[0:DE, 0, :], We), (We_s[0:DE, 1, :], We),
                             (We_s[DE:DE + 1, 0, :], row(bk)), (We_s[DE:DE + 1, 1, :], row(bv)),
                             (bias[:, 0, :], row(b2)), (bias[:, 1, :], row(bq)), (bias[:, 2, :], row(bskip)),
                             (bias[:, 3, :], row(bf2)), (bias[:, 4, :], row(b1)),
                             (g1_col[:], col(g1)), (b1_col[:], col(b1)), (gamma_col[:], col(gamma)),
                             (beta_col[:], col(beta)), (eps1[:], row(eps).to_broadcast([P, 1]))]
                    for t in range(T):
                        loads.append((bf1_col[:, t:t + 1], col(bf1[t * D:(t + 1) * D])))
                        loads.append((g1_row[:, t, :], row(g1).to_broadcast([P, D])))
                        loads.append((g2_row[:, t, :], row(g2).to_broadcast([P, D])))
                        loads.append((b2n_row[:, t, :], row(b2n).to_broadcast([P, D])))
                    with nc.allow_non_contiguous_dma(reason="vectors of 128, once"):
                        for to, frm in loads:
                            act.dma_start(to, frm).then_inc(s_w, 16)
                    act.wait_ge(s_w, 16 * 38)
                    act.wait_ge(s_mem, 4)
                    for z in range(N // ZC):
                        act.dma_start(agg.rearrange("n d -> (n d)")[z * P * ZC:(z + 1) * P * ZC]
                                      .rearrange("(p c) -> p c", p=P), zeros[:]).then_inc(s_zero, 16)
                    act.wait_ge(s_zero, 16 * (N // ZC))

                @block.gpsimd
                def _(pool):
                    pool.memset(ident[:], 0.0).then_inc(s_id0, 1)
                    pool.memset(head_of[:], 1.0).then_inc(s_ho, 1)
                    pool.wait_ge(s_id0, 1)
                    pool.affine_select(out=ident[:], in_=ident[:], compare_op=ALU.not_equal, fill=1.0, base=0,
                                       pattern=[[-1, P]], channel_multiplier=1).then_inc(s_id, 1)
                    pool.wait_ge(s_ho, 1)
                    pool.affine_select(out=head_of[:], in_=head_of[:], compare_op=ALU.is_ge, fill=0.0, base=0,
                                       pattern=[[1, D]], channel_multiplier=-C).then_inc(s_ho, 1)
                    pool.wait_ge(s_ho, 2)
                    pool.affine_select(out=head_of[:], in_=head_of[:], compare_op=ALU.is_ge, fill=0.0, base=C - 1,
                                       pattern=[[-1, D]], channel_multiplier=C).then_inc(s_ho, 1)

                @block.vector
                def _(dve):
                    dve.memset(dst_i[:], PAD).then_inc(s_mem, 1)
                    dve.memset(next_i[:], PAD).then_inc(s_mem, 1)
                    dve.memset(src_i[:], 0).then_inc(s_mem, 1)
                    dve.memset(zeros[:], 0.0).then_inc(s_mem, 1)
                    dve.memset(onesB[:], 1.0)
                    dve.memset(half[:], -0.5)
                    dve.memset(mid[:], 0.5)
                    dve.memset(root_d[:], float(D) ** 0.5)
                    dve.memset(brk[:], LOW).then_inc(s_mem, 1)
                    dve.wait_ge(s_idx, (6 if tail else 3) * 16)
                    for to, frm in ((dst_f, dst_i), (next_f, next_i), (src_f, src_i)):
                        dve.tensor_copy(to[:].rearrange("b t e -> b (t e)"), frm[:]).then_inc(s_f, 1)
                    dve.wait_ge(s_f, 3)
                    dve.tensor_tensor(eq[:], dst_f[:], next_f[:], ALU.is_equal).then_inc(s_eq, 1)
                    dve.wait_ge(s_eq, 1)
                    dve.scalar_tensor_tensor(out=row_f[:], in0=eq[:], scalar=float(SKIP), in1=dst_f[:],
                                             op0=ALU.mult, op1=ALU.add).then_inc(s_eq, 1)
                    dve.wait_ge(s_eq, 2)
                    for n, e in enumerate((0, P - 1)):
                        dve.tensor_tensor(eq[:], dst_f[:], dst_f[:, :, e:e + 1].to_broadcast([NB, T, P]),
                                          ALU.is_equal).then_inc(s_eq, 1)
                        dve.wait_ge(s_eq, 3 + 2 * n)
                        dve.scalar_tensor_tensor(out=row_f[:], in0=eq[:], scalar=float(SKIP), in1=row_f[:],
                                                 op0=ALU.mult, op1=ALU.add).then_inc(s_eq, 1)
                        dve.wait_ge(s_eq, 4 + 2 * n)
                    dve.tensor_tensor(eq[:, :, 0:P - 1], dst_f[:, :, 1:P], dst_f[:, :, 0:P - 1],
                                      ALU.is_equal).then_inc(s_eq, 1)
                    dve.wait_ge(s_eq, 7)
                    dve.wait_ge(s_mem, 5)
                    dve.tensor_scalar(brk[:, :, 1:P], eq[:, :, 0:P - 1], -1.0, -LOW, ALU.add, ALU.mult)\
                       .then_inc(s_brk, 1)
                    dve.tensor_copy(ends[:], dst_f[:, :, 0:P:P - 1]).then_inc(s_ends, 1)
                    dve.wait_ge(s_keyb, 16)
                    dve.memset(same_item[:], 0.0).then_inc(s_item, 1)
                    dve.memset(count_item[:], 1.0).then_inc(s_item, 1)
                    dve.wait_ge(s_item, 1)
                    dve.tensor_tensor(same_item[:, 1:NI], key_b[:, 1:NI], key_b[:, 0:NI - 1], ALU.is_equal)\
                       .then_inc(s_item, 1)
                    dve.wait_ge(s_item, 3)
                    dve.tensor_scalar(count_item[:, 1:NI:2], same_item[:, 1:NI:2], -1.0, 1.0, ALU.mult, ALU.add)\
                       .then_inc(s_item, 1)
                    dve.tensor_copy(key_skip[0:1, NI - 1:NI], key_b[0:1, NI - 1:NI]).then_inc(s_v, 1)
                    dve.scalar_tensor_tensor(out=key_skip[0:1, 0:NI - 1], in0=same_item[0:1, 1:NI],
                                             scalar=float(SKIP), in1=key_b[0:1, 0:NI - 1],
                                             op0=ALU.mult, op1=ALU.add).then_inc(s_item, 1)
                    dve.wait_ge(s_item, 5)
                    dve.wait_ge(s_v, 1)
                    dve.tensor_copy(key_skip_i[:], key_skip[:]).then_inc(s_item, 1)
                    dve.wait_ge(s_w, 16 * 38)
                    dve.tensor_scalar(eps1[:], eps1[:], 1.0, None, ALU.add).then_inc(s_v, 1)
                    dve.tensor_tensor(bias[:, 3, :], bias[:, 3, :], bias[:, 4, :], ALU.add).then_inc(s_bp, 1)
                    dve.wait_ge(s_bp, 1)
                    left = bias[:, 0:4, :]
                    for r in range(3):
                        for t in range(T):
                            last = dve.tensor_copy(part_b[:, :, r, t, :], left)
                        last.then_inc(s_bp, 1)
                        if r < 2:
                            dve.wait_ge(s_bp, 2 + 2 * r)
                            dve.tensor_tensor(rest[:], left, part_b[:, :, r, 0, :], ALU.subtract).then_inc(s_bp, 1)
                            dve.wait_ge(s_bp, 3 + 2 * r)
                            left = rest[:]
                    dve.wait_ge(s_id, 1)
                    dve.tensor_tensor(Wskip_s[:], Wskip_s[:], ident[:], ALU.add).then_inc(s_v, 1)
                    for n in range(3):
                        dve.wait_ge(s_turn, n + 1)
                        for t in range(T):
                            last = dve.tensor_copy(idx_cols[:, :, (1, 0, 2)[n], t], turn[:, n, t * P:t * P + NB])
                            if n == 0:
                                last = dve.tensor_copy(dst_cols[:, :, t], turn[:, n, t * P:t * P + NB])
                        last.then_inc(s_col, 1)
                    dve.wait_ge(s_turn, 4)
                    dve.tensor_copy(W1T[:], turn[:, 3, 0:D])
                    dve.tensor_copy(W2T[:], turn[:, 3, D:2 * D]).then_inc(s_col, 1)

                @block.tensor
                def _(pe):
                    pe.wait_ge(s_id, 1)
                    pe.wait_ge(s_eq, 6)
                    for n, table in enumerate((dst_f, src_f, row_f)):
                        for t in range(T):
                            mm = pe.transpose(turn[:, n, t * P:t * P + NB], table[:, t, :], ident[0:NB, 0:NB])
                        mm.then_inc(s_turn, 1)
                    pe.wait_ge(s_w, 16 * 38)
                    pe.transpose(turn[:, 3, 0:D], W1_l[:], ident[:])
                    pe.transpose(turn[:, 3, D:2 * D], W2_l[:], ident[:]).then_inc(s_turn, 1)

        clear()
        edges0(nc, sem, NB, NI, x, agg, rows_side[0], ident, idx_cols, dst_cols, N)
        joins0(nc, sem, NI, CI, PI, rows_side[0], agg, ident, same_item, count_item, row_item, N)
        part_sems.clear()
        stats(nc, sem, NG, N, group, geometry, x, agg, eps1, half, W1T, gamma_col, beta_col, bn_scale, bn_shift,
              ident)
        clear()
        nodes0(nc, sem, NG, group, geometry, x, agg, x1, eps1, half, mid, root_d, ident, W1T, W2T,
               bn_scale, bn_shift, onesB, b2_3)
        clear()
        edges1(nc, sem, NB, E_LAST, N, x1, agg, edge_attr, rows_side[1], soft_side, breaks, ident, idx_cols, dst_cols,
               Wq_s, Wk_s, Wv_s, We_s, onesB, bq_3)
        joins1(nc, sem, NI, CI, PI, rows_side[1], soft_side, agg, ident, same_item, count_item, row_item, head_of, N)
        nodes1(nc, sem, NG, group, geometry, x1, agg, out, half, mid, root_d, ident, Wskip_s, Wf1_s, Wf2_s, onesB,
               bskip_3, bf2_3,
               g1_col, b1_col, bf1_col, g1_row, g2_row, b2n_row)


def scatter_rows(pool, dram, index, rows, last_row):
    return pool.indirect_dma_start(dram, bass.IndirectOffsetOnAxis(index, 0), rows, None,
                                   bounds_check=last_row, oob_is_err=False)


def gather_rows(pool, rows, dram, index, last_row):
    return pool.indirect_dma_start(rows, None, dram, bass.IndirectOffsetOnAxis(index, 0), bounds_check=last_row)


def prepare_batch(dve, i, u, idx, dst_f, idx_cols, dst_cols, idx_ready, dstf_ready):
    dve.tensor_copy(idx[:, u], idx_cols[:, bass.ds(i, 1)].rearrange("p b k t -> p (b k) t")).then_inc(idx_ready, 1)
    dve.tensor_copy(dst_f[:, u], dst_cols[:, bass.ds(i, 1)].rearrange("p b t -> p (b t)")).then_inc(dstf_ready, 1)


def side_rows(side, i, end):
    view = side.rearrange("(b t e) d -> b t e d", t=T, e=2)
    return view[bass.ds(i, 1), :, end, :]


def edges0(nc, sem, NB, NI, x, agg, side, ident, idx_cols, dst_cols, N):
    with ExitStack() as part:
        def sb(name, shape, dt=F32):
            return part.enter_context(nc.sbuf_tensor(name, shape, dt))

        idx = sb("e0_idx", [P, U, 3, T], I32)
        dst_f = sb("e0_dst_f", [P, U, T])
        rows = sb("e0_rows", [P, U, T, D])
        same = sb("e0_same", [P, U, T, P])
        sums = sb("e0_sums", [P, U, T, D])
        spread = part.enter_context(nc.psum_tensor("e0_spread", [P, 2, T, P], F32))
        total = part.enter_context(nc.psum_tensor("e0_total", [P, 2, T, D], F32))

        idx_ready, dstf_ready = sem("e0_idx_ready"), sem("e0_dstf_ready")
        spread_ready, same_ready = sem("e0_spread_ready"), sem("e0_same_ready")
        total_ready, sums_ready = sem("e0_total_ready"), sem("e0_sums_ready")
        begun = sem("e0_begun")
        gathered = [sem(f"e0_gathered{u}") for u in range(U)]
        scattered = [sem(f"e0_scattered{u}") for u in range(U)]
        sided = [sem(f"e0_sided{u}") for u in range(U)]

        with nc.Block() as block:
            @block.vector
            def _(dve):
                dve.memset(dst_f[:], 0.0).then_inc(begun, 1)
                dve.wait_ge(begun, 1)

                def body(j, u):
                    i = j * U + u
                    if works(i, NB):
                        if late(j):
                            dve.wait_ge(scattered[u], j * T * 16)
                        prepare_batch(dve, i, u, idx, dst_f, idx_cols, dst_cols, idx_ready, dstf_ready)
                    jb, ub, ib = back(j, u, 1)
                    if works(ib, NB):
                        dve.wait_ge(spread_ready, ib + 1)
                        dve.wait_ge(dstf_ready, ib + 1)
                        if late(jb):
                            dve.wait_ge(total_ready, ib - U + 1)
                        dve.tensor_tensor(same[:, ub], spread[:, ub % 2],
                                          dst_f[:, ub].unsqueeze(2).to_broadcast([P, T, P]),
                                          ALU.is_equal).then_inc(same_ready, 1)

                walk(dve, NB, 1, body)

            @block.tensor
            def _(pe):
                def body(j, u):
                    i = j * U + u
                    if works(i, NB):
                        pe.wait_ge(dstf_ready, i + 1)
                        if not isinstance(i, int) or i >= 2:
                            pe.wait_ge(same_ready, i - 1)
                        for t in range(T):
                            mm = pe.transpose(spread[:, u % 2, t, :], dst_f[:, u, t:t + 1].to_broadcast([P, P]),
                                              ident[:])
                        mm.then_inc(spread_ready, 1)
                    jb, ub, ib = back(j, u, 2)
                    if works(ib, NB):
                        pe.wait_ge(same_ready, ib + 1)
                        pe.wait_ge(gathered[ub], (jb + 1) * T * 16)
                        if not isinstance(ib, int) or ib >= 2:
                            pe.wait_ge(sums_ready, ib - 1)
                        for t in range(T):
                            mm = pe.matmul(total[:, ub % 2, t, :], same[:, ub, t, :], rows[:, ub, t, :],
                                           start=True, stop=True)
                        mm.then_inc(total_ready, 1)

                walk(pe, NB, 2, body)

            @block.scalar
            def _(act):
                def body(j, u):
                    i = j * U + u
                    act.wait_ge(total_ready, i + 1)
                    if late(j):
                        act.wait_ge(scattered[u], j * T * 16)
                        act.wait_ge(sided[u], j * 32)
                    act.activation(sums[:, u], total[:, u % 2], ACT.Copy).then_inc(sums_ready, 1)

                walk(act, NB, 0, body)

            @block.gpsimd
            def _(pool):
                last_row = pool.to_reg(N - 1)

                def body(j, u):
                    i = j * U + u
                    if works(i, NB):
                        now, free = ready_values(pool, i + 1, i - U + 1)
                        pool.wait_ge(begun, 1)
                        pool.wait_ge(idx_ready, now)
                        if late(j):
                            pool.wait_ge(total_ready, free)
                        for t in range(T):
                            gather_rows(pool, rows[:, u, t, :], x, idx[:, u, 0, t:t + 1].bitcast(U32), last_row)\
                                .then_inc(gathered[u], 16)
                    jb, ub, ib = back(j, u, 3)
                    if works(ib, NB):
                        (now,) = ready_values(pool, ib + 1)
                        pool.wait_ge(begun, 1)
                        pool.wait_ge(sums_ready, now)
                        for t in range(T):
                            scatter_rows(pool, agg, idx[:, ub, 2, t:t + 1].bitcast(U32), sums[:, ub, t, :], last_row)\
                                .then_inc(scattered[ub], 16)

                walk(pool, NB, 3, body)
                for u in range(U):
                    pool.wait_ge(scattered[u], len(range(u, NB, U)) * T * 16)

            @block.sync
            def _(sp):
                def body(j, u):
                    i = j * U + u
                    sp.wait_ge(sums_ready, i + 1)
                    for end, p in enumerate((0, P - 1)):
                        sp.dma_start(side_rows(side, i, end), sums[p:p + 1, u]).then_inc(sided[u], 16)

                walk(sp, NB, 0, body)
                for u in range(U):
                    sp.wait_ge(sided[u], len(range(u, NB, U)) * 32)


def joins0(nc, sem, NI, CI, PI, side, agg, ident, same_item, count_item, row_item, N):
    with ExitStack() as part:
        items = part.enter_context(nc.sbuf_tensor("j0_items", [PI, CI, D], F32))
        flat = part.enter_context(nc.sbuf_tensor("j0_flat", [D, NI], F32))
        run = part.enter_context(nc.sbuf_tensor("j0_run", [D, NI], F32))
        turn = part.enter_context(nc.psum_tensor("j0_turn", [P, CI, P], F32))
        s_in, s_turn, s_flat = sem("j0_in"), sem("j0_turned"), sem("j0_flat_steps")
        s_back, s_rows, s_out = sem("j0_turned_back"), sem("j0_rows"), sem("j0_out")

        with nc.Block() as block:
            @block.sync
            def _(sp):
                sp.dma_start(items[:], side.rearrange("(c p) d -> p c d", p=PI)).then_inc(s_in, 16)

            @block.tensor
            def _(pe):
                pe.wait_ge(s_in, 16)
                for c in range(CI):
                    mm = pe.transpose(turn[:, c, 0:PI], items[:, c, :], ident[0:PI, 0:PI])
                mm.then_inc(s_turn, 1)
                pe.wait_ge(s_flat, 2)
                for c in range(CI):
                    mm = pe.transpose(turn[0:PI, c, :], run[:, c * PI:(c + 1) * PI], ident[:])
                mm.then_inc(s_back, 1)

            @block.vector
            def _(dve):
                dve.wait_ge(s_turn, 1)
                dve.tensor_tensor(flat[:].rearrange("d (c p) -> d c p", p=PI), turn[:, :, 0:PI],
                                  count_item[:].rearrange("d (c p) -> d c p", p=PI), ALU.mult).then_inc(s_flat, 1)
                dve.wait_ge(s_flat, 1)
                dve.tensor_tensor_scan(run[:], same_item[:], flat[:], 0.0, ALU.mult, ALU.add).then_inc(s_flat, 1)
                dve.wait_ge(s_back, 1)
                dve.tensor_copy(items[:], turn[0:PI]).then_inc(s_rows, 1)

            @block.gpsimd
            def _(pool):
                pool.wait_ge(s_rows, 1)
                for c in range(CI):
                    scatter_rows(pool, agg, row_item[:, c:c + 1].bitcast(U32), items[:, c, :], N - 1)\
                        .then_inc(s_out, 16)
                pool.wait_ge(s_out, CI * 16)


def stats(nc, sem, NG, N, group, geometry, x, agg, eps1, half, W1T, gamma_col, beta_col, bn_scale, bn_shift,
          ident):
    with ExitStack() as part:
        def sb(name, shape, dt=F32):
            return part.enter_context(nc.sbuf_tensor(name, shape, dt))

        xs = sb("st_x", [P, U, T, D])
        ags = sb("st_agg", [P, U, T, D])
        h = sb("st_h", [P, U, T, D + 1])
        gram = sb("st_gram", [D, D + 1])
        mean = sb("st_mean", [D, 1])
        mean_row = sb("st_mean_row", [1, D])
        cov = sb("st_cov", [D, D])
        prod = sb("st_prod", [D, D])
        ones = sb("st_ones", [P, 1])
        small = sb("st_small", [D, 4])
        G = part.enter_context(nc.psum_tensor("st_G", [D, 512], F32))
        M = part.enter_context(nc.psum_tensor("st_M", [D, 4, 512], F32))
        M_row = part.enter_context(nc.psum_tensor("st_row", [1, 512], F32))

        x_in = [sem(f"st_x_in{u}") for u in range(U)]
        agg_in = [sem(f"st_agg_in{u}") for u in range(U)]
        h_ready, h_used, ones_set = sem("st_h_ready"), sem("st_h_used"), sem("st_ones_set")
        fin_d, fin_p, fin_g = sem("st_vector_steps"), sem("st_product_steps"), sem("st_pool_steps")

        with nc.Block() as block:
            @block.sync
            def _(sp):
                def body(j, u):
                    g = j * U + u
                    p, t = geometry(g)
                    if late(j):
                        sp.wait_ge(h_ready, g - U + 1)
                    sp.dma_start(xs[0:p, u, 0:t], group(x, g)).then_inc(x_in[u], 16)
                    sp.dma_start(ags[0:p, u, 0:t], group(agg, g)).then_inc(agg_in[u], 16)

                walk(sp, NG, 0, body)

            @block.vector
            def _(dve):
                dve.memset(ones[:], 1.0).then_inc(ones_set, 1)
                dve.memset(h[:], 1.0).then_inc(ones_set, 1)
                dve.wait_ge(ones_set, 2)

                def body(j, u):
                    g = j * U + u
                    p, t = geometry(g)
                    dve.wait_ge(x_in[u], (j + 1) * 16)
                    dve.wait_ge(agg_in[u], (j + 1) * 16)
                    if late(j):
                        dve.wait_ge(h_used, g - U + 1)
                    dve.scalar_tensor_tensor(out=h[0:p, u, 0:t, 0:D], in0=xs[0:p, u, 0:t], scalar=eps1[0:p],
                                             in1=ags[0:p, u, 0:t], op0=ALU.mult, op1=ALU.add).then_inc(h_ready, 1)

                walk(dve, NG, 0, body)
                dve.wait_ge(h_used, NG)
                dve.tensor_scalar(gram[:], G[:, 0:D + 1], 1.0 / N, None, ALU.mult).then_inc(fin_d, 1)
                dve.wait_ge(fin_p, 1)
                dve.tensor_copy(mean_row[:], M_row[0:1, 0:D]).then_inc(fin_d, 1)
                dve.wait_ge(fin_p, 2)
                dve.tensor_tensor(cov[:], gram[:, 0:D], M[:, 0, 0:D], ALU.subtract).then_inc(fin_d, 1)
                dve.wait_ge(fin_p, 3)
                dve.tensor_tensor(prod[:], M[:, 1, 0:D], W1T[:], ALU.mult).then_inc(fin_d, 1)
                dve.wait_ge(fin_p, 5)
                dve.tensor_scalar(small[:, 0:1], M[:, 2, 0:1], 0.0, BN_EPS, ALU.max, ALU.add).then_inc(fin_d, 1)
                dve.wait_ge(fin_g, 1)
                dve.tensor_tensor(bn_scale[:], small[:, 1:2], gamma_col[:], ALU.mult).then_inc(fin_d, 1)
                dve.wait_ge(fin_d, 6)
                dve.tensor_tensor(small[:, 2:3], M[:, 3, 0:1], bn_scale[:], ALU.mult).then_inc(fin_d, 1)
                dve.wait_ge(fin_d, 7)
                dve.tensor_tensor(bn_shift[:], beta_col[:], small[:, 2:3], ALU.subtract).then_inc(fin_d, 1)

            @block.gpsimd
            def _(pool):
                pool.wait_ge(fin_d, 5)
                pool.tensor_tensor(small[:, 1:2], small[:, 0:1], half[:, 0:1], ALU.pow).then_inc(fin_g, 1)

            @block.tensor
            def _(pe):
                def body(j, u):
                    g = j * U + u
                    p, t = geometry(g)
                    pe.wait_ge(h_ready, g + 1)
                    for c in range(t):
                        first = isinstance(g, int) and g == 0 and c == 0
                        last = isinstance(g, int) and g == NG - 1 and c == t - 1
                        mm = pe.matmul(G[:, 0:D + 1], h[0:p, u, c, 0:D], h[0:p, u, c, :], start=first, stop=last)
                    mm.then_inc(h_used, 1)

                walk(pe, NG, 0, body)
                pe.wait_ge(fin_d, 1)
                pe.transpose(M_row[0:1, 0:D], gram[:, D:D + 1], ident[:]).then_inc(fin_p, 1)
                pe.wait_ge(fin_d, 2)
                pe.matmul(M[:, 0, 0:D], mean_row[:], mean_row[:], start=True, stop=True).then_inc(fin_p, 1)
                pe.wait_ge(fin_d, 3)
                pe.matmul(M[:, 1, 0:D], cov[:], W1T[:], start=True, stop=True).then_inc(fin_p, 1)
                pe.matmul(M[:, 3, 0:1], W1T[:], gram[:, D:D + 1], start=True, stop=True).then_inc(fin_p, 1)
                pe.wait_ge(fin_d, 4)
                pe.matmul(M[:, 2, 0:1], prod[:], ones[:], start=True, stop=True).then_inc(fin_p, 1)


class Norm:

    def __init__(self, part, nc, sem, name):
        def sb(what, last):
            return part.enter_context(nc.sbuf_tensor(f"{name}_{what}", [P, U, T] + last, F32))

        self.stat, self.both = sb("stat", [6]), sb("both", [2])
        self.gap, self.gap2, self.spread = sb("gap", []), sb("gap2", []), sb("spread", [])
        self.root, self.mean, self.rstd = sb("root", []), sb("mean", []), sb("rstd", [])
        self.stat_ready, self.both_ready = sem(f"{name}_stat_ready"), sem(f"{name}_both_ready")
        self.gap_ready, self.spread_ready = sem(f"{name}_gap_ready"), sem(f"{name}_spread_ready")
        self.root_ready, self.rstd_ready = sem(f"{name}_root_ready"), sem(f"{name}_rstd_ready")


def norm_stats(dve, n, y, p, t, u, g, y_ready):
    dve.wait_ge(y_ready, g + 1)
    for c in range(t):
        last = dve.bn_stats(n.stat[0:p, u, c, :], y[0:p, c, :])
    last.then_inc(n.stat_ready, 1)
    s = n.stat[0:p, u, 0:t]
    dve.wait_ge(n.stat_ready, g + 1)
    dve.tensor_tensor(n.gap[0:p, u, 0:t], s[:, :, 1], s[:, :, 4], ALU.subtract).then_inc(n.gap_ready, 1)
    dve.tensor_tensor(n.both[0:p, u, 0:t], s[:, :, 1:3], s[:, :, 4:6], ALU.add).then_inc(n.both_ready, 1)
    dve.wait_ge(n.gap_ready, 2 * g + 1)
    dve.scalar_tensor_tensor(out=n.gap2[0:p, u, 0:t], in0=n.gap[0:p, u, 0:t], scalar=D / 4.0,
                             in1=n.gap[0:p, u, 0:t], op0=ALU.mult, op1=ALU.mult).then_inc(n.gap_ready, 1)
    dve.wait_ge(n.gap_ready, 2 * g + 2)
    dve.scalar_tensor_tensor(out=n.spread[0:p, u, 0:t], in0=n.both[0:p, u, 0:t, 1], scalar=D * LN_EPS,
                             in1=n.gap2[0:p, u, 0:t], op0=ALU.add, op1=ALU.add).then_inc(n.spread_ready, 1)


def norm_root(pool, n, p, t, u, g, half, mid, root_d):
    pool.wait_ge(n.both_ready, g + 1)
    pool.tensor_tensor(n.mean[0:p, u, 0:t], n.both[0:p, u, 0:t, 0], mid[0:p, 0:t], ALU.mult)
    pool.wait_ge(n.spread_ready, g + 1)
    pool.tensor_tensor(n.root[0:p, u, 0:t], n.spread[0:p, u, 0:t], half[0:p, 0:t], ALU.pow)\
        .then_inc(n.root_ready, 1)
    pool.wait_ge(n.root_ready, g + 1)
    pool.tensor_tensor(n.rstd[0:p, u, 0:t], n.root[0:p, u, 0:t], root_d[0:p, 0:t], ALU.mult)\
        .then_inc(n.rstd_ready, 1)


def norm_apply(dve, n, to, y, p, t, u, g, ready):
    dve.wait_ge(n.rstd_ready, g + 1)
    for c in range(t):
        last = dve.tensor_scalar(to[0:p, c, :], y[0:p, c, :], n.mean[0:p, u, c:c + 1],
                                 n.rstd[0:p, u, c:c + 1], ALU.subtract, ALU.mult)
    last.then_inc(ready, 1)


def nodes0(nc, sem, NG, group, geometry, x, agg, x1, eps1, half, mid, root_d, ident, W1T, W2T, bn_scale, bn_shift,
           onesB, b2_3):
    with ExitStack() as part:
        def sb(name, shape, dt=F32):
            return part.enter_context(nc.sbuf_tensor(name, shape, dt))

        def ps(name):
            return part.enter_context(nc.psum_tensor(name, [P, 2, T * P], F32))

        xs = sb("n0_x", [P, U, T, D])
        ags = sb("n0_agg", [P, U, T, D])
        h = sb("n0_h", [P, U, T, D])
        hT = sb("n0_hT", [D, U, T * P])
        rT = sb("n0_rT", [D, U, T * P])
        y = sb("n0_y", [P, U, T, D])
        o = sb("n0_o", [P, U, T, D])
        turned, lin1, lin2 = ps("n0_turned"), ps("n0_lin1"), ps("n0_lin2")
        n1 = Norm(part, nc, sem, "n0_norm")

        x_in = [sem(f"n0_x_in{u}") for u in range(U)]
        agg_in = [sem(f"n0_agg_in{u}") for u in range(U)]
        x1_out = [sem(f"n0_x1_out{u}") for u in range(U)]
        h_ready, turned_ready, hT_ready = sem("n0_h_ready"), sem("n0_turned_ready"), sem("n0_hT_ready")
        lin1_ready, rT_ready, lin2_ready = sem("n0_lin1_ready"), sem("n0_rT_ready"), sem("n0_lin2_ready")
        y_ready, o_ready = sem("n0_y_ready"), sem("n0_o_ready")

        with nc.Block() as block:
            @block.sync
            def _(sp):
                def body(j, u):
                    g = j * U + u
                    if works(g, NG):
                        p, t = geometry(g)
                        if late(j):
                            sp.wait_ge(y_ready, g - U + 1)
                        sp.dma_start(xs[0:p, u, 0:t], group(x, g)).then_inc(x_in[u], 16)
                        sp.dma_start(ags[0:p, u, 0:t], group(agg, g)).then_inc(agg_in[u], 16)
                    jb, ub, gb = back(j, u, 4)
                    if works(gb, NG):
                        p, t = geometry(gb)
                        sp.wait_ge(o_ready, gb + 1)
                        sp.dma_start(group(x1, gb), o[0:p, ub, 0:t]).then_inc(x1_out[ub], 16)

                walk(sp, NG, 4, body)
                for u in range(U):
                    sp.wait_ge(x1_out[u], len(range(u, NG, U)) * 16)

            @block.vector
            def _(dve):
                def body(j, u):
                    g = j * U + u
                    if works(g, NG):
                        p, t = geometry(g)
                        dve.wait_ge(x_in[u], (j + 1) * 16)
                        dve.wait_ge(agg_in[u], (j + 1) * 16)
                        if late(j):
                            dve.wait_ge(turned_ready, g - U + 1)
                        dve.scalar_tensor_tensor(out=h[0:p, u, 0:t], in0=xs[0:p, u, 0:t], scalar=eps1[0:p],
                                                 in1=ags[0:p, u, 0:t], op0=ALU.mult, op1=ALU.add)\
                           .then_inc(h_ready, 1)
                    jb, ub, gb = back(j, u, 3)
                    if works(gb, NG):
                        p, t = geometry(gb)
                        dve.wait_ge(lin2_ready, gb + 1)
                        if late(jb):
                            dve.wait_ge(o_ready, gb - U + 1)
                        dve.tensor_tensor(y[0:p, ub, 0:t], lin2[0:p, gb_parity(ub), 0:t * D].rearrange(
                            "p (t d) -> p t d", d=D), xs[0:p, ub, 0:t], ALU.add).then_inc(y_ready, 1)
                        norm_stats(dve, n1, y[:, ub], p, t, ub, gb, y_ready)
                    jb, ub, gb = back(j, u, 4)
                    if works(gb, NG):
                        p, t = geometry(gb)
                        if late(jb):
                            dve.wait_ge(x1_out[ub], jb * 16)
                        norm_apply(dve, n1, o[:, ub], y[:, ub], p, t, ub, gb, o_ready)

                walk(dve, NG, 4, body)

            @block.gpsimd
            def _(pool):
                def body(j, u):
                    g = j * U + u
                    p, t = geometry(g)
                    norm_root(pool, n1, p, t, u, g, half, mid, root_d)

                walk(pool, NG, 0, body)

            @block.scalar
            def _(act):
                def body(j, u):
                    g = j * U + u
                    if works(g, NG):
                        p, t = geometry(g)
                        act.wait_ge(turned_ready, g + 1)
                        if late(j):
                            act.wait_ge(lin1_ready, g - U + 1)
                        act.activation(hT[:, u, 0:t * p], turned[:, u % 2, 0:t * p], ACT.Copy)\
                           .then_inc(hT_ready, 1)
                    jb, ub, gb = back(j, u, 1)
                    if works(gb, NG):
                        p, t = geometry(gb)
                        act.wait_ge(lin1_ready, gb + 1)
                        if late(jb):
                            act.wait_ge(lin2_ready, gb - U + 1)
                        act.activation(rT[:, ub, 0:t * p], lin1[:, gb_parity(ub), 0:t * p], ACT.Relu,
                                       bias=bn_shift[:], scale=bn_scale[:]).then_inc(rT_ready, 1)

                walk(act, NG, 1, body)

            @block.tensor
            def _(pe):
                def body(j, u):
                    g = j * U + u
                    if works(g, NG):
                        p, t = geometry(g)
                        pe.wait_ge(h_ready, g + 1)
                        if not isinstance(g, int) or g >= 2:
                            pe.wait_ge(hT_ready, g - 1)
                        for c in range(t):
                            mm = pe.transpose(turned[:, u % 2, c * p:(c + 1) * p], h[0:p, u, c, :], ident[0:p, 0:p])
                        mm.then_inc(turned_ready, 1)
                    jb, ub, gb = back(j, u, 1)
                    if works(gb, NG):
                        p, t = geometry(gb)
                        pe.wait_ge(hT_ready, gb + 1)
                        if not isinstance(gb, int) or gb >= 2:
                            pe.wait_ge(rT_ready, gb - 1)
                        pe.matmul(lin1[:, gb_parity(ub), 0:t * p], W1T[:], hT[:, ub, 0:t * p],
                                  start=True, stop=True).then_inc(lin1_ready, 1)
                    jb, ub, gb = back(j, u, 2)
                    if works(gb, NG):
                        p, t = geometry(gb)
                        pe.wait_ge(rT_ready, gb + 1)
                        if not isinstance(gb, int) or gb >= 2:
                            pe.wait_ge(y_ready, gb - 1)
                        add_bias(pe, lin2[0:p, gb_parity(ub), 0:t * D], onesB, b2_3, p, t)
                        for c in range(t):
                            mm = pe.matmul(lin2[0:p, gb_parity(ub), c * D:(c + 1) * D],
                                           rT[:, ub, c * p:(c + 1) * p], W2T[:], start=False, stop=(c == t - 1))
                        mm.then_inc(lin2_ready, 1)

                walk(pe, NG, 2, body)


def gb_parity(u):
    return u % 2


def add_bias(pe, to, onesB, bias_3, p, t):
    pe.matmul(to, onesB[:, 0:p], bias_3[:, 0:t].rearrange("r t d -> r (t d)"), start=True, stop=False)


def edges1(nc, sem, NB, E_LAST, N, x1, agg, edge_attr, side, soft_side, breaks, ident, idx_cols, dst_cols,
           Wq_s, Wk_s, Wv_s, We_s, onesB, bq_3):
    TH = T * H
    with ExitStack() as part:
        def sb(name, shape, dt=F32):
            return part.enter_context(nc.sbuf_tensor(name, shape, dt))

        def ps(name, shape):
            return part.enter_context(nc.psum_tensor(name, shape, F32))

        idx = sb("e1_idx", [P, U, 3, T], I32)
        dst_f = sb("e1_dst_f", [P, U, T])
        xs = sb("e1_xs", [P, U, T, D])
        xd = sb("e1_xd", [P, U, T, D])
        ea = sb("e1_ea", [P, U, T, DE + 1])
        brk = sb("e1_brk", [TH, U, P + 1])
        xsT = sb("e1_xsT", [D, T, P])
        xdT = sb("e1_xdT", [D, T, P])
        eaT = sb("e1_eaT", [DE + 1, T, P])
        q = sb("e1_q", [P, T * D])
        qk = sb("e1_qk", [P, T * D])
        logit = sb("e1_logit", [P, TH])
        run = sb("e1_run", [TH, P])
        top = sb("e1_top", [TH, P])
        diff = sb("e1_diff", [P, TH])
        ex = sb("e1_ex", [P, TH])
        exv = sb("e1_exv", [P, T, D])
        same = sb("e1_same", [P, T, P])
        rden = sb("e1_rden", [P, TH])
        att = sb("e1_att", [P, U, T, D])
        soft = sb("e1_soft", [P, U, T, 2 * H])
        xsT_p, xdT_p, eaT_p = ps("e1_xsT_p", [D, T, P]), ps("e1_xdT_p", [D, T, P]), ps("e1_eaT_p", [DE + 1, T, P])
        k_p, v_p, q_p = ps("e1_k_p", [P, T * D]), ps("e1_v_p", [P, T * D]), ps("e1_q_p", [P, T * D])
        wide = ps("e1_wide", [P, T, P])
        misc = ps("e1_misc", [P, 512])
        logitT_p = misc[0:TH, 0:P]
        top_p = misc[:, P:P + TH]
        den_p = misc[:, 2 * P:2 * P + TH]

        idx_ready, dstf_ready = sem("e1_idx_ready"), sem("e1_dstf_ready")
        xs_in = [sem(f"e1_xs_in{u}") for u in range(U)]
        xd_in = [sem(f"e1_xd_in{u}") for u in range(U)]
        ea_in = [sem(f"e1_ea_in{u}") for u in range(U)]
        brk_in = [sem(f"e1_brk_in{u}") for u in range(U)]
        scattered = [sem(f"e1_scattered{u}") for u in range(U)]
        sided = [sem(f"e1_sided{u}") for u in range(U)]
        begun = sem("e1_begun")
        ea_set, turned_ready, xT_ready = sem("e1_ea_set"), sem("e1_turned_ready"), sem("e1_xT_ready")
        kqv_ready, q_ready, qk_ready, logit_ready = sem("e1_kqv_ready"), sem("e1_q_ready"), sem("e1_qk_ready"), sem("e1_logit_ready")
        logitT_ready, run_ready, top_ready = sem("e1_logitT_ready"), sem("e1_run_ready"), sem("e1_top_ready")
        topT_ready, diff_ready, ex_ready = sem("e1_topT_ready"), sem("e1_diff_ready"), sem("e1_ex_ready")
        top_kept, spread_ready, same_ready = sem("e1_top_kept"), sem("e1_spread_ready"), sem("e1_same_ready")
        exv_ready, sums_ready, rden_ready, att_ready = sem("e1_exv_ready"), sem("e1_sums_ready"), sem("e1_rden_ready"), sem("e1_att_ready")
        den_kept = sem("e1_den_kept")

        with nc.Block() as block:
            @block.gpsimd
            def _(pool):
                last_row = pool.to_reg(N - 1)
                def body(j, u):
                    i = j * U + u
                    if works(i, NB):
                        now, free = ready_values(pool, i + 1, i - U + 1)
                        pool.wait_ge(begun, 1)
                        pool.wait_ge(idx_ready, now)
                        if late(j):
                            pool.wait_ge(turned_ready, free)
                        for t in range(T):
                            gather_rows(pool, xs[:, u, t, :], x1, idx[:, u, 0, t:t + 1].bitcast(U32), last_row)\
                                .then_inc(xs_in[u], 16)
                            gather_dst(pool, xd[:, u, t, :], x1, idx[:, u, 1, t:t + 1].bitcast(U32), last_row)\
                                .then_inc(xd_in[u], 16)
                    jb, ub, ib = back(j, u, 3)
                    if works(ib, NB):
                        (now,) = ready_values(pool, ib + 1)
                        pool.wait_ge(begun, 1)
                        pool.wait_ge(att_ready, now)
                        for t in range(T):
                            scatter_rows(pool, agg, idx[:, ub, 2, t:t + 1].bitcast(U32), att[:, ub, t, :], last_row)\
                                .then_inc(scattered[ub], 16)

                walk(pool, NB, 3, body)
                for u in range(U):
                    pool.wait_ge(scattered[u], len(range(u, NB, U)) * T * 16)

            @block.sync
            def _(sp):
                sp.wait_ge(ea_set, 1)

                def body(j, u):
                    i = j * U + u
                    if works(i, NB):
                        if late(j):
                            sp.wait_ge(turned_ready, i - U + 1)
                        if isinstance(i, int) and i == NB - 1:
                            full, rest = E_LAST // P, E_LAST % P
                            if full:
                                sp.dma_start(ea[:, u, 0:full, 0:DE],
                                             edge_attr[i * B:i * B + full * P].rearrange("(t p) d -> p t d", p=P))\
                                  .then_inc(ea_in[u], 16)
                            if rest:
                                sp.dma_start(ea[0:rest, u, full, 0:DE],
                                             edge_attr[i * B + full * P:i * B + E_LAST]).then_inc(ea_in[u], 16)
                        else:
                            sp.dma_start(ea[:, u, :, 0:DE],
                                         edge_attr[bass.ds(i * B, B)].rearrange("(t p) d -> p t d", p=P))\
                              .then_inc(ea_in[u], 16)
                        if late(j):
                            sp.wait_ge(top_ready, i - U + 1)
                        sp.dma_start(brk[:, u], breaks[bass.ds(i, 1)].rearrange("b t h e -> (b t h) e"))\
                          .then_inc(brk_in[u], 16)
                    jb, ub, ib = back(j, u, 3)
                    if works(ib, NB):
                        sp.wait_ge(att_ready, ib + 1)
                        sp.wait_ge(den_kept, ib + 1)
                        sp.wait_ge(top_kept, ib + 1)
                        for end, p in enumerate((0, P - 1)):
                            sp.dma_start(side_rows(side, ib, end), att[p:p + 1, ub]).then_inc(sided[ub], 16)
                            sp.dma_start(side_rows(soft_side, ib, end), soft[p:p + 1, ub]).then_inc(sided[ub], 16)

                walk(sp, NB, 3, body)
                for u in range(U):
                    sp.wait_ge(sided[u], len(range(u, NB, U)) * 64)

            @block.scalar
            def _(act):
                def body(j, u):
                    i = j * U + u
                    if works(i, NB):
                        act.wait_ge(turned_ready, i + 1)
                        if not isinstance(i, int) or i >= 1:
                            act.wait_ge(kqv_ready, i)
                        act.activation(xsT[:], xsT_p[:], ACT.Copy)
                        act.activation(xdT[:], xdT_p[:], ACT.Copy)
                        act.activation(eaT[:], eaT_p[:], ACT.Copy).then_inc(xT_ready, 1)
                    jb, ub, ib = back(j, u, 1)
                    if works(ib, NB):
                        act.wait_ge(diff_ready, ib + 1)
                        if not isinstance(ib, int) or ib >= 1:
                            act.wait_ge(sums_ready, ib)
                        act.activation(ex[:], diff[:], ACT.Exp, scale=float(C) ** -0.5).then_inc(ex_ready, 1)
                    if works(i, NB):
                        act.wait_ge(kqv_ready, i + 1)
                        if not isinstance(i, int) or i >= 1:
                            act.wait_ge(qk_ready, i)
                        act.activation(q[:], q_p[:], ACT.Copy).then_inc(q_ready, 1)

                walk(act, NB, 1, body)

            @block.vector
            def _(dve):
                dve.memset(ea[:], 1.0).then_inc(ea_set, 1)
                dve.memset(xd[:], 0.0).then_inc(begun, 1)

                def body(j, u):
                    i = j * U + u
                    if works(i, NB):
                        if late(j):
                            dve.wait_ge(scattered[u], j * T * 16)
                        prepare_batch(dve, i, u, idx, dst_f, idx_cols, dst_cols, idx_ready, dstf_ready)
                    jb, ub, ib = back(j, u, 2)
                    if works(ib, NB):
                        dve.wait_ge(sums_ready, ib + 1)
                        dve.reciprocal(rden[:], den_p).then_inc(rden_ready, 1)
                        if late(jb):
                            dve.wait_ge(sided[ub], jb * 64)
                            dve.wait_ge(scattered[ub], jb * T * 16)
                        dve.tensor_copy(soft[:, ub, :, H:2 * H], den_p.rearrange("p (t h) -> p t h", h=H))\
                           .then_inc(den_kept, 1)
                        dve.wait_ge(rden_ready, ib + 1)
                        dve.tensor_tensor(att[:, ub].rearrange("p t (h c) -> p (t h) c", c=C),
                                          wide[:].rearrange("p t (h c) -> p (t h) c", c=C),
                                          rden[:].unsqueeze(2).to_broadcast([P, TH, C]), ALU.mult)\
                           .then_inc(att_ready, 1)
                    jb, ub, ib = back(j, u, 1)
                    if works(ib, NB):
                        dve.wait_ge(q_ready, ib + 1)
                        dve.tensor_tensor(qk[:], k_p[:], q[:], ALU.mult).then_inc(qk_ready, 1)
                        dve.wait_ge(qk_ready, ib + 1)
                        dve.tensor_reduce(logit[:], qk[:].rearrange("p (n c) -> p n c", c=C),
                                          mybir.AxisListType.X, ALU.add).then_inc(logit_ready, 1)
                        dve.wait_ge(logitT_ready, ib + 1)
                        dve.wait_ge(brk_in[ub], (jb + 1) * 16)
                        dve.tensor_tensor_scan(run[:], brk[:, ub, 0:P], logitT_p, LOW, ALU.add, ALU.max)\
                           .then_inc(run_ready, 1)
                        dve.wait_ge(run_ready, ib + 1)
                        dve.tensor_tensor_scan(top[:, ::-1], brk[:, ub, 1:P + 1][:, ::-1], run[:, ::-1], LOW,
                                               ALU.add, ALU.max).then_inc(top_ready, 1)
                        dve.wait_ge(spread_ready, ib + 1)
                        dve.wait_ge(dstf_ready, ib + 1)
                        dve.tensor_tensor(same[:], wide[:], dst_f[:, ub].unsqueeze(2).to_broadcast([P, T, P]),
                                          ALU.is_equal).then_inc(same_ready, 1)
                        dve.wait_ge(topT_ready, ib + 1)
                        dve.tensor_tensor(diff[:], logit[:], top_p, ALU.subtract).then_inc(diff_ready, 1)
                        if late(jb):
                            dve.wait_ge(sided[ub], jb * 64)
                        dve.tensor_copy(soft[:, ub, :, 0:H], top_p.rearrange("p (t h) -> p t h", h=H))\
                           .then_inc(top_kept, 1)
                        dve.wait_ge(ex_ready, ib + 1)
                        dve.tensor_tensor(exv[:].rearrange("p t (h c) -> p (t h) c", c=C),
                                          v_p[:].rearrange("p (n c) -> p n c", c=C),
                                          ex[:].unsqueeze(2).to_broadcast([P, TH, C]), ALU.mult)\
                           .then_inc(exv_ready, 1)

                walk(dve, NB, 2, body)

            @block.tensor
            def _(pe):
                def body(j, u):
                    i = j * U + u
                    if works(i, NB):
                        pe.wait_ge(xs_in[u], (j + 1) * T * 16)
                        pe.wait_ge(xd_in[u], (j + 1) * T * 16)
                        split = 2 if isinstance(i, int) and i == NB - 1 and E_LAST >= P and E_LAST % P else 1
                        pe.wait_ge(ea_in[u], (j + split) * 16)
                        if not isinstance(i, int) or i >= 1:
                            pe.wait_ge(xT_ready, i)
                        for t in range(T):
                            pe.transpose(xsT_p[:, t], xs[:, u, t], ident[:])
                            pe.transpose(xdT_p[:, t], xd[:, u, t], ident[:])
                            mm = pe.transpose(eaT_p[:, t], ea[:, u, t], ident[:])
                        mm.then_inc(turned_ready, 1)
                    jb, ub, ib = back(j, u, 1)
                    if works(ib, NB):
                        pe.wait_ge(logit_ready, ib + 1)
                        pe.transpose(logitT_p, logit[:], ident[:]).then_inc(logitT_ready, 1)
                        pe.wait_ge(dstf_ready, ib + 1)
                        if not isinstance(ib, int) or ib >= 1:
                            pe.wait_ge(att_ready, ib)
                            pe.wait_ge(den_kept, ib)
                        pe.wait_ge(top_ready, ib + 1)
                        for t in range(T):
                            mm = pe.transpose(wide[:, t, :], dst_f[:, ub, t:t + 1].to_broadcast([P, P]), ident[:])
                        mm.then_inc(spread_ready, 1)
                        pe.transpose(top_p, top[:], ident[0:TH, 0:TH]).then_inc(topT_ready, 1)
                        pe.wait_ge(exv_ready, ib + 1)
                        for t in range(T):
                            pe.matmul(wide[:, t, :], same[:, t, :], exv[:, t, :], start=True, stop=True)
                            mm = pe.matmul(den_p[:, t * H:(t + 1) * H], same[:, t, :], ex[:, t * H:(t + 1) * H],
                                           start=True, stop=True)
                        mm.then_inc(sums_ready, 1)
                    if works(i, NB):
                        pe.wait_ge(xT_ready, i + 1)
                        if not isinstance(i, int) or i >= 1:
                            pe.wait_ge(q_ready, i)
                        add_bias(pe, q_p[:], onesB, bq_3, P, T)
                        for t in range(T):
                            pe.matmul(q_p[:, t * D:(t + 1) * D], xdT[:, t], Wq_s[:], start=False, stop=(t == T - 1))
                        for t in range(T):
                            for n, (to, w) in enumerate(((k_p, Wk_s), (v_p, Wv_s))):
                                o = to[:, t * D:(t + 1) * D]
                                pe.matmul(o, xsT[:, t], w[:], start=True, stop=False)
                                mm = pe.matmul(o, eaT[:, t], We_s[:, n, :], start=False, stop=True)
                        mm.then_inc(kqv_ready, 1)

                walk(pe, NB, 1, body)


def gather_dst(pool, rows, dram, index, last_row):
    return pool.indirect_dma_start(rows, None, dram, bass.IndirectOffsetOnAxis(index, 0), bounds_check=last_row,
                                   oob_is_err=False)


def joins1(nc, sem, NI, CI, PI, side, soft_side, agg, ident, same_item, count_item, row_item, head_of, N):
    with ExitStack() as part:
        def sb(name, shape, dt=F32):
            return part.enter_context(nc.sbuf_tensor(name, shape, dt))

        items = sb("j1_items", [PI, CI, D])
        soft = sb("j1_soft", [PI, CI, 2 * H])
        av = sb("j1_av", [D, NI])
        brk = sb("j1_brk", [H, NI + 1])
        top = sb("j1_top", [H, NI])
        run = sb("j1_run", [H, NI])
        whole = sb("j1_whole", [H, NI])
        den = sb("j1_den", [H, NI])
        w = sb("j1_w", [H, NI])
        num_run = sb("j1_num_run", [D, NI])
        den_run = sb("j1_den_run", [D, NI])
        W8 = -(-CI // 2)
        turn = part.enter_context(nc.psum_tensor("j1_turn", [P, 2, 2, 512], F32))
        s_in, s_turn, s_v, s_p = sem("j1_in"), sem("j1_turned"), sem("j1_vector_steps"), sem("j1_product_steps")
        s_a, s_rows, s_out, s_rt = sem("j1_act_steps"), sem("j1_rows"), sem("j1_out"), sem("j1_rows_turned")
        s_rt2 = sem("j1_scans")
        chunks = [(c * PI, min(CI, c + W8) * PI) for c in range(0, CI, W8)]
        assert all(b - a <= 512 for a, b in chunks) and H <= 32

        with nc.Block() as block:
            @block.sync
            def _(sp):
                sp.dma_start(items[:], side.rearrange("(c p) d -> p c d", p=PI)).then_inc(s_in, 16)
                sp.dma_start(soft[:], soft_side.rearrange("(c p) d -> p c d", p=PI)).then_inc(s_in, 16)

            @block.tensor
            def _(pe):
                def col(n, c):
                    k, r = divmod(c, W8)
                    return turn[:, n, k, r * PI:(r + 1) * PI]

                pe.wait_ge(s_in, 32)
                for c in range(CI):
                    pe.transpose(col(0, c)[0:H], soft[:, c, 0:H], ident[0:PI, 0:PI])
                    mm = pe.transpose(col(1, c)[0:H], soft[:, c, H:2 * H], ident[0:PI, 0:PI])
                mm.then_inc(s_turn, 1)
                pe.wait_ge(s_v, 2)
                for c in range(CI):
                    mm = pe.transpose(col(0, c), items[:, c, :], ident[0:PI, 0:PI])
                mm.then_inc(s_turn, 1)
                pe.wait_ge(s_v, 8)
                for k, (a, b) in enumerate(chunks):
                    mm = pe.matmul(turn[:, 1, k, 0:b - a], head_of[:], w[:, a:b], start=True, stop=True)
                mm.then_inc(s_p, 1)
                for c in range(CI):
                    if c == 0:
                        pe.wait_ge(s_v, 14)
                    elif c % 4 == 0:
                        pe.wait_ge(s_rows, c // 4)
                    mm = pe.transpose(turn[0:PI, 0, 0, (c % 4) * P:(c % 4 + 1) * P],
                                      av[:, c * PI:(c + 1) * PI], ident[:])
                    if c % 4 == 3 or c == CI - 1:
                        mm.then_inc(s_rt, 1)

            @block.scalar
            def _(act):
                act.wait_ge(s_v, 6)
                act.activation(w[:], w[:], ACT.Exp, scale=float(C) ** -0.5).then_inc(s_a, 1)

            @block.vector
            def _(dve):
                def halves(to, n, rows):
                    for k, (a, b) in enumerate(chunks):
                        last = dve.tensor_copy(to[:, a:b], turn[0:rows, n, k, 0:b - a])
                    return last

                dve.wait_ge(s_turn, 1)
                halves(top, 0, H).then_inc(s_v, 1)
                halves(den, 1, H).then_inc(s_v, 1)
                dve.memset(brk[:], LOW).then_inc(s_v, 1)
                dve.wait_ge(s_v, 3)
                dve.tensor_scalar(brk[:, 0:NI], same_item[0:H], -1.0, -LOW, ALU.add, ALU.mult).then_inc(s_v, 1)
                dve.wait_ge(s_v, 4)
                dve.tensor_tensor_scan(run[:], brk[:, 0:NI], top[:], LOW, ALU.add, ALU.max).then_inc(s_v, 1)
                dve.wait_ge(s_v, 5)
                dve.tensor_tensor_scan(whole[:, ::-1], brk[:, 1:NI + 1][:, ::-1], run[:, ::-1], LOW,
                                       ALU.add, ALU.max).then_inc(s_rt2, 1)
                dve.wait_ge(s_rt2, 1)
                dve.tensor_tensor(w[:], top[:], whole[:], ALU.subtract).then_inc(s_v, 1)
                dve.wait_ge(s_a, 1)
                dve.tensor_tensor(w[:], w[:], den[:], ALU.mult).then_inc(s_v, 1)
                dve.wait_ge(s_v, 7)
                dve.tensor_tensor(w[:], w[:], count_item[0:H], ALU.mult).then_inc(s_v, 1)
                dve.wait_ge(s_turn, 2)
                halves(av, 0, D).then_inc(s_v, 1)
                dve.wait_ge(s_p, 1)
                halves(den_run, 1, D).then_inc(s_v, 1)
                dve.wait_ge(s_v, 10)
                dve.tensor_tensor(av[:], av[:], den_run[:], ALU.mult).then_inc(s_v, 1)
                dve.wait_ge(s_v, 11)
                dve.tensor_tensor_scan(num_run[:], same_item[:], av[:], 0.0, ALU.mult, ALU.add).then_inc(s_v, 1)
                dve.wait_ge(s_v, 12)
                dve.tensor_tensor_scan(av[:], same_item[:], den_run[:], 0.0, ALU.mult, ALU.add).then_inc(s_rt2, 1)
                dve.wait_ge(s_rt2, 2)
                dve.reciprocal(den_run[:], av[:]).then_inc(s_v, 1)
                dve.wait_ge(s_v, 13)
                dve.tensor_tensor(av[:], num_run[:], den_run[:], ALU.mult).then_inc(s_v, 1)
                for c in range(0, CI, 4):
                    n = min(4, CI - c)
                    dve.wait_ge(s_rt, c // 4 + 1)
                    dve.tensor_copy(items[:, c:c + n, :].rearrange("p c d -> p (c d)"), turn[0:PI, 0, 0, 0:n * P])\
                       .then_inc(s_rows, 1)

            @block.gpsimd
            def _(pool):
                for c in range(CI):
                    if c % 4 == 0:
                        pool.wait_ge(s_rows, c // 4 + 1)
                    scatter_rows(pool, agg, row_item[:, c:c + 1].bitcast(U32), items[:, c, :], N - 1)\
                        .then_inc(s_out, 16)
                pool.wait_ge(s_out, CI * 16)


def nodes1(nc, sem, NG, group, geometry, x1, agg, out, half, mid, root_d, ident, Wskip_s, Wf1_s, Wf2_s, onesB,
           bskip_3, bf2_3, g1_col, b1_col, bf1_col, g1_row, g2_row, b2n_row):
    F = FF // D
    with ExitStack() as part:
        def sb(name, shape, dt=F32):
            return part.enter_context(nc.sbuf_tensor(name, shape, dt))

        def ps(name, shape):
            return part.enter_context(nc.psum_tensor(name, shape, F32))

        xs, ags = sb("n1_x", [P, U, T, D]), sb("n1_agg", [P, U, T, D])
        xT = sb("n1_xT", [D, 2, T * P])
        y, z = sb("n1_y", [P, 2, T, D]), sb("n1_z", [P, U, T, D])
        zg = sb("n1_zg", [P, U, T, D])
        xb = sb("n1_xb", [P, U, T, D])
        hT = sb("n1_hT", [D, 2, T * P])
        act_T = sb("n1_act_T", [D, 2, F, T * P])
        w, wn = sb("n1_w", [P, 2, T, D]), sb("n1_wn", [P, 2, T, D])
        wg = sb("n1_wg", [P, 2, T, D])
        r, o = sb("n1_r", [P, 2, T, D]), sb("n1_o", [P, U, T, D])
        xT_p, skip_p = ps("n1_xT_p", [D, T * P]), ps("n1_skip_p", [P, T * D])
        zT_p, lin2_p = ps("n1_zT_p", [D, T * P]), ps("n1_lin2_p", [P, T * D])
        lin1_p = ps("n1_lin1_p", [D, F, T * P])
        nm1, nm2, nm3 = (Norm(part, nc, sem, f"n1_norm{k}") for k in (1, 2, 3))

        x_in = [sem(f"n1_x_in{u}") for u in range(U)]
        agg_in = [sem(f"n1_agg_in{u}") for u in range(U)]
        stored = [sem(f"n1_stored{u}") for u in range(U)]
        xT_p_ready, xT_ready, skip_ready = sem("n1_xT_p_ready"), sem("n1_xT_ready"), sem("n1_skip_ready")
        y_ready, z_ready, zT_p_ready = sem("n1_y_ready"), sem("n1_z_ready"), sem("n1_zT_p_ready")
        hT_ready, lin1_ready, gelu_ready = sem("n1_hT_ready"), sem("n1_lin1_ready"), sem("n1_gelu_ready")
        lin2_ready, w_ready, wn_ready = sem("n1_lin2_ready"), sem("n1_w_ready"), sem("n1_wn_ready")
        zg_ready, wg_ready, xb_ready = sem("n1_zg_ready"), sem("n1_wg_ready"), sem("n1_xb_ready")
        r_ready, o_ready = sem("n1_r_ready"), sem("n1_o_ready")

        def rows(psum, p, t):
            return psum[0:p, 0:t * D].rearrange("p (t d) -> p t d", d=D)

        with nc.Block() as block:
            @block.sync
            def _(sp):
                def body(j, u):
                    g = j * U + u
                    if works(g, NG):
                        p, t = geometry(g)
                        if late(j):
                            sp.wait_ge(xT_p_ready, g - U + 1)
                            sp.wait_ge(xb_ready, g - U + 1)
                            sp.wait_ge(y_ready, g - U + 1)
                        sp.dma_start(xs[0:p, u, 0:t], group(x1, g)).then_inc(x_in[u], 16)
                        sp.dma_start(ags[0:p, u, 0:t], group(agg, g)).then_inc(agg_in[u], 16)

                walk(sp, NG, 0, body)

            @block.tensor
            def _(pe):
                def body(j, u):
                    g = j * U + u
                    if works(g, NG):
                        p, t = geometry(g)
                        pe.wait_ge(x_in[u], (j + 1) * 16)
                        if not isinstance(g, int) or g >= 1:
                            pe.wait_ge(xT_ready, g)
                        for c in range(t):
                            mm = pe.transpose(xT_p[:, c * p:(c + 1) * p], xs[0:p, u, c, :], ident[0:p, 0:p])
                        mm.then_inc(xT_p_ready, 1)
                    jb, ub, gb = back(j, u, 2)
                    if works(gb, NG):
                        p, t = geometry(gb)
                        pe.wait_ge(z_ready, gb + 1)
                        if not isinstance(gb, int) or gb >= 1:
                            pe.wait_ge(hT_ready, gb)
                        for c in range(t):
                            mm = pe.transpose(zT_p[:, c * p:(c + 1) * p], z[0:p, ub, c, :], ident[0:p, 0:p])
                        mm.then_inc(zT_p_ready, 1)
                    jb, ub, gb = back(j, u, 3)
                    if works(gb, NG):
                        p, t = geometry(gb)
                        pe.wait_ge(gelu_ready, F * gb + F)
                        if not isinstance(gb, int) or gb >= 1:
                            pe.wait_ge(w_ready, gb)
                        add_bias(pe, lin2_p[0:p, 0:t * D], onesB, bf2_3, p, t)
                        for c in range(t):
                            for f in range(F):
                                mm = pe.matmul(lin2_p[0:p, c * D:(c + 1) * D],
                                               act_T[:, ub % 2, f, c * p:(c + 1) * p], Wf2_s[:, f, :],
                                               start=False, stop=(c == t - 1 and f == F - 1))
                        mm.then_inc(lin2_ready, 1)
                    if works(g, NG):
                        p, t = geometry(g)
                        pe.wait_ge(xT_ready, g + 1)
                        if not isinstance(g, int) or g >= 1:
                            pe.wait_ge(y_ready, g)
                        add_bias(pe, skip_p[0:p, 0:t * D], onesB, bskip_3, p, t)
                        for c in range(t):
                            mm = pe.matmul(skip_p[0:p, c * D:(c + 1) * D], xT[:, u % 2, c * p:(c + 1) * p],
                                           Wskip_s[:], start=False, stop=(c == t - 1))
                        mm.then_inc(skip_ready, 1)
                    jb, ub, gb = back(j, u, 2)
                    if works(gb, NG):
                        p, t = geometry(gb)
                        pe.wait_ge(hT_ready, gb + 1)
                        for f in range(F):
                            if not isinstance(gb, int) or gb >= 1:
                                pe.wait_ge(gelu_ready, F * gb - F + f + 1)
                            pe.matmul(lin1_p[:, f, 0:t * p], Wf1_s[:, f * D:(f + 1) * D], hT[:, ub % 2, 0:t * p],
                                      start=True, stop=True).then_inc(lin1_ready, 1)

                walk(pe, NG, 3, body)

            @block.scalar
            def _(act):
                def body(j, u):
                    g = j * U + u
                    if works(g, NG):
                        p, t = geometry(g)
                        act.wait_ge(xT_p_ready, g + 1)
                        if not isinstance(g, int) or g >= 2:
                            act.wait_ge(skip_ready, g - 1)
                        act.activation(xT[:, u % 2, 0:t * p], xT_p[:, 0:t * p], ACT.Copy).then_inc(xT_ready, 1)
                    jb, ub, gb = back(j, u, 2)
                    if works(gb, NG):
                        p, t = geometry(gb)
                        act.wait_ge(zT_p_ready, gb + 1)
                        if not isinstance(gb, int) or gb >= 2:
                            act.wait_ge(lin1_ready, F * gb - F)
                        act.activation(hT[:, ub % 2, 0:t * p], zT_p[:, 0:t * p], ACT.Identity, bias=b1_col[:],
                                       scale=g1_col[:]).then_inc(hT_ready, 1)
                        if not isinstance(gb, int) or gb >= 2:
                            act.wait_ge(lin2_ready, gb - 1)
                        for f in range(F):
                            act.wait_ge(lin1_ready, F * gb + f + 1)
                            act.activation(act_T[:, ub % 2, f, 0:t * p], lin1_p[:, f, 0:t * p], ACT.Gelu,
                                           bias=bf1_col[:, f:f + 1]).then_inc(gelu_ready, 1)
                    jb, ub, gb = back(j, u, 6)
                    if works(gb, NG):
                        p, t = geometry(gb)
                        act.wait_ge(o_ready, gb + 1)
                        act.dma_start(group(out, gb), o[0:p, ub, 0:t]).then_inc(stored[ub], 16)

                walk(act, NG, 6, body)
                for u in range(U):
                    act.wait_ge(stored[u], len(range(u, NG, U)) * 16)

            @block.vector
            def _(dve):
                def body(j, u):
                    g = j * U + u
                    jb, ub, gb = back(j, u, 5)
                    if works(gb, NG):
                        p, t = geometry(gb)
                        if late(jb):
                            dve.wait_ge(stored[ub], jb * 16)
                        norm_apply(dve, nm3, o[:, ub], r[:, ub % 2], p, t, ub, gb, o_ready)
                    jb, ub, gb = back(j, u, 4)
                    if works(gb, NG):
                        p, t = geometry(gb)
                        dve.wait_ge(wg_ready, gb + 1)
                        dve.wait_ge(xb_ready, gb + 1)
                        dve.tensor_tensor(r[0:p, ub % 2, 0:t], wg[0:p, ub % 2, 0:t], xb[0:p, ub, 0:t], ALU.add)\
                           .then_inc(r_ready, 1)
                        norm_stats(dve, nm3, r[:, ub % 2], p, t, ub, gb, r_ready)
                    if works(g, NG):
                        p, t = geometry(g)
                        dve.wait_ge(skip_ready, g + 1)
                        dve.wait_ge(agg_in[u], (j + 1) * 16)
                        dve.tensor_tensor(y[0:p, u % 2, 0:t], rows(skip_p, p, t), ags[0:p, u, 0:t], ALU.add)\
                           .then_inc(y_ready, 1)
                        norm_stats(dve, nm1, y[:, u % 2], p, t, u, g, y_ready)
                    jb, ub, gb = back(j, u, 3)
                    if works(gb, NG):
                        p, t = geometry(gb)
                        dve.wait_ge(lin2_ready, gb + 1)
                        dve.wait_ge(zg_ready, gb + 1)
                        dve.tensor_tensor(w[0:p, ub % 2, 0:t], rows(lin2_p, p, t), zg[0:p, ub, 0:t], ALU.add)\
                           .then_inc(w_ready, 1)
                        norm_stats(dve, nm2, w[:, ub % 2], p, t, ub, gb, w_ready)
                    if works(g, NG):
                        p, t = geometry(g)
                        if late(j):
                            dve.wait_ge(zT_p_ready, g - U + 1)
                            dve.wait_ge(zg_ready, g - U + 1)
                        norm_apply(dve, nm1, z[:, u], y[:, u % 2], p, t, u, g, z_ready)
                    if works(gb, NG):
                        p, t = geometry(gb)
                        if not isinstance(gb, int) or gb >= 2:
                            dve.wait_ge(wg_ready, gb - 1)
                        norm_apply(dve, nm2, wn[:, ub % 2], w[:, ub % 2], p, t, ub, gb, wn_ready)

                walk(dve, NG, 5, body)

            @block.gpsimd
            def _(pool):
                def body(j, u):
                    g = j * U + u
                    if works(g, NG):
                        p, t = geometry(g)
                        if late(j):
                            pool.wait_ge(r_ready, g - U + 1)
                        pool.wait_ge(x_in[u], (j + 1) * 16)
                        pool.tensor_tensor(xb[0:p, u, 0:t], xs[0:p, u, 0:t], b2n_row[0:p, 0:t], ALU.add)\
                            .then_inc(xb_ready, 1)
                    jb, ub, gb = back(j, u, 4)
                    if works(gb, NG):
                        p, t = geometry(gb)
                        norm_root(pool, nm3, p, t, ub, gb, half, mid, root_d)
                    if works(g, NG):
                        p, t = geometry(g)
                        norm_root(pool, nm1, p, t, u, g, half, mid, root_d)
                    jb, ub, gb = back(j, u, 3)
                    if works(gb, NG):
                        pb, tb = geometry(gb)
                        norm_root(pool, nm2, pb, tb, ub, gb, half, mid, root_d)
                    if works(g, NG):
                        pool.wait_ge(z_ready, g + 1)
                        if late(j):
                            pool.wait_ge(w_ready, g - U + 1)
                        pool.tensor_tensor(zg[0:p, u, 0:t], z[0:p, u, 0:t], g1_row[0:p, 0:t], ALU.mult)\
                            .then_inc(zg_ready, 1)
                    if works(gb, NG):
                        pool.wait_ge(wn_ready, gb + 1)
                        if not isinstance(gb, int) or gb >= 2:
                            pool.wait_ge(r_ready, gb - 1)
                        pool.tensor_tensor(wg[0:pb, ub % 2, 0:tb], wn[0:pb, ub % 2, 0:tb], g2_row[0:pb, 0:tb],
                                           ALU.mult).then_inc(wg_ready, 1)

                walk(pool, NG, 4, body)


_INS = ['x', 'src', 'dst', 'edge_attr_64', 'L0_gnn_W1', 'L0_gnn_gamma', 'L0_gnn_beta', 'L0_gnn_W2', 'L0_gnn_b2',
        'L0_gnn_eps', 'L1_gnn_Wq', 'L1_gnn_bq', 'L1_gnn_Wk', 'L1_gnn_bk', 'L1_gnn_Wv', 'L1_gnn_bv', 'L1_gnn_We',
        'L1_gnn_Wskip', 'L1_gnn_bskip', 'L1_gnn_g1', 'L1_gnn_b1', 'L1_gnn_g2', 'L1_gnn_b2', 'L1_gnn_Wf1',
        'L1_gnn_bf1', 'L1_gnn_Wf2', 'L1_gnn_bf2']


def kernel(**inputs):
    import numpy as _np
    import concourse.bacc as _bacc
    from concourse.bass_utils import run_bass_kernel_spmd as _run

    nc = _bacc.Bacc("TRN2", target_bir_lowering=False, num_devices=1)
    arrays, args = {}, []
    for name in _INS:
        a = _np.ascontiguousarray(inputs[name])
        if a.ndim == 0:
            a = a.reshape(1)
        arrays[f"in_{name}"] = a
        args.append(nc.dram_tensor(f"in_{name}", a.shape, mybir.dt.from_np(a.dtype), kind="ExternalInput").ap())
    n = inputs['x'].shape[0]
    args.append(nc.dram_tensor("out_0", (n, D), F32, kind="ExternalOutput").ap())
    build(nc, *args)
    r = _run(nc, [arrays], core_ids=[0])
    return r.results[0]["out_0"]
```

```python
from contextlib import ExitStack

import concourse.bass as bass
from concourse import mybir

ALU = mybir.AluOpType
ACT = mybir.ActivationFunctionType
F32 = mybir.dt.float32
BF16 = mybir.dt.bfloat16
I32 = mybir.dt.int32
U32 = mybir.dt.uint32

P = 128
D = 128
T = 4
B = T * P
H = 8
C = D // H
DE = 64
FF = 4 * D
U = 8
S = 4
AHEAD = 2
LN_EPS = 1e-5
BN_EPS = 1e-5
LOW = -1e30
PAD = 200000
SKIP = 1 << 20


def walk(eng, steps, lag, body):
    full = (steps - 1) // U
    if full <= 2:
        for i in range(steps + lag):
            body(i // U, i % U)
        return
    for i in range(2 * U):
        body(i // U, i % U)
    with eng.Fori(2, full) as j:
        for u in range(U):
            body(j, u)
    for i in range(full * U, steps + lag):
        body(i // U, i % U)


def turn_of(j, u):
    return j * (U // S) + u // S, u % S


def back(j, u, lag):
    k = u - lag
    return j + k // U, k % U, j * U + k


def ready_values(eng, *values):
    return [v if isinstance(v, int) else eng.to_reg(v) for v in values]


def works(i, steps):
    return not isinstance(i, int) or 0 <= i < steps


def late(j, n=1):
    return not isinstance(j, int) or j >= n


def build(nc, x, src, dst, edge_attr, W1, gamma, beta, W2, b2, eps, Wq, bq, Wk, bk, Wv, bv, We, Wskip, bskip,
          g1, b1, g2, b2n, Wf1, bf1, Wf2, bf2, out):
    N = x.shape[0]
    E = src.shape[0]
    NB = -(-E // B)
    NG = -(-N // B)
    E_LAST = E - (NB - 1) * B
    N_LAST = N - (NG - 1) * B
    P_LAST = next(p for p in (128, 112, 96, 80, 64, 48, 32, 16) if N_LAST % p == 0 and N_LAST // p <= T)
    T_LAST = N_LAST // P_LAST
    NI = NB * T * 2
    CI = next(c for c in range(1, NI + 1) if NI % c == 0 and NI // c <= P)
    PI = NI // CI
    ZC = next(c for c in range(4096, 0, -1) if N % c == 0)

    agg = nc.dram_tensor("agg", [N, D], F32).ap()
    x1 = nc.dram_tensor("x1", [N, D], F32).ap()
    rows_side = nc.dram_tensor("rows_side", [2, NI, D], F32).ap()
    soft_side = nc.dram_tensor("soft_side", [NI, 2 * H], F32).ap()
    breaks = nc.dram_tensor("breaks", [NB, T, H, P + 1], F32).ap()
    keys = nc.dram_tensor("keys", [1, NI], F32).ap()
    key_rows = nc.dram_tensor("key_rows", [1, NI], I32).ap()

    def geometry(g):
        if isinstance(g, int) and g == NG - 1:
            return P_LAST, T_LAST
        return P, T

    def group(dram, g):
        p, t = geometry(g)
        rows = dram[bass.ds(g * B, p * t), :] if not isinstance(g, int) else dram[g * B:g * B + p * t, :]
        return rows.rearrange("(p t) d -> p t d", t=t)

    with ExitStack() as ctx:
        def keep(name, shape, dt=F32):
            return ctx.enter_context(nc.sbuf_tensor(name, shape, dt))

        zeros = keep("zeros", [P, ZC])
        s_zero = nc.alloc_semaphore("agg_zeroed")
        part_sems = []

        def sem(name):
            part_sems.append(nc.alloc_semaphore(name))
            return part_sems[-1]

        def clear():
            nc.clear_and_free_semaphores(part_sems[:])
            nc.all_engine_barrier()
            part_sems.clear()

        ident = keep("ident", [P, P])
        idx_cols = keep("idx_cols", [P, NB, 3, T], I32)
        dst_cols = keep("dst_cols", [P, NB, T])
        same_item = keep("same_item", [P, NI])
        count_item = keep("count_item", [P, NI])
        row_item = keep("row_item", [PI, CI], I32)
        W1T = keep("W1T", [D, D])
        W2T = keep("W2T", [D, D])
        Wq_s = keep("Wq_s", [D, D])
        Wk_s = keep("Wk_s", [D, D])
        Wv_s = keep("Wv_s", [D, D])
        We_s = keep("We_s", [DE + 1, 2, D])
        Wskip_s = keep("Wskip_s", [D, D])
        Wf1_s = keep("Wf1_s", [D, FF])
        Wf2_s = keep("Wf2_s", [D, T, D])
        onesB = keep("onesB", [3, P], BF16)
        b2_3 = keep("b2_3", [3, T, D], BF16)
        bq_3 = keep("bq_3", [3, T, D], BF16)
        bskip_3 = keep("bskip_3", [3, T, D], BF16)
        bf2_3 = keep("bf2_3", [3, T, D], BF16)
        g1_col = keep("g1_col", [D, 1])
        b1_col = keep("b1_col", [D, 1])
        bf1_col = keep("bf1_col", [D, T])
        g1_row = keep("g1_row", [P, T, D])
        g2_row = keep("g2_row", [P, T, D])
        b2n_row = keep("b2n_row", [P, T, D])
        gamma_col = keep("gamma_col", [D, 1])
        beta_col = keep("beta_col", [D, 1])
        eps1 = keep("eps1", [P, 1])
        half = keep("half", [P, T])
        mid = keep("mid", [P, T])
        root_d = keep("root_d", [P, T])
        bn_scale = keep("bn_scale", [D, 1])
        bn_shift = keep("bn_shift", [D, 1])
        head_of = keep("head_of", [H, D])

        with ExitStack() as part:
            def sb(name, shape, dt=F32):
                return part.enter_context(nc.sbuf_tensor(name, shape, dt))

            def ps(name, shape):
                return part.enter_context(nc.psum_tensor(name, shape, F32))

            dst_i = sb("dst_i", [NB, B], I32)
            next_i = sb("next_i", [NB, B], I32)
            src_i = sb("src_i", [NB, B], I32)
            dst_f = sb("dst_f", [NB, T, P])
            next_f = sb("next_f", [NB, T, P])
            src_f = sb("src_f", [NB, T, P])
            row_f = sb("row_f", [NB, T, P])
            eq = sb("eq", [NB, T, P])
            brk = sb("brk", [NB, T, P + 1])
            ends = sb("ends", [NB, T, 2])
            key_b = sb("key_b", [P, NI])
            go_on = sb("go_on", [1, NI])
            key_skip = sb("key_skip", [1, NI])
            key_skip_i = sb("key_skip_i", [1, NI], I32)
            W1_l = sb("W1_l", [D, D])
            W2_l = sb("W2_l", [D, D])
            bias = sb("bias", [1, 5, D])
            part_b = sb("part_b", [1, 4, 3, T, D], BF16)
            rest = sb("rest", [1, 4, D])
            turn = ps("turn", [P, 4, 512])

            s_mem, s_idx, s_w, s_wb = sem("tables_cleared"), sem("indices_in"), sem("weights_in"), sem("bias_parts_in")
            s_id0, s_id, s_ho = sem("ident_zero"), sem("ident_ready"), sem("head_of_steps")
            s_f, s_eq, s_brk = sem("indices_float"), sem("row_steps"), sem("breaks_ready")
            s_ends, s_keys, s_keyb, s_item = sem("ends_ready"), sem("keys_out"), sem("keys_in"), sem("item_steps")
            s_rowo, s_rowi, s_brko = sem("item_rows_out"), sem("item_rows_in"), sem("breaks_out")
            s_turn, s_col, s_bp, s_v = sem("turned"), sem("turned_read"), sem("bias_steps"), sem("small_steps")
            tail = NB - 1

            with nc.Block() as block:
                @block.sync
                def _(sp):
                    sp.wait_ge(s_mem, 3)
                    for tile_, dram, off in ((dst_i, dst, 0), (next_i, dst, 1), (src_i, src, 0)):
                        if tail:
                            sp.dma_start(tile_[0:tail, :], dram[off:off + tail * B].rearrange("(b e) -> b e", e=B))\
                              .then_inc(s_idx, 16)
                        sp.dma_start(tile_[tail:NB, 0:E_LAST - off],
                                     dram[off + tail * B:E].rearrange("(b e) -> b e", b=1)).then_inc(s_idx, 16)
                    sp.wait_ge(s_ends, 1)
                    sp.dma_start(keys.rearrange("a (b i) -> (a b) i", i=2 * T),
                                 ends[:].rearrange("b t e -> b (t e)")).then_inc(s_keys, 16)
                    sp.wait_ge(s_keys, 16)
                    sp.dma_start(key_b[:], keys.to_broadcast([P, NI])).then_inc(s_keyb, 16)
                    sp.wait_ge(s_brk, 1)
                    for h in range(H):
                        sp.dma_start(breaks[:, :, h, :], brk[:]).then_inc(s_brko, 16)
                    sp.wait_ge(s_item, 6)
                    sp.dma_start(key_rows, key_skip_i[:]).then_inc(s_rowo, 16)
                    sp.wait_ge(s_rowo, 16)
                    with nc.allow_non_contiguous_dma(reason="a few hundred indices, once"):
                        sp.dma_start(row_item[:], key_rows.rearrange("a (c p) -> p (a c)", p=PI)).then_inc(s_rowi, 16)
                    sp.wait_ge(s_bp, 6)
                    for n, t in enumerate((b2_3, bq_3, bskip_3, bf2_3)):
                        for r in range(3):
                            sp.dma_start(t[r:r + 1], part_b[0:1, n, r]).then_inc(s_wb, 16)
                    sp.wait_ge(s_wb, 12 * 16)
                    sp.wait_ge(s_rowi, 16)
                    sp.wait_ge(s_brko, H * 16)

                @block.scalar
                def _(act):
                    def col(v):
                        return v.rearrange("(d a) -> d a", a=1)

                    def row(v):
                        return v.rearrange("(a d) -> a d", a=1)

                    loads = [(W1_l[:], W1), (W2_l[:], W2), (Wq_s[:], Wq), (Wk_s[:], Wk), (Wv_s[:], Wv),
                             (Wskip_s[:], Wskip), (Wf1_s[:], Wf1), (Wf2_s[:], Wf2.rearrange("(t f) d -> f t d", t=T)),
                             (We_s[0:DE, 0, :], We), (We_s[0:DE, 1, :], We),
                             (We_s[DE:DE + 1, 0, :], row(bk)), (We_s[DE:DE + 1, 1, :], row(bv)),
                             (bias[:, 0, :], row(b2)), (bias[:, 1, :], row(bq)), (bias[:, 2, :], row(bskip)),
                             (bias[:, 3, :], row(bf2)), (bias[:, 4, :], row(b1)),
                             (g1_col[:], col(g1)), (b1_col[:], col(b1)), (gamma_col[:], col(gamma)),
                             (beta_col[:], col(beta)), (eps1[:], row(eps).to_broadcast([P, 1]))]
                    for t in range(T):
                        loads.append((bf1_col[:, t:t + 1], col(bf1[t * D:(t + 1) * D])))
                        loads.append((g1_row[:, t, :], row(g1).to_broadcast([P, D])))
                        loads.append((g2_row[:, t, :], row(g2).to_broadcast([P, D])))
                        loads.append((b2n_row[:, t, :], row(b2n).to_broadcast([P, D])))
                    with nc.allow_non_contiguous_dma(reason="vectors of 128, once"):
                        for to, frm in loads:
                            act.dma_start(to, frm).then_inc(s_w, 16)
                    act.wait_ge(s_w, 16 * 38)
                    act.wait_ge(s_mem, 4)
                    for z in range(N // ZC):
                        act.dma_start(agg.rearrange("n d -> (n d)")[z * P * ZC:(z + 1) * P * ZC]
                                      .rearrange("(p c) -> p c", p=P), zeros[:]).then_inc(s_zero, 16)

                @block.gpsimd
                def _(pool):
                    pool.memset(ident[:], 0.0).then_inc(s_id0, 1)
                    pool.memset(head_of[:], 1.0).then_inc(s_ho, 1)
                    pool.wait_ge(s_id0, 1)
                    pool.affine_select(out=ident[:], in_=ident[:], compare_op=ALU.not_equal, fill=1.0, base=0,
                                       pattern=[[-1, P]], channel_multiplier=1).then_inc(s_id, 1)
                    pool.wait_ge(s_ho, 1)
                    pool.affine_select(out=head_of[:], in_=head_of[:], compare_op=ALU.is_ge, fill=0.0, base=0,
                                       pattern=[[1, D]], channel_multiplier=-C).then_inc(s_ho, 1)
                    pool.wait_ge(s_ho, 2)
                    pool.affine_select(out=head_of[:], in_=head_of[:], compare_op=ALU.is_ge, fill=0.0, base=C - 1,
                                       pattern=[[-1, D]], channel_multiplier=C).then_inc(s_ho, 1)

                @block.vector
                def _(dve):
                    dve.memset(dst_i[:], PAD).then_inc(s_mem, 1)
                    dve.memset(next_i[:], PAD).then_inc(s_mem, 1)
                    dve.memset(src_i[:], 0).then_inc(s_mem, 1)
                    dve.memset(zeros[:], 0.0).then_inc(s_mem, 1)
                    dve.memset(onesB[:], 1.0)
                    dve.memset(half[:], -0.5)
                    dve.memset(mid[:], 0.5)
                    dve.memset(root_d[:], float(D) ** 0.5)
                    dve.memset(brk[:], LOW).then_inc(s_mem, 1)
                    dve.wait_ge(s_idx, (6 if tail else 3) * 16)
                    for to, frm in ((dst_f, dst_i), (next_f, next_i), (src_f, src_i)):
                        dve.tensor_copy(to[:].rearrange("b t e -> b (t e)"), frm[:]).then_inc(s_f, 1)
                    dve.wait_ge(s_f, 3)
                    dve.tensor_tensor(eq[:], dst_f[:], next_f[:], ALU.is_equal).then_inc(s_eq, 1)
                    dve.wait_ge(s_eq, 1)
                    dve.scalar_tensor_tensor(out=row_f[:], in0=eq[:], scalar=float(SKIP), in1=dst_f[:],
                                             op0=ALU.mult, op1=ALU.add).then_inc(s_eq, 1)
                    dve.wait_ge(s_eq, 2)
                    for n, e in enumerate((0, P - 1)):
                        dve.tensor_tensor(eq[:], dst_f[:], dst_f[:, :, e:e + 1].to_broadcast([NB, T, P]),
                                          ALU.is_equal).then_inc(s_eq, 1)
                        dve.wait_ge(s_eq, 3 + 2 * n)
                        dve.scalar_tensor_tensor(out=row_f[:], in0=eq[:], scalar=float(SKIP), in1=row_f[:],
                                                 op0=ALU.mult, op1=ALU.add).then_inc(s_eq, 1)
                        dve.wait_ge(s_eq, 4 + 2 * n)
                    dve.tensor_tensor(eq[:, :, 0:P - 1], dst_f[:, :, 1:P], dst_f[:, :, 0:P - 1],
                                      ALU.is_equal).then_inc(s_eq, 1)
                    dve.wait_ge(s_eq, 7)
                    dve.wait_ge(s_mem, 5)
                    dve.tensor_scalar(brk[:, :, 1:P], eq[:, :, 0:P - 1], -1.0, -LOW, ALU.add, ALU.mult)\
                       .then_inc(s_brk, 1)
                    dve.tensor_copy(ends[:], dst_f[:, :, 0:P:P - 1]).then_inc(s_ends, 1)
                    dve.wait_ge(s_keyb, 16)
                    dve.memset(same_item[:], 0.0).then_inc(s_item, 1)
                    dve.memset(count_item[:], 1.0).then_inc(s_item, 1)
                    dve.wait_ge(s_item, 1)
                    dve.tensor_tensor(same_item[:, 1:NI], key_b[:, 1:NI], key_b[:, 0:NI - 1], ALU.is_equal)\
                       .then_inc(s_item, 1)
                    dve.wait_ge(s_item, 3)
                    dve.tensor_scalar(count_item[:, 1:NI:2], same_item[:, 1:NI:2], -1.0, 1.0, ALU.mult, ALU.add)\
                       .then_inc(s_item, 1)
                    dve.tensor_copy(key_skip[0:1, NI - 1:NI], key_b[0:1, NI - 1:NI]).then_inc(s_v, 1)
                    dve.scalar_tensor_tensor(out=key_skip[0:1, 0:NI - 1], in0=same_item[0:1, 1:NI],
                                             scalar=float(SKIP), in1=key_b[0:1, 0:NI - 1],
                                             op0=ALU.mult, op1=ALU.add).then_inc(s_item, 1)
                    dve.wait_ge(s_item, 5)
                    dve.wait_ge(s_v, 1)
                    dve.tensor_copy(key_skip_i[:], key_skip[:]).then_inc(s_item, 1)
                    dve.wait_ge(s_w, 16 * 38)
                    dve.tensor_scalar(eps1[:], eps1[:], 1.0, None, ALU.add).then_inc(s_v, 1)
                    dve.tensor_tensor(bias[:, 3, :], bias[:, 3, :], bias[:, 4, :], ALU.add).then_inc(s_bp, 1)
                    dve.wait_ge(s_bp, 1)
                    left = bias[:, 0:4, :]
                    for r in range(3):
                        for t in range(T):
                            last = dve.tensor_copy(part_b[:, :, r, t, :], left)
                        last.then_inc(s_bp, 1)
                        if r < 2:
                            dve.wait_ge(s_bp, 2 + 2 * r)
                            dve.tensor_tensor(rest[:], left, part_b[:, :, r, 0, :], ALU.subtract).then_inc(s_bp, 1)
                            dve.wait_ge(s_bp, 3 + 2 * r)
                            left = rest[:]
                    dve.wait_ge(s_id, 1)
                    dve.tensor_tensor(Wskip_s[:], Wskip_s[:], ident[:], ALU.add).then_inc(s_v, 1)
                    for n in range(3):
                        dve.wait_ge(s_turn, n + 1)
                        for t in range(T):
                            last = dve.tensor_copy(idx_cols[:, :, (1, 0, 2)[n], t], turn[:, n, t * P:t * P + NB])
                            if n == 0:
                                last = dve.tensor_copy(dst_cols[:, :, t], turn[:, n, t * P:t * P + NB])
                        last.then_inc(s_col, 1)
                    dve.wait_ge(s_turn, 4)
                    dve.tensor_copy(W1T[:], turn[:, 3, 0:D])
                    dve.tensor_copy(W2T[:], turn[:, 3, D:2 * D]).then_inc(s_col, 1)

                @block.tensor
                def _(pe):
                    pe.wait_ge(s_id, 1)
                    pe.wait_ge(s_eq, 6)
                    for n, table in enumerate((dst_f, src_f, row_f)):
                        for t in range(T):
                            mm = pe.transpose(turn[:, n, t * P:t * P + NB], table[:, t, :], ident[0:NB, 0:NB])
                        mm.then_inc(s_turn, 1)
                    pe.wait_ge(s_w, 16 * 38)
                    pe.transpose(turn[:, 3, 0:D], W1_l[:], ident[:])
                    pe.transpose(turn[:, 3, D:2 * D], W2_l[:], ident[:]).then_inc(s_turn, 1)

        clear()
        edges0(nc, sem, NB, NI, x, agg, rows_side[0], ident, idx_cols, dst_cols, N, s_zero, 16 * (N // ZC))
        joins0(nc, sem, NI, CI, PI, rows_side[0], agg, ident, same_item, count_item, row_item, N)
        part_sems.clear()
        stats(nc, sem, NG, N, group, geometry, x, agg, eps1, half, W1T, gamma_col, beta_col, bn_scale, bn_shift,
              ident)
        clear()
        nodes0(nc, sem, NG, group, geometry, x, agg, x1, eps1, half, mid, root_d, ident, W1T, W2T,
               bn_scale, bn_shift, onesB, b2_3)
        clear()
        edges1(nc, sem, NB, E_LAST, N, x1, agg, edge_attr, rows_side[1], soft_side, breaks, ident, idx_cols, dst_cols,
               Wq_s, Wk_s, Wv_s, We_s, onesB, bq_3)
        joins1(nc, sem, NI, CI, PI, rows_side[1], soft_side, agg, ident, same_item, count_item, row_item, head_of, N)
        nodes1(nc, sem, NG, group, geometry, x1, agg, out, half, mid, root_d, ident, Wskip_s, Wf1_s, Wf2_s, onesB,
               bskip_3, bf2_3,
               g1_col, b1_col, bf1_col, g1_row, g2_row, b2n_row)


def scatter_rows(pool, dram, index, rows, last_row):
    return pool.indirect_dma_start(dram, bass.IndirectOffsetOnAxis(index, 0), rows, None,
                                   bounds_check=last_row, oob_is_err=False)


def gather_rows(pool, rows, dram, index, last_row):
    return pool.indirect_dma_start(rows, None, dram, bass.IndirectOffsetOnAxis(index, 0), bounds_check=last_row)


def prepare_batch(dve, i, u, idx, dst_f, idx_cols, dst_cols, idx_ready, dstf_ready):
    dve.tensor_copy(idx[:, u], idx_cols[:, bass.ds(i, 1)].rearrange("p b k t -> p (b k) t")).then_inc(idx_ready, 1)
    dve.tensor_copy(dst_f[:, u], dst_cols[:, bass.ds(i, 1)].rearrange("p b t -> p (b t)")).then_inc(dstf_ready, 1)


def side_rows(side, i, end):
    view = side.rearrange("(b t e) d -> b t e d", t=T, e=2)
    return view[bass.ds(i, 1), :, end, :]


def edges0(nc, sem, NB, NI, x, agg, side, ident, idx_cols, dst_cols, N, zeroed, zeroed_value):
    with ExitStack() as part:
        def sb(name, shape, dt=F32):
            return part.enter_context(nc.sbuf_tensor(name, shape, dt))

        idx = sb("e0_idx", [P, U, 3, T], I32)
        dst_f = sb("e0_dst_f", [P, U, T])
        rows = sb("e0_rows", [P, S, T, D])
        same = sb("e0_same", [P, S, T, P])
        sums = sb("e0_sums", [P, S, T, D])
        spread = part.enter_context(nc.psum_tensor("e0_spread", [P, 2, T, P], F32))
        total = part.enter_context(nc.psum_tensor("e0_total", [P, 2, T, D], F32))

        idx_ready, dstf_ready = sem("e0_idx_ready"), sem("e0_dstf_ready")
        spread_ready, same_ready = sem("e0_spread_ready"), sem("e0_same_ready")
        total_ready, sums_ready = sem("e0_total_ready"), sem("e0_sums_ready")
        begun = sem("e0_begun")
        gathered = [sem(f"e0_gathered{s}") for s in range(S)]
        scattered = [sem(f"e0_scattered{s}") for s in range(S)]
        sided = [sem(f"e0_sided{s}") for s in range(S)]

        with nc.Block() as block:
            @block.vector
            def _(dve):
                dve.memset(dst_f[:], 0.0).then_inc(begun, 1)
                dve.wait_ge(begun, 1)

                def body(j, u):
                    i = j * U + u
                    if works(i, NB):
                        if late(j):
                            r, s = turn_of(j, u)
                            dve.wait_ge(scattered[s], (r - 1) * T * 16)
                        prepare_batch(dve, i, u, idx, dst_f, idx_cols, dst_cols, idx_ready, dstf_ready)
                    jb, ub, ib = back(j, u, 1)
                    if works(ib, NB):
                        dve.wait_ge(spread_ready, ib + 1)
                        dve.wait_ge(dstf_ready, ib + 1)
                        r, s = turn_of(jb, ub)
                        if late(r):
                            dve.wait_ge(total_ready, ib - S + 1)
                        dve.tensor_tensor(same[:, s], spread[:, ub % 2],
                                          dst_f[:, ub].unsqueeze(2).to_broadcast([P, T, P]),
                                          ALU.is_equal).then_inc(same_ready, 1)

                walk(dve, NB, 1, body)

            @block.tensor
            def _(pe):
                def body(j, u):
                    i = j * U + u
                    if works(i, NB):
                        pe.wait_ge(dstf_ready, i + 1)
                        if not isinstance(i, int) or i >= 2:
                            pe.wait_ge(same_ready, i - 1)
                        for t in range(T):
                            mm = pe.transpose(spread[:, u % 2, t, :], dst_f[:, u, t:t + 1].to_broadcast([P, P]),
                                              ident[:])
                        mm.then_inc(spread_ready, 1)
                    jb, ub, ib = back(j, u, 2)
                    if works(ib, NB):
                        pe.wait_ge(same_ready, ib + 1)
                        r, s = turn_of(jb, ub)
                        pe.wait_ge(gathered[s], (r + 1) * T * 16)
                        if not isinstance(ib, int) or ib >= 2:
                            pe.wait_ge(sums_ready, ib - 1)
                        for t in range(T):
                            mm = pe.matmul(total[:, ub % 2, t, :], same[:, s, t, :], rows[:, s, t, :],
                                           start=True, stop=True)
                        mm.then_inc(total_ready, 1)

                walk(pe, NB, 2, body)

            @block.scalar
            def _(act):
                def body(j, u):
                    i = j * U + u
                    act.wait_ge(total_ready, i + 1)
                    r, s = turn_of(j, u)
                    if late(r):
                        act.wait_ge(scattered[s], r * T * 16)
                        act.wait_ge(sided[s], r * 32)
                    act.activation(sums[:, s], total[:, u % 2], ACT.Copy).then_inc(sums_ready, 1)

                walk(act, NB, 0, body)

            @block.gpsimd
            def _(pool):
                last_row = pool.to_reg(N - 1)

                def body(j, u):
                    i = j * U + u
                    if works(i, NB):
                        now, free = ready_values(pool, i + 1, i - S + 1)
                        r, s = turn_of(j, u)
                        pool.wait_ge(begun, 1)
                        pool.wait_ge(idx_ready, now)
                        if late(r):
                            pool.wait_ge(total_ready, free)
                        for t in range(T):
                            gather_rows(pool, rows[:, s, t, :], x, idx[:, u, 0, t:t + 1].bitcast(U32), last_row)\
                                .then_inc(gathered[s], 16)
                    jb, ub, ib = back(j, u, 3)
                    if works(ib, NB):
                        (now,) = ready_values(pool, ib + 1)
                        pool.wait_ge(begun, 1)
                        pool.wait_ge(sums_ready, now)
                        s = ub % S
                        if isinstance(ib, int) and ib == 0:
                            pool.wait_ge(zeroed, zeroed_value)
                        for t in range(T):
                            scatter_rows(pool, agg, idx[:, ub, 2, t:t + 1].bitcast(U32), sums[:, s, t, :], last_row)\
                                .then_inc(scattered[s], 16)

                walk(pool, NB, 3, body)
                for s in range(S):
                    pool.wait_ge(scattered[s], len(range(s, NB, S)) * T * 16)

            @block.sync
            def _(sp):
                def body(j, u):
                    i = j * U + u
                    sp.wait_ge(sums_ready, i + 1)
                    for end, p in enumerate((0, P - 1)):
                        sp.dma_start(side_rows(side, i, end), sums[p:p + 1, u % S]).then_inc(sided[u % S], 16)

                walk(sp, NB, 0, body)
                for s in range(S):
                    sp.wait_ge(sided[s], len(range(s, NB, S)) * 32)


def joins0(nc, sem, NI, CI, PI, side, agg, ident, same_item, count_item, row_item, N):
    with ExitStack() as part:
        items = part.enter_context(nc.sbuf_tensor("j0_items", [PI, CI, D], F32))
        flat = part.enter_context(nc.sbuf_tensor("j0_flat", [D, NI], F32))
        run = part.enter_context(nc.sbuf_tensor("j0_run", [D, NI], F32))
        turn = part.enter_context(nc.psum_tensor("j0_turn", [P, CI, P], F32))
        s_in, s_turn, s_flat = sem("j0_in"), sem("j0_turned"), sem("j0_flat_steps")
        s_back, s_rows, s_out = sem("j0_turned_back"), sem("j0_rows"), sem("j0_out")

        with nc.Block() as block:
            @block.sync
            def _(sp):
                sp.dma_start(items[:], side.rearrange("(c p) d -> p c d", p=PI)).then_inc(s_in, 16)

            @block.tensor
            def _(pe):
                pe.wait_ge(s_in, 16)
                for c in range(CI):
                    mm = pe.transpose(turn[:, c, 0:PI], items[:, c, :], ident[0:PI, 0:PI])
                mm.then_inc(s_turn, 1)
                pe.wait_ge(s_flat, 2)
                for c in range(CI):
                    mm = pe.transpose(turn[0:PI, c, :], run[:, c * PI:(c + 1) * PI], ident[:])
                mm.then_inc(s_back, 1)

            @block.vector
            def _(dve):
                dve.wait_ge(s_turn, 1)
                dve.tensor_tensor(flat[:].rearrange("d (c p) -> d c p", p=PI), turn[:, :, 0:PI],
                                  count_item[:].rearrange("d (c p) -> d c p", p=PI), ALU.mult).then_inc(s_flat, 1)
                dve.wait_ge(s_flat, 1)
                dve.tensor_tensor_scan(run[:], same_item[:], flat[:], 0.0, ALU.mult, ALU.add).then_inc(s_flat, 1)
                dve.wait_ge(s_back, 1)
                dve.tensor_copy(items[:], turn[0:PI]).then_inc(s_rows, 1)

            @block.gpsimd
            def _(pool):
                pool.wait_ge(s_rows, 1)
                for c in range(CI):
                    scatter_rows(pool, agg, row_item[:, c:c + 1].bitcast(U32), items[:, c, :], N - 1)\
                        .then_inc(s_out, 16)
                pool.wait_ge(s_out, CI * 16)


def stats(nc, sem, NG, N, group, geometry, x, agg, eps1, half, W1T, gamma_col, beta_col, bn_scale, bn_shift,
          ident):
    with ExitStack() as part:
        def sb(name, shape, dt=F32):
            return part.enter_context(nc.sbuf_tensor(name, shape, dt))

        xs = sb("st_x", [P, U, T, D])
        ags = sb("st_agg", [P, U, T, D])
        h = sb("st_h", [P, U, T, D + 1])
        gram = sb("st_gram", [D, D + 1])
        mean = sb("st_mean", [D, 1])
        mean_row = sb("st_mean_row", [1, D])
        cov = sb("st_cov", [D, D])
        prod = sb("st_prod", [D, D])
        ones = sb("st_ones", [P, 1])
        small = sb("st_small", [D, 4])
        G = part.enter_context(nc.psum_tensor("st_G", [D, 512], F32))
        M = part.enter_context(nc.psum_tensor("st_M", [D, 4, 512], F32))
        M_row = part.enter_context(nc.psum_tensor("st_row", [1, 512], F32))

        rows_in = [sem(f"st_rows_in{u}") for u in range(U)]
        h_ready, h_used, ones_set = sem("st_h_ready"), sem("st_h_used"), sem("st_ones_set")
        fin_d, fin_p, fin_g = sem("st_vector_steps"), sem("st_product_steps"), sem("st_pool_steps")

        with nc.Block() as block:
            @block.sync
            def _(sp):
                def body(j, u):
                    g = j * U + u
                    p, t = geometry(g)
                    if late(j):
                        sp.wait_ge(h_ready, g - U + 1)
                    sp.dma_start(xs[0:p, u, 0:t], group(x, g)).then_inc(rows_in[u], 16)
                    sp.dma_start(ags[0:p, u, 0:t], group(agg, g)).then_inc(rows_in[u], 16)

                walk(sp, NG, 0, body)

            @block.vector
            def _(dve):
                dve.memset(ones[:], 1.0).then_inc(ones_set, 1)
                dve.memset(h[:], 1.0).then_inc(ones_set, 1)
                dve.wait_ge(ones_set, 2)

                def body(j, u):
                    g = j * U + u
                    p, t = geometry(g)
                    dve.wait_ge(rows_in[u], (j + 1) * 32)
                    if late(j):
                        dve.wait_ge(h_used, g - U + 1)
                    dve.scalar_tensor_tensor(out=h[0:p, u, 0:t, 0:D], in0=xs[0:p, u, 0:t], scalar=eps1[0:p],
                                             in1=ags[0:p, u, 0:t], op0=ALU.mult, op1=ALU.add).then_inc(h_ready, 1)

                walk(dve, NG, 0, body)
                dve.wait_ge(h_used, NG)
                dve.tensor_scalar(gram[:], G[:, 0:D + 1], 1.0 / N, None, ALU.mult).then_inc(fin_d, 1)
                dve.wait_ge(fin_p, 1)
                dve.tensor_copy(mean_row[:], M_row[0:1, 0:D]).then_inc(fin_d, 1)
                dve.wait_ge(fin_p, 2)
                dve.tensor_tensor(cov[:], gram[:, 0:D], M[:, 0, 0:D], ALU.subtract).then_inc(fin_d, 1)
                dve.wait_ge(fin_p, 3)
                dve.tensor_tensor(prod[:], M[:, 1, 0:D], W1T[:], ALU.mult).then_inc(fin_d, 1)
                dve.wait_ge(fin_p, 5)
                dve.tensor_scalar(small[:, 0:1], M[:, 2, 0:1], 0.0, BN_EPS, ALU.max, ALU.add).then_inc(fin_d, 1)
                dve.wait_ge(fin_g, 1)
                dve.tensor_tensor(bn_scale[:], small[:, 1:2], gamma_col[:], ALU.mult).then_inc(fin_d, 1)
                dve.wait_ge(fin_d, 6)
                dve.tensor_tensor(small[:, 2:3], M[:, 3, 0:1], bn_scale[:], ALU.mult).then_inc(fin_d, 1)
                dve.wait_ge(fin_d, 7)
                dve.tensor_tensor(bn_shift[:], beta_col[:], small[:, 2:3], ALU.subtract).then_inc(fin_d, 1)

            @block.gpsimd
            def _(pool):
                pool.wait_ge(fin_d, 5)
                pool.tensor_tensor(small[:, 1:2], small[:, 0:1], half[:, 0:1], ALU.pow).then_inc(fin_g, 1)

            @block.tensor
            def _(pe):
                def body(j, u):
                    g = j * U + u
                    p, t = geometry(g)
                    pe.wait_ge(h_ready, g + 1)
                    for c in range(t):
                        first = isinstance(g, int) and g == 0 and c == 0
                        last = isinstance(g, int) and g == NG - 1 and c == t - 1
                        mm = pe.matmul(G[:, 0:D + 1], h[0:p, u, c, 0:D], h[0:p, u, c, :], start=first, stop=last)
                    mm.then_inc(h_used, 1)

                walk(pe, NG, 0, body)
                pe.wait_ge(fin_d, 1)
                pe.transpose(M_row[0:1, 0:D], gram[:, D:D + 1], ident[:]).then_inc(fin_p, 1)
                pe.wait_ge(fin_d, 2)
                pe.matmul(M[:, 0, 0:D], mean_row[:], mean_row[:], start=True, stop=True).then_inc(fin_p, 1)
                pe.wait_ge(fin_d, 3)
                pe.matmul(M[:, 1, 0:D], cov[:], W1T[:], start=True, stop=True).then_inc(fin_p, 1)
                pe.matmul(M[:, 3, 0:1], W1T[:], gram[:, D:D + 1], start=True, stop=True).then_inc(fin_p, 1)
                pe.wait_ge(fin_d, 4)
                pe.matmul(M[:, 2, 0:1], prod[:], ones[:], start=True, stop=True).then_inc(fin_p, 1)


class Norm:

    def __init__(self, part, nc, sem, name):
        def sb(what, last):
            return part.enter_context(nc.sbuf_tensor(f"{name}_{what}", [P, U, T] + last, F32))

        self.stat, self.both = sb("stat", [6]), sb("both", [2])
        self.gap, self.gap2, self.spread = sb("gap", []), sb("gap2", []), sb("spread", [])
        self.root, self.mean, self.rstd = sb("root", []), sb("mean", []), sb("rstd", [])
        self.shift = sb("shift", [])
        self.stat_ready, self.both_ready = sem(f"{name}_stat_ready"), sem(f"{name}_both_ready")
        self.gap_ready, self.spread_ready = sem(f"{name}_gap_ready"), sem(f"{name}_spread_ready")
        self.root_ready, self.rstd_ready = sem(f"{name}_root_ready"), sem(f"{name}_rstd_ready")
        self.mean_ready, self.shift_ready = sem(f"{name}_mean_ready"), sem(f"{name}_shift_ready")


def norm_stats(dve, n, y, p, t, u, g, y_ready):
    dve.wait_ge(y_ready, g + 1)
    for c in range(t):
        last = dve.bn_stats(n.stat[0:p, u, c, :], y[0:p, c, :])
    last.then_inc(n.stat_ready, 1)
    s = n.stat[0:p, u, 0:t]
    dve.wait_ge(n.stat_ready, g + 1)
    dve.tensor_tensor(n.gap[0:p, u, 0:t], s[:, :, 1], s[:, :, 4], ALU.subtract).then_inc(n.gap_ready, 1)
    dve.tensor_tensor(n.both[0:p, u, 0:t], s[:, :, 1:3], s[:, :, 4:6], ALU.add).then_inc(n.both_ready, 1)
    dve.wait_ge(n.gap_ready, 2 * g + 1)
    dve.scalar_tensor_tensor(out=n.gap2[0:p, u, 0:t], in0=n.gap[0:p, u, 0:t], scalar=D / 4.0,
                             in1=n.gap[0:p, u, 0:t], op0=ALU.mult, op1=ALU.mult).then_inc(n.gap_ready, 1)
    dve.wait_ge(n.gap_ready, 2 * g + 2)
    dve.scalar_tensor_tensor(out=n.spread[0:p, u, 0:t], in0=n.both[0:p, u, 0:t, 1], scalar=D * LN_EPS,
                             in1=n.gap2[0:p, u, 0:t], op0=ALU.add, op1=ALU.add).then_inc(n.spread_ready, 1)


def norm_root(pool, n, p, t, u, g, half, mid, root_d, shift=False):
    pool.wait_ge(n.both_ready, g + 1)
    pool.tensor_tensor(n.mean[0:p, u, 0:t], n.both[0:p, u, 0:t, 0], (half if shift else mid)[0:p, 0:t], ALU.mult)\
        .then_inc(n.mean_ready, 1)
    pool.wait_ge(n.spread_ready, g + 1)
    pool.tensor_tensor(n.root[0:p, u, 0:t], n.spread[0:p, u, 0:t], half[0:p, 0:t], ALU.pow)\
        .then_inc(n.root_ready, 1)
    pool.wait_ge(n.root_ready, g + 1)
    pool.tensor_tensor(n.rstd[0:p, u, 0:t], n.root[0:p, u, 0:t], root_d[0:p, 0:t], ALU.mult)\
        .then_inc(n.rstd_ready, 1)
    if shift:
        pool.wait_ge(n.rstd_ready, g + 1)
        pool.wait_ge(n.mean_ready, g + 1)
        pool.tensor_tensor(n.shift[0:p, u, 0:t], n.mean[0:p, u, 0:t], n.rstd[0:p, u, 0:t], ALU.mult)\
            .then_inc(n.shift_ready, 1)


def norm_apply(dve, n, to, y, p, t, u, g, ready):
    dve.wait_ge(n.rstd_ready, g + 1)
    for c in range(t):
        last = dve.tensor_scalar(to[0:p, c, :], y[0:p, c, :], n.mean[0:p, u, c:c + 1],
                                 n.rstd[0:p, u, c:c + 1], ALU.subtract, ALU.mult)
    last.then_inc(ready, 1)


def norm_apply_act(act, n, to, y, p, t, u, g, ready):
    act.wait_ge(n.shift_ready, g + 1)
    for c in range(t):
        last = act.activation(to[0:p, c, :], y[0:p, c, :], ACT.Identity, bias=n.shift[0:p, u, c:c + 1],
                              scale=n.rstd[0:p, u, c:c + 1])
    last.then_inc(ready, 1)


def nodes0(nc, sem, NG, group, geometry, x, agg, x1, eps1, half, mid, root_d, ident, W1T, W2T, bn_scale, bn_shift,
           onesB, b2_3):
    with ExitStack() as part:
        def sb(name, shape, dt=F32):
            return part.enter_context(nc.sbuf_tensor(name, shape, dt))

        def ps(name):
            return part.enter_context(nc.psum_tensor(name, [P, 2, T * P], F32))

        xs = sb("n0_x", [P, U, T, D])
        ags = sb("n0_agg", [P, U, T, D])
        h = sb("n0_h", [P, S, T, D])
        hT = sb("n0_hT", [D, S, T * P])
        rT = sb("n0_rT", [D, S, T * P])
        y = sb("n0_y", [P, S, T, D])
        o = sb("n0_o", [P, S, T, D])
        turned, lin1, lin2 = ps("n0_turned"), ps("n0_lin1"), ps("n0_lin2")
        n1 = Norm(part, nc, sem, "n0_norm")

        rows_in = [sem(f"n0_rows_in{u}") for u in range(U)]
        x1_out = [sem(f"n0_x1_out{s}") for s in range(S)]
        h_ready, turned_ready, hT_ready = sem("n0_h_ready"), sem("n0_turned_ready"), sem("n0_hT_ready")
        lin1_ready, rT_ready, lin2_ready = sem("n0_lin1_ready"), sem("n0_rT_ready"), sem("n0_lin2_ready")
        y_ready, o_ready = sem("n0_y_ready"), sem("n0_o_ready")

        with nc.Block() as block:
            @block.sync
            def _(sp):
                def body(j, u):
                    g = j * U + u
                    if works(g, NG):
                        p, t = geometry(g)
                        if late(j):
                            sp.wait_ge(y_ready, g - U + 1)
                        sp.dma_start(xs[0:p, u, 0:t], group(x, g)).then_inc(rows_in[u], 16)
                        sp.dma_start(ags[0:p, u, 0:t], group(agg, g)).then_inc(rows_in[u], 16)

                walk(sp, NG, 0, body)

            @block.vector
            def _(dve):
                def body(j, u):
                    g = j * U + u
                    if works(g, NG):
                        p, t = geometry(g)
                        r, s = turn_of(j, u)
                        dve.wait_ge(rows_in[u], (j + 1) * 32)
                        if late(r):
                            dve.wait_ge(turned_ready, g - S + 1)
                        dve.scalar_tensor_tensor(out=h[0:p, s, 0:t], in0=xs[0:p, u, 0:t], scalar=eps1[0:p],
                                                 in1=ags[0:p, u, 0:t], op0=ALU.mult, op1=ALU.add)\
                           .then_inc(h_ready, 1)
                    jb, ub, gb = back(j, u, 3)
                    if works(gb, NG):
                        p, t = geometry(gb)
                        r, s = turn_of(jb, ub)
                        dve.wait_ge(lin2_ready, gb + 1)
                        if late(r):
                            dve.wait_ge(o_ready, gb - S + 1)
                        dve.tensor_tensor(y[0:p, s, 0:t], lin2[0:p, ub % 2, 0:t * D].rearrange(
                            "p (t d) -> p t d", d=D), xs[0:p, ub, 0:t], ALU.add).then_inc(y_ready, 1)
                        norm_stats(dve, n1, y[:, s], p, t, ub, gb, y_ready)

                walk(dve, NG, 3, body)

            @block.gpsimd
            def _(pool):
                def body(j, u):
                    g = j * U + u
                    p, t = geometry(g)
                    norm_root(pool, n1, p, t, u, g, half, mid, root_d, shift=True)

                walk(pool, NG, 0, body)

            @block.scalar
            def _(act):
                def body(j, u):
                    g = j * U + u
                    if works(g, NG):
                        p, t = geometry(g)
                        act.wait_ge(turned_ready, g + 1)
                        r, s = turn_of(j, u)
                        if late(r):
                            act.wait_ge(lin1_ready, g - S + 1)
                        act.activation(hT[:, s, 0:t * p], turned[:, u % 2, 0:t * p], ACT.Copy)\
                           .then_inc(hT_ready, 1)
                    jb, ub, gb = back(j, u, 1)
                    if works(gb, NG):
                        p, t = geometry(gb)
                        act.wait_ge(lin1_ready, gb + 1)
                        r, s = turn_of(jb, ub)
                        if late(r):
                            act.wait_ge(lin2_ready, gb - S + 1)
                        act.activation(rT[:, s, 0:t * p], lin1[:, ub % 2, 0:t * p], ACT.Relu,
                                       bias=bn_shift[:], scale=bn_scale[:]).then_inc(rT_ready, 1)

                    jb, ub, gb = back(j, u, 4)
                    if works(gb, NG):
                        p, t = geometry(gb)
                        r, s = turn_of(jb, ub)
                        if late(r):
                            act.wait_ge(x1_out[s], r * 16)
                        norm_apply_act(act, n1, o[:, s], y[:, s], p, t, ub, gb, o_ready)
                    jb, ub, gb = back(j, u, 5)
                    if works(gb, NG):
                        p, t = geometry(gb)
                        act.wait_ge(o_ready, gb + 1)
                        act.dma_start(group(x1, gb), o[0:p, ub % S, 0:t]).then_inc(x1_out[ub % S], 16)

                walk(act, NG, 5, body)
                for s in range(S):
                    act.wait_ge(x1_out[s], len(range(s, NG, S)) * 16)

            @block.tensor
            def _(pe):
                def body(j, u):
                    g = j * U + u
                    if works(g, NG):
                        p, t = geometry(g)
                        pe.wait_ge(h_ready, g + 1)
                        if not isinstance(g, int) or g >= 2:
                            pe.wait_ge(hT_ready, g - 1)
                        for c in range(t):
                            mm = pe.transpose(turned[:, u % 2, c * p:(c + 1) * p], h[0:p, u % S, c, :], ident[0:p, 0:p])
                        mm.then_inc(turned_ready, 1)
                    jb, ub, gb = back(j, u, 1)
                    if works(gb, NG):
                        p, t = geometry(gb)
                        pe.wait_ge(hT_ready, gb + 1)
                        if not isinstance(gb, int) or gb >= 2:
                            pe.wait_ge(rT_ready, gb - 1)
                        pe.matmul(lin1[:, ub % 2, 0:t * p], W1T[:], hT[:, ub % S, 0:t * p],
                                  start=True, stop=True).then_inc(lin1_ready, 1)
                    jb, ub, gb = back(j, u, 2)
                    if works(gb, NG):
                        p, t = geometry(gb)
                        pe.wait_ge(rT_ready, gb + 1)
                        if not isinstance(gb, int) or gb >= 2:
                            pe.wait_ge(y_ready, gb - 1)
                        add_bias(pe, lin2[0:p, ub % 2, 0:t * D], onesB, b2_3, p, t)
                        for c in range(t):
                            mm = pe.matmul(lin2[0:p, ub % 2, c * D:(c + 1) * D],
                                           rT[:, ub % S, c * p:(c + 1) * p], W2T[:], start=False, stop=(c == t - 1))
                        mm.then_inc(lin2_ready, 1)

                walk(pe, NG, 2, body)


def add_bias(pe, to, onesB, bias_3, p, t):
    pe.matmul(to, onesB[:, 0:p], bias_3[:, 0:t].rearrange("r t d -> r (t d)"), start=True, stop=False)


def edges1(nc, sem, NB, E_LAST, N, x1, agg, edge_attr, side, soft_side, breaks, ident, idx_cols, dst_cols,
           Wq_s, Wk_s, Wv_s, We_s, onesB, bq_3):
    TH = T * H
    with ExitStack() as part:
        def sb(name, shape, dt=F32):
            return part.enter_context(nc.sbuf_tensor(name, shape, dt))

        def ps(name, shape):
            return part.enter_context(nc.psum_tensor(name, shape, F32))

        idx = sb("e1_idx", [P, U, 3, T], I32)
        dst_f = sb("e1_dst_f", [P, U, T])
        xs = sb("e1_xs", [P, S, T, D])
        xd = sb("e1_xd", [P, S, T, D])
        ea = sb("e1_ea", [P, S, T, DE + 1])
        brk = sb("e1_brk", [TH, S, P + 1])
        xsT = sb("e1_xsT", [D, 2, T, P])
        xdT = sb("e1_xdT", [D, 2, T, P])
        eaT = sb("e1_eaT", [DE + 1, 2, T, P])
        q = sb("e1_q", [P, T * D])
        qk = sb("e1_qk", [P, T * D])
        logit = sb("e1_logit", [P, TH])
        run = sb("e1_run", [TH, P])
        top = sb("e1_top", [TH, P])
        diff = sb("e1_diff", [P, TH])
        ex = sb("e1_ex", [P, TH])
        exv = sb("e1_exv", [P, T, D])
        same = sb("e1_same", [P, T, P])
        rden = sb("e1_rden", [P, TH])
        att = sb("e1_att", [P, S, T, D])
        soft = sb("e1_soft", [P, S, T, 2 * H])
        xsT_p, xdT_p, eaT_p = ps("e1_xsT_p", [D, T, P]), ps("e1_xdT_p", [D, T, P]), ps("e1_eaT_p", [DE + 1, T, P])
        k_p, v_p, q_p = ps("e1_k_p", [P, T * D]), ps("e1_v_p", [P, T * D]), ps("e1_q_p", [P, T * D])
        wide = ps("e1_wide", [P, T, P])
        misc = ps("e1_misc", [P, 512])
        logitT_p = misc[0:TH, 0:P]
        top_p = misc[:, P:P + TH]
        den_p = misc[:, 2 * P:2 * P + TH]

        idx_ready, dstf_ready = sem("e1_idx_ready"), sem("e1_dstf_ready")
        rows_in = [sem(f"e1_rows_in{s}") for s in range(S)]
        ea_in = [sem(f"e1_ea_in{s}") for s in range(S)]
        brk_in = [sem(f"e1_brk_in{s}") for s in range(S)]
        scattered = [sem(f"e1_scattered{s}") for s in range(S)]
        sided = [sem(f"e1_sided{s}") for s in range(S)]
        begun = sem("e1_begun")
        ea_set, turned_ready, xT_ready = sem("e1_ea_set"), sem("e1_turned_ready"), sem("e1_xT_ready")
        kq_ready, v_ready, q_ready, qk_ready, logit_ready = sem("e1_kq_ready"), sem("e1_v_ready"), sem("e1_q_ready"), sem("e1_qk_ready"), sem("e1_logit_ready")
        logitT_ready, run_ready, top_ready = sem("e1_logitT_ready"), sem("e1_run_ready"), sem("e1_top_ready")
        topT_ready, diff_ready, ex_ready = sem("e1_topT_ready"), sem("e1_diff_ready"), sem("e1_ex_ready")
        top_kept, spread_ready, same_ready = sem("e1_top_kept"), sem("e1_spread_ready"), sem("e1_same_ready")
        exv_ready, sums_ready, rden_ready, att_ready = sem("e1_exv_ready"), sem("e1_sums_ready"), sem("e1_rden_ready"), sem("e1_att_ready")
        den_kept = sem("e1_den_kept")

        with nc.Block() as block:
            @block.gpsimd
            def _(pool):
                last_row = pool.to_reg(N - 1)
                pool.wait_ge(begun, 1)

                def body(j, u):
                    i = j * U + u
                    if works(i, NB):
                        now, free = ready_values(pool, i + 1, i - S + 1)
                        r, s = turn_of(j, u)
                        pool.wait_ge(begun, 1)
                        pool.wait_ge(idx_ready, now)
                        if late(r):
                            pool.wait_ge(turned_ready, free)
                        for t in range(T):
                            gather_rows(pool, xs[:, s, t, :], x1, idx[:, u, 0, t:t + 1].bitcast(U32), last_row)\
                                .then_inc(rows_in[s], 16)
                            gather_dst(pool, xd[:, s, t, :], x1, idx[:, u, 1, t:t + 1].bitcast(U32), last_row)\
                                .then_inc(rows_in[s], 16)
                    jb, ub, ib = back(j, u, AHEAD + 3)
                    if works(ib, NB):
                        (now,) = ready_values(pool, ib + 1)
                        pool.wait_ge(begun, 1)
                        pool.wait_ge(att_ready, now)
                        s = ub % S
                        for t in range(T):
                            scatter_rows(pool, agg, idx[:, ub, 2, t:t + 1].bitcast(U32), att[:, s, t, :], last_row)\
                                .then_inc(scattered[s], 16)

                walk(pool, NB, AHEAD + 3, body)
                for s in range(S):
                    pool.wait_ge(scattered[s], len(range(s, NB, S)) * T * 16)

            @block.sync
            def _(sp):
                sp.wait_ge(ea_set, 1)

                def body(j, u):
                    i = j * U + u
                    if works(i, NB):
                        r, s = turn_of(j, u)
                        if late(r):
                            sp.wait_ge(turned_ready, i - S + 1)
                        if isinstance(i, int) and i == NB - 1:
                            full, rest = E_LAST // P, E_LAST % P
                            if full:
                                sp.dma_start(ea[:, s, 0:full, 0:DE],
                                             edge_attr[i * B:i * B + full * P].rearrange("(t p) d -> p t d", p=P))\
                                  .then_inc(ea_in[s], 16)
                            if rest:
                                sp.dma_start(ea[0:rest, s, full, 0:DE],
                                             edge_attr[i * B + full * P:i * B + E_LAST]).then_inc(ea_in[s], 16)
                        else:
                            sp.dma_start(ea[:, s, :, 0:DE],
                                         edge_attr[bass.ds(i * B, B)].rearrange("(t p) d -> p t d", p=P))\
                              .then_inc(ea_in[s], 16)
                    jb, ub, ib = back(j, u, AHEAD)
                    if works(ib, NB):
                        r, s = turn_of(jb, ub)
                        if late(r):
                            sp.wait_ge(top_ready, ib - S + 1)
                        sp.dma_start(brk[:, s], breaks[bass.ds(ib, 1)].rearrange("b t h e -> (b t h) e"))\
                          .then_inc(brk_in[s], 16)
                    jb, ub, ib = back(j, u, AHEAD + 3)
                    if works(ib, NB):
                        s = ub % S
                        sp.wait_ge(att_ready, ib + 1)
                        sp.wait_ge(den_kept, ib + 1)
                        sp.wait_ge(top_kept, ib + 1)
                        for end, p in enumerate((0, P - 1)):
                            sp.dma_start(side_rows(side, ib, end), att[p:p + 1, s]).then_inc(sided[s], 16)
                            sp.dma_start(side_rows(soft_side, ib, end), soft[p:p + 1, s]).then_inc(sided[s], 16)

                walk(sp, NB, AHEAD + 3, body)
                for s in range(S):
                    sp.wait_ge(sided[s], len(range(s, NB, S)) * 64)

            @block.scalar
            def _(act):
                def body(j, u):
                    j, u, i = back(j, u, AHEAD)
                    jb, ub, ib = back(j, u, 1)
                    if works(ib, NB):
                        act.wait_ge(kq_ready, ib + 1)
                        if not isinstance(ib, int) or ib >= 1:
                            act.wait_ge(qk_ready, ib)
                        act.activation(q[:], q_p[:], ACT.Copy).then_inc(q_ready, 1)
                    jb, ub, ib = back(j, u, 2)
                    if works(ib, NB):
                        act.wait_ge(diff_ready, ib + 1)
                        if not isinstance(ib, int) or ib >= 1:
                            act.wait_ge(sums_ready, ib)
                        act.activation(ex[:], diff[:], ACT.Exp, scale=float(C) ** -0.5).then_inc(ex_ready, 1)
                    if works(i, NB):
                        act.wait_ge(turned_ready, i + 1)
                        if not isinstance(i, int) or i >= 2:
                            act.wait_ge(v_ready, i - 1)
                        act.activation(xsT[:, u % 2], xsT_p[:], ACT.Copy)
                        act.activation(xdT[:, u % 2], xdT_p[:], ACT.Copy)
                        act.activation(eaT[:, u % 2], eaT_p[:], ACT.Copy).then_inc(xT_ready, 1)

                walk(act, NB, AHEAD + 2, body)

            @block.vector
            def _(dve):
                dve.memset(ea[:], 1.0).then_inc(ea_set, 1)
                dve.memset(xd[:], 0.0).then_inc(begun, 1)

                def body(j, u):
                    i = j * U + u
                    if works(i, NB):
                        if late(j):
                            r, s = turn_of(j, u)
                            dve.wait_ge(scattered[s], (r - 1) * T * 16)
                        prepare_batch(dve, i, u, idx, dst_f, idx_cols, dst_cols, idx_ready, dstf_ready)
                    j, u, i = back(j, u, AHEAD)
                    jb, ub, ib = back(j, u, 2)
                    if works(ib, NB):
                        r, s = turn_of(jb, ub)
                        dve.wait_ge(logitT_ready, ib + 1)
                        dve.wait_ge(brk_in[s], (r + 1) * 16)
                        dve.tensor_tensor_scan(run[:], brk[:, s, 0:P], logitT_p, LOW, ALU.add, ALU.max)\
                           .then_inc(run_ready, 1)
                        dve.wait_ge(run_ready, ib + 1)
                        dve.tensor_tensor_scan(top[:, ::-1], brk[:, s, 1:P + 1][:, ::-1], run[:, ::-1], LOW,
                                               ALU.add, ALU.max).then_inc(top_ready, 1)
                        dve.wait_ge(spread_ready, ib + 1)
                        dve.wait_ge(dstf_ready, ib + 1)
                        dve.tensor_tensor(same[:], wide[:], dst_f[:, ub].unsqueeze(2).to_broadcast([P, T, P]),
                                          ALU.is_equal).then_inc(same_ready, 1)
                        dve.wait_ge(topT_ready, ib + 1)
                        dve.tensor_tensor(diff[:], logit[:], top_p, ALU.subtract).then_inc(diff_ready, 1)
                        if late(r):
                            dve.wait_ge(sided[s], r * 64)
                        dve.tensor_copy(soft[:, s, :, 0:H], top_p.rearrange("p (t h) -> p t h", h=H))\
                           .then_inc(top_kept, 1)
                        dve.wait_ge(ex_ready, ib + 1)
                        dve.wait_ge(v_ready, ib + 1)
                        dve.tensor_tensor(exv[:].rearrange("p t (h c) -> p (t h) c", c=C),
                                          v_p[:].rearrange("p (n c) -> p n c", c=C),
                                          ex[:].unsqueeze(2).to_broadcast([P, TH, C]), ALU.mult)\
                           .then_inc(exv_ready, 1)
                    jb, ub, ib = back(j, u, 1)
                    if works(ib, NB):
                        dve.wait_ge(q_ready, ib + 1)
                        dve.tensor_tensor(qk[:], k_p[:], q[:], ALU.mult).then_inc(qk_ready, 1)
                        dve.wait_ge(qk_ready, ib + 1)
                        if not isinstance(ib, int) or ib >= 1:
                            dve.wait_ge(diff_ready, ib)
                        dve.tensor_reduce(logit[:], qk[:].rearrange("p (n c) -> p n c", c=C),
                                          mybir.AxisListType.X, ALU.add).then_inc(logit_ready, 1)
                    jb, ub, ib = back(j, u, 2)
                    if works(ib, NB):
                        r, s = turn_of(jb, ub)
                        dve.wait_ge(sums_ready, ib + 1)
                        dve.reciprocal(rden[:], den_p).then_inc(rden_ready, 1)
                        if late(r):
                            dve.wait_ge(scattered[s], r * T * 16)
                        dve.tensor_copy(soft[:, s, :, H:2 * H], den_p.rearrange("p (t h) -> p t h", h=H))\
                           .then_inc(den_kept, 1)
                        dve.wait_ge(rden_ready, ib + 1)
                        dve.tensor_tensor(att[:, s].rearrange("p t (h c) -> p (t h) c", c=C),
                                          wide[:].rearrange("p t (h c) -> p (t h) c", c=C),
                                          rden[:].unsqueeze(2).to_broadcast([P, TH, C]), ALU.mult)\
                           .then_inc(att_ready, 1)

                walk(dve, NB, AHEAD + 2, body)

            @block.tensor
            def _(pe):
                def body(j, u):
                    j, u, i = back(j, u, AHEAD)
                    jb, ub, ib = back(j, u, 2)
                    if works(ib, NB):
                        pe.wait_ge(logit_ready, ib + 1)
                        if not isinstance(ib, int) or ib >= 1:
                            pe.wait_ge(den_kept, ib)
                        pe.transpose(logitT_p, logit[:], ident[:]).then_inc(logitT_ready, 1)
                    jb, ub, ib = back(j, u, 1)
                    if works(ib, NB):
                        pe.wait_ge(xT_ready, ib + 1)
                        if not isinstance(ib, int) or ib >= 1:
                            pe.wait_ge(qk_ready, ib)
                        add_bias(pe, q_p[:], onesB, bq_3, P, T)
                        for t in range(T):
                            pe.matmul(q_p[:, t * D:(t + 1) * D], xdT[:, ub % 2, t], Wq_s[:], start=False,
                                      stop=(t == T - 1))
                        for t in range(T):
                            pe.matmul(k_p[:, t * D:(t + 1) * D], xsT[:, ub % 2, t], Wk_s[:], start=True, stop=False)
                            mm = pe.matmul(k_p[:, t * D:(t + 1) * D], eaT[:, ub % 2, t], We_s[:, 0, :],
                                           start=False, stop=True)
                        mm.then_inc(kq_ready, 1)
                    jb, ub, ib = back(j, u, 2)
                    if works(ib, NB):
                        pe.wait_ge(top_ready, ib + 1)
                        pe.wait_ge(dstf_ready, ib + 1)
                        if not isinstance(ib, int) or ib >= 1:
                            pe.wait_ge(att_ready, ib)
                        for t in range(T):
                            mm = pe.transpose(wide[:, t, :], dst_f[:, ub, t:t + 1].to_broadcast([P, P]), ident[:])
                        mm.then_inc(spread_ready, 1)
                        pe.transpose(top_p, top[:], ident[0:TH, 0:TH]).then_inc(topT_ready, 1)
                    if works(i, NB):
                        r, s = turn_of(j, u)
                        pe.wait_ge(rows_in[s], (r + 1) * 2 * T * 16)
                        split = 2 if isinstance(i, int) and i == NB - 1 and E_LAST >= P and E_LAST % P else 1
                        pe.wait_ge(ea_in[s], (r + split) * 16)
                        if not isinstance(i, int) or i >= 1:
                            pe.wait_ge(xT_ready, i)
                        for t in range(T):
                            pe.transpose(xsT_p[:, t], xs[:, s, t], ident[:])
                            pe.transpose(xdT_p[:, t], xd[:, s, t], ident[:])
                            mm = pe.transpose(eaT_p[:, t], ea[:, s, t], ident[:])
                        mm.then_inc(turned_ready, 1)
                    if works(ib, NB):
                        pe.wait_ge(exv_ready, ib + 1)
                        for t in range(T):
                            pe.matmul(wide[:, t, :], same[:, t, :], exv[:, t, :], start=True, stop=True)
                            mm = pe.matmul(den_p[:, t * H:(t + 1) * H], same[:, t, :], ex[:, t * H:(t + 1) * H],
                                           start=True, stop=True)
                        mm.then_inc(sums_ready, 1)
                    jb, ub, ib = back(j, u, 1)
                    if works(ib, NB):
                        if not isinstance(ib, int) or ib >= 1:
                            pe.wait_ge(exv_ready, ib)
                        for t in range(T):
                            pe.matmul(v_p[:, t * D:(t + 1) * D], xsT[:, ub % 2, t], Wv_s[:], start=True, stop=False)
                            mm = pe.matmul(v_p[:, t * D:(t + 1) * D], eaT[:, ub % 2, t], We_s[:, 1, :],
                                           start=False, stop=True)
                        mm.then_inc(v_ready, 1)

                walk(pe, NB, AHEAD + 2, body)



def gather_dst(pool, rows, dram, index, last_row):
    return pool.indirect_dma_start(rows, None, dram, bass.IndirectOffsetOnAxis(index, 0), bounds_check=last_row,
                                   oob_is_err=False)


def joins1(nc, sem, NI, CI, PI, side, soft_side, agg, ident, same_item, count_item, row_item, head_of, N):
    with ExitStack() as part:
        def sb(name, shape, dt=F32):
            return part.enter_context(nc.sbuf_tensor(name, shape, dt))

        items = sb("j1_items", [PI, CI, D])
        soft = sb("j1_soft", [PI, CI, 2 * H])
        av = sb("j1_av", [D, NI])
        brk = sb("j1_brk", [H, NI + 1])
        top = sb("j1_top", [H, NI])
        run = sb("j1_run", [H, NI])
        whole = sb("j1_whole", [H, NI])
        den = sb("j1_den", [H, NI])
        w = sb("j1_w", [H, NI])
        num_run = sb("j1_num_run", [D, NI])
        den_run = sb("j1_den_run", [D, NI])
        W8 = -(-CI // 2)
        turn = part.enter_context(nc.psum_tensor("j1_turn", [P, 2, 2, 512], F32))
        s_in, s_turn, s_v, s_p = sem("j1_in"), sem("j1_turned"), sem("j1_vector_steps"), sem("j1_product_steps")
        s_a, s_rows, s_out, s_rt = sem("j1_act_steps"), sem("j1_rows"), sem("j1_out"), sem("j1_rows_turned")
        s_rt2 = sem("j1_scans")
        chunks = [(c * PI, min(CI, c + W8) * PI) for c in range(0, CI, W8)]
        assert all(b - a <= 512 for a, b in chunks) and H <= 32

        with nc.Block() as block:
            @block.sync
            def _(sp):
                sp.dma_start(items[:], side.rearrange("(c p) d -> p c d", p=PI)).then_inc(s_in, 16)
                sp.dma_start(soft[:], soft_side.rearrange("(c p) d -> p c d", p=PI)).then_inc(s_in, 16)

            @block.tensor
            def _(pe):
                def col(n, c):
                    k, r = divmod(c, W8)
                    return turn[:, n, k, r * PI:(r + 1) * PI]

                pe.wait_ge(s_in, 32)
                for c in range(CI):
                    pe.transpose(col(0, c)[0:H], soft[:, c, 0:H], ident[0:PI, 0:PI])
                    mm = pe.transpose(col(1, c)[0:H], soft[:, c, H:2 * H], ident[0:PI, 0:PI])
                mm.then_inc(s_turn, 1)
                pe.wait_ge(s_v, 2)
                for c in range(CI):
                    mm = pe.transpose(col(0, c), items[:, c, :], ident[0:PI, 0:PI])
                mm.then_inc(s_turn, 1)
                pe.wait_ge(s_v, 8)
                for k, (a, b) in enumerate(chunks):
                    mm = pe.matmul(turn[:, 1, k, 0:b - a], head_of[:], w[:, a:b], start=True, stop=True)
                mm.then_inc(s_p, 1)
                for c in range(CI):
                    if c == 0:
                        pe.wait_ge(s_v, 14)
                    elif c % 4 == 0:
                        pe.wait_ge(s_rows, c // 4)
                    mm = pe.transpose(turn[0:PI, 0, 0, (c % 4) * P:(c % 4 + 1) * P],
                                      av[:, c * PI:(c + 1) * PI], ident[:])
                    if c % 4 == 3 or c == CI - 1:
                        mm.then_inc(s_rt, 1)

            @block.scalar
            def _(act):
                act.wait_ge(s_v, 6)
                act.activation(w[:], w[:], ACT.Exp, scale=float(C) ** -0.5).then_inc(s_a, 1)

            @block.vector
            def _(dve):
                def halves(to, n, rows):
                    for k, (a, b) in enumerate(chunks):
                        last = dve.tensor_copy(to[:, a:b], turn[0:rows, n, k, 0:b - a])
                    return last

                dve.wait_ge(s_turn, 1)
                halves(top, 0, H).then_inc(s_v, 1)
                halves(den, 1, H).then_inc(s_v, 1)
                dve.memset(brk[:], LOW).then_inc(s_v, 1)
                dve.wait_ge(s_v, 3)
                dve.tensor_scalar(brk[:, 0:NI], same_item[0:H], -1.0, -LOW, ALU.add, ALU.mult).then_inc(s_v, 1)
                dve.wait_ge(s_v, 4)
                dve.tensor_tensor_scan(run[:], brk[:, 0:NI], top[:], LOW, ALU.add, ALU.max).then_inc(s_v, 1)
                dve.wait_ge(s_v, 5)
                dve.tensor_tensor_scan(whole[:, ::-1], brk[:, 1:NI + 1][:, ::-1], run[:, ::-1], LOW,
                                       ALU.add, ALU.max).then_inc(s_rt2, 1)
                dve.wait_ge(s_rt2, 1)
                dve.tensor_tensor(w[:], top[:], whole[:], ALU.subtract).then_inc(s_v, 1)
                dve.wait_ge(s_a, 1)
                dve.tensor_tensor(w[:], w[:], den[:], ALU.mult).then_inc(s_v, 1)
                dve.wait_ge(s_v, 7)
                dve.tensor_tensor(w[:], w[:], count_item[0:H], ALU.mult).then_inc(s_v, 1)
                dve.wait_ge(s_turn, 2)
                halves(av, 0, D).then_inc(s_v, 1)
                dve.wait_ge(s_p, 1)
                halves(den_run, 1, D).then_inc(s_v, 1)
                dve.wait_ge(s_v, 10)
                dve.tensor_tensor(av[:], av[:], den_run[:], ALU.mult).then_inc(s_v, 1)
                dve.wait_ge(s_v, 11)
                dve.tensor_tensor_scan(num_run[:], same_item[:], av[:], 0.0, ALU.mult, ALU.add).then_inc(s_v, 1)
                dve.wait_ge(s_v, 12)
                dve.tensor_tensor_scan(av[:], same_item[:], den_run[:], 0.0, ALU.mult, ALU.add).then_inc(s_rt2, 1)
                dve.wait_ge(s_rt2, 2)
                dve.reciprocal(den_run[:], av[:]).then_inc(s_v, 1)
                dve.wait_ge(s_v, 13)
                dve.tensor_tensor(av[:], num_run[:], den_run[:], ALU.mult).then_inc(s_v, 1)
                for c in range(0, CI, 4):
                    n = min(4, CI - c)
                    dve.wait_ge(s_rt, c // 4 + 1)
                    dve.tensor_copy(items[:, c:c + n, :].rearrange("p c d -> p (c d)"), turn[0:PI, 0, 0, 0:n * P])\
                       .then_inc(s_rows, 1)

            @block.gpsimd
            def _(pool):
                for c in range(CI):
                    if c % 4 == 0:
                        pool.wait_ge(s_rows, c // 4 + 1)
                    scatter_rows(pool, agg, row_item[:, c:c + 1].bitcast(U32), items[:, c, :], N - 1)\
                        .then_inc(s_out, 16)
                pool.wait_ge(s_out, CI * 16)


def nodes1(nc, sem, NG, group, geometry, x1, agg, out, half, mid, root_d, ident, Wskip_s, Wf1_s, Wf2_s, onesB,
           bskip_3, bf2_3, g1_col, b1_col, bf1_col, g1_row, g2_row, b2n_row):
    F = FF // D
    with ExitStack() as part:
        def sb(name, shape, dt=F32):
            return part.enter_context(nc.sbuf_tensor(name, shape, dt))

        def ps(name, shape):
            return part.enter_context(nc.psum_tensor(name, shape, F32))

        xs, ags = sb("n1_x", [P, U, T, D]), sb("n1_agg", [P, U, T, D])
        xT = sb("n1_xT", [D, 2, T * P])
        y, z = sb("n1_y", [P, 2, T, D]), sb("n1_z", [P, S, T, D])
        zg = sb("n1_zg", [P, S, T, D])
        xb = sb("n1_xb", [P, U, T, D])
        hT = sb("n1_hT", [D, 2, T * P])
        act_T = sb("n1_act_T", [D, 2, F, T * P])
        w, wn = sb("n1_w", [P, 2, T, D]), sb("n1_wn", [P, 2, T, D])
        wg = sb("n1_wg", [P, 2, T, D])
        res, o = sb("n1_res", [P, S, T, D]), sb("n1_o", [P, S, T, D])
        xT_p, skip_p = ps("n1_xT_p", [D, T * P]), ps("n1_skip_p", [P, T * D])
        zT_p, lin2_p = ps("n1_zT_p", [D, T * P]), ps("n1_lin2_p", [P, T * D])
        lin1_p = ps("n1_lin1_p", [D, F, T * P])
        nm1, nm2, nm3 = (Norm(part, nc, sem, f"n1_norm{k}") for k in (1, 2, 3))

        rows_in = [sem(f"n1_rows_in{u}") for u in range(U)]
        stored = [sem(f"n1_stored{s}") for s in range(S)]
        xT_p_ready, xT_ready, skip_ready = sem("n1_xT_p_ready"), sem("n1_xT_ready"), sem("n1_skip_ready")
        y_ready, z_ready, zT_p_ready = sem("n1_y_ready"), sem("n1_z_ready"), sem("n1_zT_p_ready")
        hT_ready, lin1_ready, gelu_ready = sem("n1_hT_ready"), sem("n1_lin1_ready"), sem("n1_gelu_ready")
        lin2_ready, w_ready, wn_ready = sem("n1_lin2_ready"), sem("n1_w_ready"), sem("n1_wn_ready")
        zg_ready, wg_ready, xb_ready = sem("n1_zg_ready"), sem("n1_wg_ready"), sem("n1_xb_ready")
        r_ready, o_ready = sem("n1_r_ready"), sem("n1_o_ready")

        def rows(psum, p, t):
            return psum[0:p, 0:t * D].rearrange("p (t d) -> p t d", d=D)

        with nc.Block() as block:
            @block.sync
            def _(sp):
                def body(j, u):
                    g = j * U + u
                    if works(g, NG):
                        p, t = geometry(g)
                        if late(j):
                            sp.wait_ge(xT_p_ready, g - U + 1)
                            sp.wait_ge(xb_ready, g - U + 1)
                            sp.wait_ge(y_ready, g - U + 1)
                        sp.dma_start(xs[0:p, u, 0:t], group(x1, g)).then_inc(rows_in[u], 16)
                        sp.dma_start(ags[0:p, u, 0:t], group(agg, g)).then_inc(rows_in[u], 16)
                    jb, ub, gb = back(j, u, 7)
                    if works(gb, NG):
                        p, t = geometry(gb)
                        sp.wait_ge(o_ready, gb + 1)
                        sp.dma_start(group(out, gb), o[0:p, ub % S, 0:t]).then_inc(stored[ub % S], 16)

                walk(sp, NG, 7, body)
                for s in range(S):
                    sp.wait_ge(stored[s], len(range(s, NG, S)) * 16)

            @block.tensor
            def _(pe):
                def body(j, u):
                    g = j * U + u
                    if works(g, NG):
                        p, t = geometry(g)
                        pe.wait_ge(rows_in[u], (j + 1) * 32)
                        if not isinstance(g, int) or g >= 1:
                            pe.wait_ge(xT_ready, g)
                        for c in range(t):
                            mm = pe.transpose(xT_p[:, c * p:(c + 1) * p], xs[0:p, u, c, :], ident[0:p, 0:p])
                        mm.then_inc(xT_p_ready, 1)
                    jb, ub, gb = back(j, u, 2)
                    if works(gb, NG):
                        p, t = geometry(gb)
                        pe.wait_ge(z_ready, gb + 1)
                        if not isinstance(gb, int) or gb >= 1:
                            pe.wait_ge(hT_ready, gb)
                        for c in range(t):
                            mm = pe.transpose(zT_p[:, c * p:(c + 1) * p], z[0:p, ub % S, c, :], ident[0:p, 0:p])
                        mm.then_inc(zT_p_ready, 1)
                    jb, ub, gb = back(j, u, 3)
                    if works(gb, NG):
                        p, t = geometry(gb)
                        pe.wait_ge(gelu_ready, F * gb + F)
                        if not isinstance(gb, int) or gb >= 1:
                            pe.wait_ge(w_ready, gb)
                        add_bias(pe, lin2_p[0:p, 0:t * D], onesB, bf2_3, p, t)
                        for c in range(t):
                            for f in range(F):
                                mm = pe.matmul(lin2_p[0:p, c * D:(c + 1) * D],
                                               act_T[:, ub % 2, f, c * p:(c + 1) * p], Wf2_s[:, f, :],
                                               start=False, stop=(c == t - 1 and f == F - 1))
                        mm.then_inc(lin2_ready, 1)
                    if works(g, NG):
                        p, t = geometry(g)
                        pe.wait_ge(xT_ready, g + 1)
                        if not isinstance(g, int) or g >= 1:
                            pe.wait_ge(y_ready, g)
                        add_bias(pe, skip_p[0:p, 0:t * D], onesB, bskip_3, p, t)
                        for c in range(t):
                            mm = pe.matmul(skip_p[0:p, c * D:(c + 1) * D], xT[:, u % 2, c * p:(c + 1) * p],
                                           Wskip_s[:], start=False, stop=(c == t - 1))
                        mm.then_inc(skip_ready, 1)
                    jb, ub, gb = back(j, u, 2)
                    if works(gb, NG):
                        p, t = geometry(gb)
                        pe.wait_ge(hT_ready, gb + 1)
                        for f in range(F):
                            if not isinstance(gb, int) or gb >= 1:
                                pe.wait_ge(gelu_ready, F * gb - F + f + 1)
                            pe.matmul(lin1_p[:, f, 0:t * p], Wf1_s[:, f * D:(f + 1) * D], hT[:, ub % 2, 0:t * p],
                                      start=True, stop=True).then_inc(lin1_ready, 1)

                walk(pe, NG, 3, body)

            @block.scalar
            def _(act):
                def body(j, u):
                    g = j * U + u
                    if works(g, NG):
                        p, t = geometry(g)
                        act.wait_ge(xT_p_ready, g + 1)
                        if not isinstance(g, int) or g >= 2:
                            act.wait_ge(skip_ready, g - 1)
                        act.activation(xT[:, u % 2, 0:t * p], xT_p[:, 0:t * p], ACT.Copy).then_inc(xT_ready, 1)
                    jb, ub, gb = back(j, u, 2)
                    if works(gb, NG):
                        p, t = geometry(gb)
                        act.wait_ge(zT_p_ready, gb + 1)
                        if not isinstance(gb, int) or gb >= 2:
                            act.wait_ge(lin1_ready, F * gb - F)
                        act.activation(hT[:, ub % 2, 0:t * p], zT_p[:, 0:t * p], ACT.Identity, bias=b1_col[:],
                                       scale=g1_col[:]).then_inc(hT_ready, 1)
                    jo, uo, go = back(j, u, 5)
                    if works(go, NG):
                        po, to = geometry(go)
                        r, s = turn_of(jo, uo)
                        if late(r):
                            act.wait_ge(stored[s], r * 16)
                        norm_apply_act(act, nm3, o[:, s], res[:, s], po, to, uo, go, o_ready)
                    if works(gb, NG):
                        if not isinstance(gb, int) or gb >= 2:
                            act.wait_ge(lin2_ready, gb - 1)
                        for f in range(F):
                            act.wait_ge(lin1_ready, F * gb + f + 1)
                            act.activation(act_T[:, ub % 2, f, 0:t * p], lin1_p[:, f, 0:t * p], ACT.Gelu,
                                           bias=bf1_col[:, f:f + 1]).then_inc(gelu_ready, 1)

                walk(act, NG, 5, body)

            @block.vector
            def _(dve):
                def body(j, u):
                    g = j * U + u
                    jb, ub, gb = back(j, u, 4)
                    if works(gb, NG):
                        p, t = geometry(gb)
                        r, s = turn_of(jb, ub)
                        dve.wait_ge(wg_ready, gb + 1)
                        dve.wait_ge(xb_ready, gb + 1)
                        if late(r):
                            dve.wait_ge(o_ready, gb - S + 1)
                        dve.tensor_tensor(res[0:p, s, 0:t], wg[0:p, ub % 2, 0:t], xb[0:p, ub, 0:t], ALU.add)\
                           .then_inc(r_ready, 1)
                        norm_stats(dve, nm3, res[:, s], p, t, ub, gb, r_ready)
                    jb, ub, gb = back(j, u, 3)
                    if works(gb, NG):
                        pb, tb = geometry(gb)
                        dve.wait_ge(lin2_ready, gb + 1)
                        dve.wait_ge(zg_ready, gb + 1)
                        dve.tensor_tensor(w[0:pb, ub % 2, 0:tb], rows(lin2_p, pb, tb), zg[0:pb, ub % S, 0:tb],
                                          ALU.add).then_inc(w_ready, 1)
                        norm_stats(dve, nm2, w[:, ub % 2], pb, tb, ub, gb, w_ready)
                    if works(g, NG):
                        p, t = geometry(g)
                        dve.wait_ge(skip_ready, g + 1)
                        dve.wait_ge(rows_in[u], (j + 1) * 32)
                        dve.tensor_tensor(y[0:p, u % 2, 0:t], rows(skip_p, p, t), ags[0:p, u, 0:t], ALU.add)\
                           .then_inc(y_ready, 1)
                        norm_stats(dve, nm1, y[:, u % 2], p, t, u, g, y_ready)
                    if works(gb, NG):
                        if not isinstance(gb, int) or gb >= 2:
                            dve.wait_ge(wg_ready, gb - 1)
                        norm_apply(dve, nm2, wn[:, ub % 2], w[:, ub % 2], pb, tb, ub, gb, wn_ready)
                    if works(g, NG):
                        r, s = turn_of(j, u)
                        if late(r):
                            dve.wait_ge(zT_p_ready, g - S + 1)
                            dve.wait_ge(zg_ready, g - S + 1)
                        norm_apply(dve, nm1, z[:, s], y[:, u % 2], p, t, u, g, z_ready)

                walk(dve, NG, 4, body)

            @block.gpsimd
            def _(pool):
                def body(j, u):
                    g = j * U + u
                    if works(g, NG):
                        p, t = geometry(g)
                        if late(j):
                            pool.wait_ge(r_ready, g - U + 1)
                        pool.wait_ge(rows_in[u], (j + 1) * 32)
                        pool.tensor_tensor(xb[0:p, u, 0:t], xs[0:p, u, 0:t], b2n_row[0:p, 0:t], ALU.add)\
                            .then_inc(xb_ready, 1)
                    jb, ub, gb = back(j, u, 4)
                    if works(gb, NG):
                        pc, tc = geometry(gb)
                        norm_root(pool, nm3, pc, tc, ub, gb, half, mid, root_d, shift=True)
                    jb, ub, gb = back(j, u, 3)
                    if works(gb, NG):
                        pb, tb = geometry(gb)
                        norm_root(pool, nm2, pb, tb, ub, gb, half, mid, root_d)
                    if works(g, NG):
                        norm_root(pool, nm1, p, t, u, g, half, mid, root_d)
                    if works(gb, NG):
                        pool.wait_ge(wn_ready, gb + 1)
                        if not isinstance(gb, int) or gb >= 2:
                            pool.wait_ge(r_ready, gb - 1)
                        pool.tensor_tensor(wg[0:pb, ub % 2, 0:tb], wn[0:pb, ub % 2, 0:tb], g2_row[0:pb, 0:tb],
                                           ALU.mult).then_inc(wg_ready, 1)
                    if works(g, NG):
                        r, s = turn_of(j, u)
                        pool.wait_ge(z_ready, g + 1)
                        if late(r):
                            pool.wait_ge(w_ready, g - S + 1)
                        pool.tensor_tensor(zg[0:p, s, 0:t], z[0:p, s, 0:t], g1_row[0:p, 0:t], ALU.mult)\
                            .then_inc(zg_ready, 1)

                walk(pool, NG, 4, body)



_INS = ['x', 'src', 'dst', 'edge_attr_64', 'L0_gnn_W1', 'L0_gnn_gamma', 'L0_gnn_beta', 'L0_gnn_W2', 'L0_gnn_b2',
        'L0_gnn_eps', 'L1_gnn_Wq', 'L1_gnn_bq', 'L1_gnn_Wk', 'L1_gnn_bk', 'L1_gnn_Wv', 'L1_gnn_bv', 'L1_gnn_We',
        'L1_gnn_Wskip', 'L1_gnn_bskip', 'L1_gnn_g1', 'L1_gnn_b1', 'L1_gnn_g2', 'L1_gnn_b2', 'L1_gnn_Wf1',
        'L1_gnn_bf1', 'L1_gnn_Wf2', 'L1_gnn_bf2']


def kernel(**inputs):
    import numpy as _np
    import concourse.bacc as _bacc
    from concourse.bass_utils import run_bass_kernel_spmd as _run

    nc = _bacc.Bacc("TRN2", target_bir_lowering=False, num_devices=1)
    arrays, args = {}, []
    for name in _INS:
        a = _np.ascontiguousarray(inputs[name])
        if a.ndim == 0:
            a = a.reshape(1)
        arrays[f"in_{name}"] = a
        args.append(nc.dram_tensor(f"in_{name}", a.shape, mybir.dt.from_np(a.dtype), kind="ExternalInput").ap())
    n = inputs['x'].shape[0]
    args.append(nc.dram_tensor("out_0", (n, D), F32, kind="ExternalOutput").ap())
    build(nc, *args)
    r = _run(nc, [arrays], core_ids=[0])
    return r.results[0]["out_0"]
```

```python
from contextlib import ExitStack

import concourse.bass as bass
from concourse import mybir

ALU = mybir.AluOpType
ACT = mybir.ActivationFunctionType
F32 = mybir.dt.float32
BF16 = mybir.dt.bfloat16
I32 = mybir.dt.int32
U32 = mybir.dt.uint32

P = 128
D = 128
T = 4
B = T * P
H = 8
C = D // H
DE = 64
FF = 4 * D
U = 8
S = 4
AHEAD = 2
LN_EPS = 1e-5
BN_EPS = 1e-5
LOW = -1e30
PAD = 200000
SKIP = 1 << 20


def walk(eng, steps, lag, body):
    full = (steps - 1) // U
    if full <= 2:
        for i in range(steps + lag):
            body(i // U, i % U)
        return
    for i in range(2 * U):
        body(i // U, i % U)
    with eng.Fori(2, full) as j:
        for u in range(U):
            body(j, u)
    for i in range(full * U, steps + lag):
        body(i // U, i % U)


def turn_of(j, u):
    return j * (U // S) + u // S, u % S


def back(j, u, lag):
    k = u - lag
    return j + k // U, k % U, j * U + k


def ready_values(eng, *values):
    return [v if isinstance(v, int) else eng.to_reg(v) for v in values]


def works(i, steps):
    return not isinstance(i, int) or 0 <= i < steps


def late(j, n=1):
    return not isinstance(j, int) or j >= n


def build(nc, x, src, dst, edge_attr, W1, gamma, beta, W2, b2, eps, Wq, bq, Wk, bk, Wv, bv, We, Wskip, bskip,
          g1, b1, g2, b2n, Wf1, bf1, Wf2, bf2, out):
    N = x.shape[0]
    E = src.shape[0]
    NB = -(-E // B)
    NG = -(-N // B)
    E_LAST = E - (NB - 1) * B
    N_LAST = N - (NG - 1) * B
    P_LAST = next(p for p in (128, 112, 96, 80, 64, 48, 32, 16) if N_LAST % p == 0 and N_LAST // p <= T)
    T_LAST = N_LAST // P_LAST
    NI = NB * T * 2
    CI = next(c for c in range(1, NI + 1) if NI % c == 0 and NI // c <= P)
    PI = NI // CI
    ZC = next(c for c in range(2048, 0, -1) if N % c == 0)
    NZ = N // ZC
    Z_FIRST = min(10, NZ)
    NE = min(4 * U, NB // 3)

    agg = nc.dram_tensor("agg", [N, D], F32).ap()
    x1 = nc.dram_tensor("x1", [N, D], F32).ap()
    skipped = nc.dram_tensor("skipped", [N, D], F32).ap()
    rows_side = nc.dram_tensor("rows_side", [2, NI, D], F32).ap()
    soft_side = nc.dram_tensor("soft_side", [NI, 2 * H], F32).ap()
    breaks = nc.dram_tensor("breaks", [NB, T, H, P + 1], F32).ap()
    keys = nc.dram_tensor("keys", [1, NI], F32).ap()
    key_rows = nc.dram_tensor("key_rows", [1, NI], I32).ap()

    def geometry(g):
        if isinstance(g, int) and g == NG - 1:
            return P_LAST, T_LAST
        return P, T

    def group(dram, g):
        p, t = geometry(g)
        rows = dram[bass.ds(g * B, p * t), :] if not isinstance(g, int) else dram[g * B:g * B + p * t, :]
        return rows.rearrange("(p t) d -> p t d", t=t)

    with ExitStack() as ctx:
        def keep(name, shape, dt=F32):
            return ctx.enter_context(nc.sbuf_tensor(name, shape, dt))

        zeros = keep("zeros", [P, ZC])
        s_zero = [nc.alloc_semaphore(f"agg_zeroed{n}") for n in range(3)]
        part_sems = []

        def sem(name):
            part_sems.append(nc.alloc_semaphore(name))
            return part_sems[-1]

        def zero_part(eng, z):
            if z >= 3:
                eng.wait_ge(s_zero[z % 3], z // 3 * 16)
            eng.dma_start(agg.rearrange("n d -> (n d)")[z * P * ZC:(z + 1) * P * ZC]
                          .rearrange("(p c) -> p c", p=P), zeros[:]).then_inc(s_zero[z % 3], 16)

        def clear():
            nc.clear_and_free_semaphores(part_sems[:])
            nc.all_engine_barrier()
            part_sems.clear()

        ident = keep("ident", [P, P])
        idx_cols = keep("idx_cols", [P, NB, 3, T], I32)
        dst_cols = keep("dst_cols", [P, NB, T])
        same_item = keep("same_item", [P, NI])
        count_item = keep("count_item", [P, NI])
        row_item = keep("row_item", [PI, CI], I32)
        W1T = keep("W1T", [D, D])
        W2T = keep("W2T", [D, D])
        Wq_s = keep("Wq_s", [D, D])
        Wk_s = keep("Wk_s", [D, D])
        Wv_s = keep("Wv_s", [D, D])
        We_s = keep("We_s", [DE + 1, 2, D])
        Wskip_s = keep("Wskip_s", [D, D])
        Wf1_s = keep("Wf1_s", [D, FF])
        Wf2_s = keep("Wf2_s", [D, T, D])
        onesB = keep("onesB", [3, P], BF16)
        b2_3 = keep("b2_3", [3, T, D], BF16)
        bq_3 = keep("bq_3", [3, T, D], BF16)
        bskip_3 = keep("bskip_3", [3, T, D], BF16)
        bf2_3 = keep("bf2_3", [3, T, D], BF16)
        g1_col = keep("g1_col", [D, 1])
        b1_col = keep("b1_col", [D, 1])
        bf1_col = keep("bf1_col", [D, T])
        g1_row = keep("g1_row", [P, T, D])
        g2_row = keep("g2_row", [P, T, D])
        b2n_row = keep("b2n_row", [P, T, D])
        gamma_col = keep("gamma_col", [D, 1])
        beta_col = keep("beta_col", [D, 1])
        eps1 = keep("eps1", [P, 1])
        half = keep("half", [P, 3 * T])
        root_d = keep("root_d", [P, 3 * T])
        bn_scale = keep("bn_scale", [D, 1])
        bn_shift = keep("bn_shift", [D, 1])
        head_of = keep("head_of", [H, D])

        with ExitStack() as part:
            def sb(name, shape, dt=F32):
                return part.enter_context(nc.sbuf_tensor(name, shape, dt))

            def ps(name, shape):
                return part.enter_context(nc.psum_tensor(name, shape, F32))

            dst_i = sb("dst_i", [NB, B], I32)
            next_i = sb("next_i", [NB, B], I32)
            src_i = sb("src_i", [NB, B], I32)
            dst_f = sb("dst_f", [NB, T, P])
            next_f = sb("next_f", [NB, T, P])
            src_f = sb("src_f", [NB, T, P])
            row_f = sb("row_f", [NB, T, P])
            eq = sb("eq", [NB, T, P])
            brk = sb("brk", [NB, T, P + 1])
            ends = sb("ends", [NB, T, 2])
            key_b = sb("key_b", [P, NI])
            key_skip = sb("key_skip", [1, NI])
            key_skip_i = sb("key_skip_i", [1, NI], I32)
            W1_l = sb("W1_l", [D, D])
            W2_l = sb("W2_l", [D, D])
            bias = sb("bias", [1, 5, D])
            part_b = sb("part_b", [1, 4, 3, T, D], BF16)
            rest = sb("rest", [1, 4, D])
            turn = ps("turn", [P, 4, 512])

            s_mem, s_idx, s_w, s_wb = sem("tables_cleared"), sem("indices_in"), sem("weights_in"), sem("bias_parts_in")
            s_zset = sem("zeros_set")
            s_id0, s_id, s_ho = sem("ident_zero"), sem("ident_ready"), sem("head_of_steps")
            s_f, s_eq, s_brk = sem("indices_float"), sem("row_steps"), sem("breaks_ready")
            s_ends, s_keys, s_keyb, s_item = sem("ends_ready"), sem("keys_out"), sem("keys_in"), sem("item_steps")
            s_rowo, s_rowi, s_brko = sem("item_rows_out"), sem("item_rows_in"), sem("breaks_out")
            s_turn, s_col, s_bp, s_v = sem("turned"), sem("turned_read"), sem("bias_steps"), sem("small_steps")
            tail = NB - 1

            with nc.Block() as block:
                @block.sync
                def _(sp):
                    sp.wait_ge(s_mem, 3)
                    for tile_, dram, off in ((dst_i, dst, 0), (next_i, dst, 1), (src_i, src, 0)):
                        if tail:
                            sp.dma_start(tile_[0:tail, :], dram[off:off + tail * B].rearrange("(b e) -> b e", e=B))\
                              .then_inc(s_idx, 16)
                        sp.dma_start(tile_[tail:NB, 0:E_LAST - off],
                                     dram[off + tail * B:E].rearrange("(b e) -> b e", b=1)).then_inc(s_idx, 16)
                    sp.wait_ge(s_ends, 1)
                    sp.dma_start(keys.rearrange("a (b i) -> (a b) i", i=2 * T),
                                 ends[:].rearrange("b t e -> b (t e)")).then_inc(s_keys, 16)
                    sp.wait_ge(s_keys, 16)
                    sp.dma_start(key_b[:], keys.to_broadcast([P, NI])).then_inc(s_keyb, 16)
                    sp.wait_ge(s_brk, 1)
                    for h in range(H):
                        sp.dma_start(breaks[:, :, h, :], brk[:]).then_inc(s_brko, 16)
                    sp.wait_ge(s_item, 6)
                    sp.dma_start(key_rows, key_skip_i[:]).then_inc(s_rowo, 16)
                    sp.wait_ge(s_rowo, 16)
                    with nc.allow_non_contiguous_dma(reason="a few hundred indices, once"):
                        sp.dma_start(row_item[:], key_rows.rearrange("a (c p) -> p (a c)", p=PI)).then_inc(s_rowi, 16)
                    sp.wait_ge(s_bp, 6)
                    for n, t in enumerate((b2_3, bq_3, bskip_3, bf2_3)):
                        for r in range(3):
                            sp.dma_start(t[r:r + 1], part_b[0:1, n, r]).then_inc(s_wb, 16)
                    sp.wait_ge(s_wb, 12 * 16)
                    sp.wait_ge(s_rowi, 16)
                    sp.wait_ge(s_brko, H * 16)

                @block.scalar
                def _(act):
                    def col(v):
                        return v.rearrange("(d a) -> d a", a=1)

                    def row(v):
                        return v.rearrange("(a d) -> a d", a=1)

                    loads = [(W1_l[:], W1), (W2_l[:], W2), (Wq_s[:], Wq), (Wk_s[:], Wk), (Wv_s[:], Wv),
                             (Wskip_s[:], Wskip), (Wf1_s[:], Wf1), (Wf2_s[:], Wf2.rearrange("(t f) d -> f t d", t=T)),
                             (We_s[0:DE, 0, :], We), (We_s[0:DE, 1, :], We),
                             (We_s[DE:DE + 1, 0, :], row(bk)), (We_s[DE:DE + 1, 1, :], row(bv)),
                             (bias[:, 0, :], row(b2)), (bias[:, 1, :], row(bq)), (bias[:, 2, :], row(bskip)),
                             (bias[:, 3, :], row(bf2)), (bias[:, 4, :], row(b1)),
                             (g1_col[:], col(g1)), (b1_col[:], col(b1)), (gamma_col[:], col(gamma)),
                             (beta_col[:], col(beta)), (eps1[:], row(eps).to_broadcast([P, 1]))]
                    for t in range(T):
                        loads.append((bf1_col[:, t:t + 1], col(bf1[t * D:(t + 1) * D])))
                        loads.append((g1_row[:, t, :], row(g1).to_broadcast([P, D])))
                        loads.append((g2_row[:, t, :], row(g2).to_broadcast([P, D])))
                        loads.append((b2n_row[:, t, :], row(b2n).to_broadcast([P, D])))
                    with nc.allow_non_contiguous_dma(reason="vectors of 128, once"):
                        for n, (to, frm) in enumerate(loads):
                            act.dma_start(to, frm).then_inc(s_w, 16)
                            if n % 6 == 5 and n // 6 < Z_FIRST:
                                act.wait_ge(s_zset, 1)
                                zero_part(act, n // 6)
                    for z in range(len(loads) // 6, Z_FIRST):
                        zero_part(act, z)
                    act.wait_ge(s_w, 16 * 38)

                @block.gpsimd
                def _(pool):
                    pool.memset(ident[:], 0.0).then_inc(s_id0, 1)
                    pool.memset(head_of[:], 1.0).then_inc(s_ho, 1)
                    pool.wait_ge(s_id0, 1)
                    pool.affine_select(out=ident[:], in_=ident[:], compare_op=ALU.not_equal, fill=1.0, base=0,
                                       pattern=[[-1, P]], channel_multiplier=1).then_inc(s_id, 1)
                    pool.wait_ge(s_ho, 1)
                    pool.affine_select(out=head_of[:], in_=head_of[:], compare_op=ALU.is_ge, fill=0.0, base=0,
                                       pattern=[[1, D]], channel_multiplier=-C).then_inc(s_ho, 1)
                    pool.wait_ge(s_ho, 2)
                    pool.affine_select(out=head_of[:], in_=head_of[:], compare_op=ALU.is_ge, fill=0.0, base=C - 1,
                                       pattern=[[-1, D]], channel_multiplier=C).then_inc(s_ho, 1)

                @block.vector
                def _(dve):
                    dve.memset(dst_i[:], PAD).then_inc(s_mem, 1)
                    dve.memset(next_i[:], PAD).then_inc(s_mem, 1)
                    dve.memset(src_i[:], 0).then_inc(s_mem, 1)
                    dve.memset(zeros[:], 0.0).then_inc(s_zset, 1)
                    dve.memset(onesB[:], 1.0)
                    dve.memset(half[:], -0.5)
                    dve.memset(root_d[:], float(D) ** 0.5)
                    dve.memset(brk[:], LOW).then_inc(s_mem, 1)
                    dve.wait_ge(s_idx, (6 if tail else 3) * 16)
                    for to, frm in ((dst_f, dst_i), (next_f, next_i), (src_f, src_i)):
                        dve.tensor_copy(to[:].rearrange("b t e -> b (t e)"), frm[:]).then_inc(s_f, 1)
                    dve.wait_ge(s_f, 3)
                    dve.tensor_tensor(eq[:], dst_f[:], next_f[:], ALU.is_equal).then_inc(s_eq, 1)
                    dve.wait_ge(s_eq, 1)
                    dve.scalar_tensor_tensor(out=row_f[:], in0=eq[:], scalar=float(SKIP), in1=dst_f[:],
                                             op0=ALU.mult, op1=ALU.add).then_inc(s_eq, 1)
                    dve.wait_ge(s_eq, 2)
                    for n, e in enumerate((0, P - 1)):
                        dve.tensor_tensor(eq[:], dst_f[:], dst_f[:, :, e:e + 1].to_broadcast([NB, T, P]),
                                          ALU.is_equal).then_inc(s_eq, 1)
                        dve.wait_ge(s_eq, 3 + 2 * n)
                        dve.scalar_tensor_tensor(out=row_f[:], in0=eq[:], scalar=float(SKIP), in1=row_f[:],
                                                 op0=ALU.mult, op1=ALU.add).then_inc(s_eq, 1)
                        dve.wait_ge(s_eq, 4 + 2 * n)
                    dve.tensor_tensor(eq[:, :, 0:P - 1], dst_f[:, :, 1:P], dst_f[:, :, 0:P - 1],
                                      ALU.is_equal).then_inc(s_eq, 1)
                    dve.wait_ge(s_eq, 7)
                    dve.wait_ge(s_mem, 4)
                    dve.tensor_scalar(brk[:, :, 1:P], eq[:, :, 0:P - 1], -1.0, -LOW, ALU.add, ALU.mult)\
                       .then_inc(s_brk, 1)
                    dve.tensor_copy(ends[:], dst_f[:, :, 0:P:P - 1]).then_inc(s_ends, 1)
                    dve.wait_ge(s_keyb, 16)
                    dve.memset(same_item[:], 0.0).then_inc(s_item, 1)
                    dve.memset(count_item[:], 1.0).then_inc(s_item, 1)
                    dve.wait_ge(s_item, 1)
                    dve.tensor_tensor(same_item[:, 1:NI], key_b[:, 1:NI], key_b[:, 0:NI - 1], ALU.is_equal)\
                       .then_inc(s_item, 1)
                    dve.wait_ge(s_item, 3)
                    dve.tensor_scalar(count_item[:, 1:NI:2], same_item[:, 1:NI:2], -1.0, 1.0, ALU.mult, ALU.add)\
                       .then_inc(s_item, 1)
                    dve.tensor_copy(key_skip[0:1, NI - 1:NI], key_b[0:1, NI - 1:NI]).then_inc(s_v, 1)
                    dve.scalar_tensor_tensor(out=key_skip[0:1, 0:NI - 1], in0=same_item[0:1, 1:NI],
                                             scalar=float(SKIP), in1=key_b[0:1, 0:NI - 1],
                                             op0=ALU.mult, op1=ALU.add).then_inc(s_item, 1)
                    dve.wait_ge(s_item, 5)
                    dve.wait_ge(s_v, 1)
                    dve.tensor_copy(key_skip_i[:], key_skip[:]).then_inc(s_item, 1)
                    dve.wait_ge(s_w, 16 * 38)
                    dve.tensor_scalar(eps1[:], eps1[:], 1.0, None, ALU.add).then_inc(s_v, 1)
                    dve.tensor_tensor(bias[:, 3, :], bias[:, 3, :], bias[:, 4, :], ALU.add).then_inc(s_bp, 1)
                    dve.wait_ge(s_bp, 1)
                    left = bias[:, 0:4, :]
                    for r in range(3):
                        for t in range(T):
                            last = dve.tensor_copy(part_b[:, :, r, t, :], left)
                        last.then_inc(s_bp, 1)
                        if r < 2:
                            dve.wait_ge(s_bp, 2 + 2 * r)
                            dve.tensor_tensor(rest[:], left, part_b[:, :, r, 0, :], ALU.subtract).then_inc(s_bp, 1)
                            dve.wait_ge(s_bp, 3 + 2 * r)
                            left = rest[:]
                    dve.wait_ge(s_id, 1)
                    dve.tensor_tensor(Wskip_s[:], Wskip_s[:], ident[:], ALU.add).then_inc(s_v, 1)
                    for n in range(3):
                        dve.wait_ge(s_turn, n + 1)
                        for t in range(T):
                            last = dve.tensor_copy(idx_cols[:, :, (1, 0, 2)[n], t], turn[:, n, t * P:t * P + NB])
                            if n == 0:
                                last = dve.tensor_copy(dst_cols[:, :, t], turn[:, n, t * P:t * P + NB])
                        last.then_inc(s_col, 1)
                    dve.wait_ge(s_turn, 4)
                    dve.tensor_copy(W1T[:], turn[:, 3, 0:D])
                    dve.tensor_copy(W2T[:], turn[:, 3, D:2 * D]).then_inc(s_col, 1)

                @block.tensor
                def _(pe):
                    pe.wait_ge(s_id, 1)
                    pe.wait_ge(s_eq, 6)
                    for n, table in enumerate((dst_f, src_f, row_f)):
                        for t in range(T):
                            mm = pe.transpose(turn[:, n, t * P:t * P + NB], table[:, t, :], ident[0:NB, 0:NB])
                        mm.then_inc(s_turn, 1)
                    pe.wait_ge(s_w, 16 * 38)
                    pe.transpose(turn[:, 3, 0:D], W1_l[:], ident[:])
                    pe.transpose(turn[:, 3, D:2 * D], W2_l[:], ident[:]).then_inc(s_turn, 1)

        clear()
        edges0_early(nc, sem, NE, x, agg, rows_side[0], ident, idx_cols, dst_cols, N, zero_part, Z_FIRST, NZ, s_zero)
        edges0(nc, sem, NE, NB - NE, x, agg, rows_side[0], ident, idx_cols, dst_cols, N)
        joins0(nc, sem, NI, CI, PI, rows_side[0], agg, ident, same_item, count_item, row_item, N)
        part_sems.clear()
        stats(nc, sem, NG, N, group, geometry, x, agg, eps1, half, W1T, gamma_col, beta_col, bn_scale, bn_shift,
              ident)
        clear()
        nodes0(nc, sem, NG, group, geometry, x, agg, x1, eps1, half, root_d, ident, W1T, W2T,
               bn_scale, bn_shift, onesB, b2_3)
        clear()
        edges1(nc, sem, NB, E_LAST, N, x1, agg, edge_attr, rows_side[1], soft_side, breaks, ident, idx_cols, dst_cols,
               Wq_s, Wk_s, Wv_s, We_s, onesB, bq_3, NG, group, geometry, skipped, Wskip_s, bskip_3)
        joins1(nc, sem, NI, CI, PI, rows_side[1], soft_side, agg, ident, same_item, count_item, row_item, head_of, N)
        nodes1(nc, sem, NG, group, geometry, x1, skipped, agg, out, half, root_d, ident, Wf1_s, Wf2_s, onesB, bf2_3,
               g1_col, b1_col, bf1_col, g1_row, g2_row, b2n_row)


def scatter_rows(pool, dram, index, rows, last_row):
    return pool.indirect_dma_start(dram, bass.IndirectOffsetOnAxis(index, 0), rows, None,
                                   bounds_check=last_row, oob_is_err=False)


def gather_rows(pool, rows, dram, index, last_row):
    return pool.indirect_dma_start(rows, None, dram, bass.IndirectOffsetOnAxis(index, 0), bounds_check=last_row)


def prepare_batch(dve, i, u, idx, dst_f, idx_cols, dst_cols, idx_ready, dstf_ready):
    dve.tensor_copy(idx[:, u], idx_cols[:, bass.ds(i, 1)].rearrange("p b k t -> p (b k) t")).then_inc(idx_ready, 1)
    dve.tensor_copy(dst_f[:, u], dst_cols[:, bass.ds(i, 1)].rearrange("p b t -> p (b t)")).then_inc(dstf_ready, 1)


def flat(bank):
    return bank[:].rearrange("p t d -> p (t d)")


def side_rows(side, i, end):
    view = side.rearrange("(b t e) d -> b t e d", t=T, e=2)
    return view[bass.ds(i, 1), :, end, :]


def edges0_early(nc, sem, NE, x, agg, side, ident, idx_cols, dst_cols, N, zero_part, z_first, NZ, s_zero):
    with ExitStack() as part:
        def sb(name, shape, dt=F32):
            return part.enter_context(nc.sbuf_tensor(name, shape, dt))

        rows = sb("ea_rows", [P, S, T, D])
        same = sb("ea_same", [P, S, T, P])
        sums = sb("ea_sums", [P, NE, T, D])
        spread = part.enter_context(nc.psum_tensor("ea_spread", [P, 2, T, P], F32))
        total = part.enter_context(nc.psum_tensor("ea_total", [P, 2, T, D], F32))

        spread_ready, same_ready = sem("ea_spread_ready"), sem("ea_same_ready")
        total_ready, sums_ready = sem("ea_total_ready"), sem("ea_sums_ready")
        gathered = [sem(f"ea_gathered{s}") for s in range(S)]
        scattered = [sem(f"ea_scattered{s}") for s in range(S)]
        sided = [sem(f"ea_sided{s}") for s in range(S)]

        with nc.Block() as block:
            @block.gpsimd
            def _(pool):
                for i in range(NE):
                    if i >= S:
                        pool.wait_ge(total_ready, i - S + 1)
                    for t in range(T):
                        gather_rows(pool, rows[:, i % S, t, :], x, idx_cols[:, i, 0, t:t + 1].bitcast(U32), N - 1)\
                            .then_inc(gathered[i % S], 16)
                for n in range(3):
                    pool.wait_ge(s_zero[n], len(range(n, NZ, 3)) * 16)
                for i in range(NE):
                    pool.wait_ge(sums_ready, i + 1)
                    if i >= S:
                        pool.wait_ge(scattered[i % S], i // S * T * 16)
                    for t in range(T):
                        scatter_rows(pool, agg, idx_cols[:, i, 2, t:t + 1].bitcast(U32), sums[:, i, t, :], N - 1)\
                            .then_inc(scattered[i % S], 16)
                for s in range(min(S, NE)):
                    pool.wait_ge(scattered[s], len(range(s, NE, S)) * T * 16)

            @block.sync
            def _(sp):
                for z in range(z_first, NZ):
                    zero_part(sp, z)
                for i in range(NE):
                    sp.wait_ge(sums_ready, i + 1)
                    if i >= S:
                        sp.wait_ge(sided[i % S], i // S * 32)
                    for end, p in enumerate((0, P - 1)):
                        sp.dma_start(side_rows(side, i, end), sums[p:p + 1, i]).then_inc(sided[i % S], 16)
                for s in range(min(S, NE)):
                    sp.wait_ge(sided[s], len(range(s, NE, S)) * 32)

            @block.vector
            def _(dve):
                for i in range(NE):
                    dve.wait_ge(spread_ready, i + 1)
                    if i >= S:
                        dve.wait_ge(total_ready, i - S + 1)
                    dve.tensor_tensor(same[:, i % S], spread[:, i % 2],
                                      dst_cols[:, i].unsqueeze(2).to_broadcast([P, T, P]), ALU.is_equal)\
                       .then_inc(same_ready, 1)

            @block.tensor
            def _(pe):
                for i in range(NE + 1):
                    if i < NE:
                        if i >= 2:
                            pe.wait_ge(same_ready, i - 1)
                        for t in range(T):
                            mm = pe.transpose(spread[:, i % 2, t, :], dst_cols[:, i, t:t + 1].to_broadcast([P, P]),
                                              ident[:])
                        mm.then_inc(spread_ready, 1)
                    if i >= 1:
                        b = i - 1
                        pe.wait_ge(same_ready, b + 1)
                        pe.wait_ge(gathered[b % S], (b // S + 1) * T * 16)
                        if b >= 2:
                            pe.wait_ge(sums_ready, b - 1)
                        for t in range(T):
                            mm = pe.matmul(total[:, b % 2, t, :], same[:, b % S, t, :], rows[:, b % S, t, :],
                                           start=True, stop=True)
                        mm.then_inc(total_ready, 1)

            @block.scalar
            def _(act):
                for i in range(NE):
                    act.wait_ge(total_ready, i + 1)
                    act.activation(sums[:, i], total[:, i % 2], ACT.Copy).then_inc(sums_ready, 1)


def edges0(nc, sem, first, NB, x, agg, side, ident, idx_cols, dst_cols, N):
    with ExitStack() as part:
        def sb(name, shape, dt=F32):
            return part.enter_context(nc.sbuf_tensor(name, shape, dt))

        idx = sb("e0_idx", [P, U, 3, T], I32)
        dst_f = sb("e0_dst_f", [P, U, T])
        rows = sb("e0_rows", [P, S, T, D])
        same = sb("e0_same", [P, S, T, P])
        sums = sb("e0_sums", [P, S, T, D])
        spread = part.enter_context(nc.psum_tensor("e0_spread", [P, 2, T, P], F32))
        total = part.enter_context(nc.psum_tensor("e0_total", [P, 2, T, D], F32))

        idx_ready, dstf_ready = sem("e0_idx_ready"), sem("e0_dstf_ready")
        spread_ready, same_ready = sem("e0_spread_ready"), sem("e0_same_ready")
        total_ready, sums_ready = sem("e0_total_ready"), sem("e0_sums_ready")
        begun = sem("e0_begun")
        gathered = [sem(f"e0_gathered{s}") for s in range(S)]
        scattered = [sem(f"e0_scattered{s}") for s in range(S)]
        sided = [sem(f"e0_sided{s}") for s in range(S)]

        with nc.Block() as block:
            @block.vector
            def _(dve):
                dve.memset(dst_f[:], 0.0).then_inc(begun, 1)
                dve.wait_ge(begun, 1)

                def body(j, u):
                    i = j * U + u
                    if works(i, NB):
                        if late(j):
                            r, s = turn_of(j, u)
                            dve.wait_ge(scattered[s], (r - 1) * T * 16)
                        prepare_batch(dve, first + i, u, idx, dst_f, idx_cols, dst_cols, idx_ready, dstf_ready)
                    jb, ub, ib = back(j, u, 1)
                    if works(ib, NB):
                        dve.wait_ge(spread_ready, ib + 1)
                        dve.wait_ge(dstf_ready, ib + 1)
                        r, s = turn_of(jb, ub)
                        if late(r):
                            dve.wait_ge(total_ready, ib - S + 1)
                        dve.tensor_tensor(same[:, s], spread[:, ub % 2],
                                          dst_f[:, ub].unsqueeze(2).to_broadcast([P, T, P]),
                                          ALU.is_equal).then_inc(same_ready, 1)

                walk(dve, NB, 1, body)

            @block.tensor
            def _(pe):
                def body(j, u):
                    i = j * U + u
                    if works(i, NB):
                        pe.wait_ge(dstf_ready, i + 1)
                        if not isinstance(i, int) or i >= 2:
                            pe.wait_ge(same_ready, i - 1)
                        for t in range(T):
                            mm = pe.transpose(spread[:, u % 2, t, :], dst_f[:, u, t:t + 1].to_broadcast([P, P]),
                                              ident[:])
                        mm.then_inc(spread_ready, 1)
                    jb, ub, ib = back(j, u, 2)
                    if works(ib, NB):
                        pe.wait_ge(same_ready, ib + 1)
                        r, s = turn_of(jb, ub)
                        pe.wait_ge(gathered[s], (r + 1) * T * 16)
                        if not isinstance(ib, int) or ib >= 2:
                            pe.wait_ge(sums_ready, ib - 1)
                        for t in range(T):
                            mm = pe.matmul(total[:, ub % 2, t, :], same[:, s, t, :], rows[:, s, t, :],
                                           start=True, stop=True)
                        mm.then_inc(total_ready, 1)

                walk(pe, NB, 2, body)

            @block.scalar
            def _(act):
                def body(j, u):
                    i = j * U + u
                    act.wait_ge(total_ready, i + 1)
                    r, s = turn_of(j, u)
                    if late(r):
                        act.wait_ge(scattered[s], r * T * 16)
                        act.wait_ge(sided[s], r * 32)
                    act.activation(sums[:, s], total[:, u % 2], ACT.Copy).then_inc(sums_ready, 1)

                walk(act, NB, 0, body)

            @block.gpsimd
            def _(pool):
                last_row = pool.to_reg(N - 1)

                def body(j, u):
                    i = j * U + u
                    if works(i, NB):
                        now, free = ready_values(pool, i + 1, i - S + 1)
                        r, s = turn_of(j, u)
                        pool.wait_ge(begun, 1)
                        pool.wait_ge(idx_ready, now)
                        if late(r):
                            pool.wait_ge(total_ready, free)
                        for t in range(T):
                            gather_rows(pool, rows[:, s, t, :], x, idx[:, u, 0, t:t + 1].bitcast(U32), last_row)\
                                .then_inc(gathered[s], 16)
                    jb, ub, ib = back(j, u, 3)
                    if works(ib, NB):
                        (now,) = ready_values(pool, ib + 1)
                        pool.wait_ge(begun, 1)
                        pool.wait_ge(sums_ready, now)
                        s = ub % S
                        for t in range(T):
                            scatter_rows(pool, agg, idx[:, ub, 2, t:t + 1].bitcast(U32), sums[:, s, t, :], last_row)\
                                .then_inc(scattered[s], 16)

                walk(pool, NB, 3, body)
                for s in range(S):
                    pool.wait_ge(scattered[s], len(range(s, NB, S)) * T * 16)

            @block.sync
            def _(sp):
                def body(j, u):
                    i = j * U + u
                    sp.wait_ge(sums_ready, i + 1)
                    for end, p in enumerate((0, P - 1)):
                        sp.dma_start(side_rows(side, first + i, end), sums[p:p + 1, u % S]).then_inc(sided[u % S], 16)

                walk(sp, NB, 0, body)
                for s in range(S):
                    sp.wait_ge(sided[s], len(range(s, NB, S)) * 32)


def joins0(nc, sem, NI, CI, PI, side, agg, ident, same_item, count_item, row_item, N):
    with ExitStack() as part:
        items = part.enter_context(nc.sbuf_tensor("j0_items", [PI, CI, D], F32))
        flat = part.enter_context(nc.sbuf_tensor("j0_flat", [D, NI], F32))
        run = part.enter_context(nc.sbuf_tensor("j0_run", [D, NI], F32))
        turn = part.enter_context(nc.psum_tensor("j0_turn", [P, CI, P], F32))
        s_in, s_turn, s_flat = sem("j0_in"), sem("j0_turned"), sem("j0_flat_steps")
        s_back, s_rows, s_out = sem("j0_turned_back"), sem("j0_rows"), sem("j0_out")

        with nc.Block() as block:
            @block.sync
            def _(sp):
                sp.dma_start(items[:], side.rearrange("(c p) d -> p c d", p=PI)).then_inc(s_in, 16)

            @block.tensor
            def _(pe):
                pe.wait_ge(s_in, 16)
                for c in range(CI):
                    mm = pe.transpose(turn[:, c, 0:PI], items[:, c, :], ident[0:PI, 0:PI])
                mm.then_inc(s_turn, 1)
                pe.wait_ge(s_flat, 2)
                for c in range(CI):
                    mm = pe.transpose(turn[0:PI, c, :], run[:, c * PI:(c + 1) * PI], ident[:])
                mm.then_inc(s_back, 1)

            @block.vector
            def _(dve):
                dve.wait_ge(s_turn, 1)
                dve.tensor_tensor(flat[:].rearrange("d (c p) -> d c p", p=PI), turn[:, :, 0:PI],
                                  count_item[:].rearrange("d (c p) -> d c p", p=PI), ALU.mult).then_inc(s_flat, 1)
                dve.wait_ge(s_flat, 1)
                dve.tensor_tensor_scan(run[:], same_item[:], flat[:], 0.0, ALU.mult, ALU.add).then_inc(s_flat, 1)
                dve.wait_ge(s_back, 1)
                dve.tensor_copy(items[:], turn[0:PI]).then_inc(s_rows, 1)

            @block.gpsimd
            def _(pool):
                pool.wait_ge(s_rows, 1)
                for c in range(CI):
                    scatter_rows(pool, agg, row_item[:, c:c + 1].bitcast(U32), items[:, c, :], N - 1)\
                        .then_inc(s_out, 16)
                pool.wait_ge(s_out, CI * 16)


def stats(nc, sem, NG, N, group, geometry, x, agg, eps1, half, W1T, gamma_col, beta_col, bn_scale, bn_shift,
          ident):
    with ExitStack() as part:
        def sb(name, shape, dt=F32):
            return part.enter_context(nc.sbuf_tensor(name, shape, dt))

        xs = sb("st_x", [P, U, T, D])
        ags = sb("st_agg", [P, U, T, D])
        h = sb("st_h", [P, U, T, D + 1])
        gram = sb("st_gram", [D, D + 1])
        mean = sb("st_mean", [D, 1])
        mean_row = sb("st_mean_row", [1, D])
        cov = sb("st_cov", [D, D])
        prod = sb("st_prod", [D, D])
        ones = sb("st_ones", [P, 1])
        small = sb("st_small", [D, 4])
        G = part.enter_context(nc.psum_tensor("st_G", [D, 512], F32))
        M = part.enter_context(nc.psum_tensor("st_M", [D, 4, 512], F32))
        M_row = part.enter_context(nc.psum_tensor("st_row", [1, 512], F32))

        rows_in = [sem(f"st_rows_in{u}") for u in range(U)]
        h_ready, h_used, ones_set = sem("st_h_ready"), sem("st_h_used"), sem("st_ones_set")
        fin_d, fin_p, fin_g = sem("st_vector_steps"), sem("st_product_steps"), sem("st_pool_steps")

        with nc.Block() as block:
            @block.sync
            def _(sp):
                def body(j, u):
                    g = j * U + u
                    p, t = geometry(g)
                    if late(j):
                        sp.wait_ge(h_ready, g - U + 1)
                    sp.dma_start(xs[0:p, u, 0:t], group(x, g)).then_inc(rows_in[u], 16)
                    sp.dma_start(ags[0:p, u, 0:t], group(agg, g)).then_inc(rows_in[u], 16)

                walk(sp, NG, 0, body)

            @block.vector
            def _(dve):
                dve.memset(ones[:], 1.0).then_inc(ones_set, 1)
                dve.memset(h[:, :, :, D:D + 1], 1.0).then_inc(ones_set, 1)
                dve.wait_ge(ones_set, 2)

                def body(j, u):
                    g = j * U + u
                    p, t = geometry(g)
                    dve.wait_ge(rows_in[u], (j + 1) * 32)
                    if late(j):
                        dve.wait_ge(h_used, g - U + 1)
                    dve.scalar_tensor_tensor(out=h[0:p, u, 0:t, 0:D], in0=xs[0:p, u, 0:t], scalar=eps1[0:p],
                                             in1=ags[0:p, u, 0:t], op0=ALU.mult, op1=ALU.add).then_inc(h_ready, 1)

                walk(dve, NG, 0, body)
                dve.wait_ge(h_used, NG)
                dve.tensor_scalar(gram[:], G[:, 0:D + 1], 1.0 / N, None, ALU.mult).then_inc(fin_d, 1)
                dve.wait_ge(fin_p, 1)
                dve.tensor_copy(mean_row[:], M_row[0:1, 0:D]).then_inc(fin_d, 1)
                dve.wait_ge(fin_p, 2)
                dve.tensor_tensor(cov[:], gram[:, 0:D], M[:, 0, 0:D], ALU.subtract).then_inc(fin_d, 1)
                dve.wait_ge(fin_p, 3)
                dve.tensor_tensor(prod[:], M[:, 1, 0:D], W1T[:], ALU.mult).then_inc(fin_d, 1)
                dve.wait_ge(fin_p, 5)
                dve.tensor_scalar(small[:, 0:1], M[:, 2, 0:1], 0.0, BN_EPS, ALU.max, ALU.add).then_inc(fin_d, 1)
                dve.wait_ge(fin_g, 1)
                dve.tensor_tensor(bn_scale[:], small[:, 1:2], gamma_col[:], ALU.mult).then_inc(fin_d, 1)
                dve.wait_ge(fin_d, 6)
                dve.tensor_tensor(small[:, 2:3], M[:, 3, 0:1], bn_scale[:], ALU.mult).then_inc(fin_d, 1)
                dve.wait_ge(fin_d, 7)
                dve.tensor_tensor(bn_shift[:], beta_col[:], small[:, 2:3], ALU.subtract).then_inc(fin_d, 1)

            @block.gpsimd
            def _(pool):
                pool.wait_ge(fin_d, 5)
                pool.tensor_tensor(small[:, 1:2], small[:, 0:1], half[:, 0:1], ALU.pow).then_inc(fin_g, 1)

            @block.tensor
            def _(pe):
                def body(j, u):
                    g = j * U + u
                    p, t = geometry(g)
                    pe.wait_ge(h_ready, g + 1)
                    for c in range(t):
                        first = isinstance(g, int) and g == 0 and c == 0
                        last = isinstance(g, int) and g == NG - 1 and c == t - 1
                        mm = pe.matmul(G[:, 0:D + 1], h[0:p, u, c, 0:D], h[0:p, u, c, :], start=first, stop=last)
                    mm.then_inc(h_used, 1)

                walk(pe, NG, 0, body)
                pe.wait_ge(fin_d, 1)
                pe.transpose(M_row[0:1, 0:D], gram[:, D:D + 1], ident[:]).then_inc(fin_p, 1)
                pe.wait_ge(fin_d, 2)
                pe.matmul(M[:, 0, 0:D], mean_row[:], mean_row[:], start=True, stop=True).then_inc(fin_p, 1)
                pe.wait_ge(fin_d, 3)
                pe.matmul(M[:, 1, 0:D], cov[:], W1T[:], start=True, stop=True).then_inc(fin_p, 1)
                pe.matmul(M[:, 3, 0:1], W1T[:], gram[:, D:D + 1], start=True, stop=True).then_inc(fin_p, 1)
                pe.wait_ge(fin_d, 4)
                pe.matmul(M[:, 2, 0:1], prod[:], ones[:], start=True, stop=True).then_inc(fin_p, 1)


class Norm:

    def __init__(self, part, nc, sem, name):
        def sb(what, last):
            return part.enter_context(nc.sbuf_tensor(f"{name}_{what}", [P, U, T] + last, F32))

        self.stat, self.both = sb("stat", [6]), sb("both", [2])
        self.gap, self.gap2, self.spread = sb("gap", []), sb("gap2", []), sb("spread", [])
        self.root, self.mean, self.rstd = sb("root", []), sb("mean", []), sb("rstd", [])
        self.shift = sb("shift", [])
        self.scaled, self.scaled_ready = part.enter_context(nc.sbuf_tensor(f"{name}_scaled", [P, U, D], F32)), sem(f"{name}_scaled_ready")
        self.stat_ready, self.both_ready = sem(f"{name}_stat_ready"), sem(f"{name}_both_ready")
        self.gap_ready, self.spread_ready = sem(f"{name}_gap_ready"), sem(f"{name}_spread_ready")
        self.root_ready, self.rstd_ready = sem(f"{name}_root_ready"), sem(f"{name}_rstd_ready")
        self.mean_ready, self.shift_ready = sem(f"{name}_mean_ready"), sem(f"{name}_shift_ready")


def norm_stats(dve, n, y, p, rows, u):
    for c in rows:
        last = dve.bn_stats(n.stat[0:p, u, c, :], y[0:p, c, :])
    last.then_inc(n.stat_ready, 1)


def norm_sums(dve, n, p, t, u, g):
    s = n.stat[0:p, u, 0:t]
    dve.wait_ge(n.stat_ready, 2 * g + 2)
    dve.tensor_tensor(n.gap[0:p, u, 0:t], s[:, :, 1], s[:, :, 4], ALU.subtract).then_inc(n.gap_ready, 1)
    dve.tensor_tensor(n.both[0:p, u, 0:t], s[:, :, 1:3], s[:, :, 4:6], ALU.add).then_inc(n.both_ready, 1)


def norm_gap2(dve, n, p, t, u, g):
    dve.wait_ge(n.gap_ready, 2 * g + 1)
    dve.scalar_tensor_tensor(out=n.gap2[0:p, u, 0:t], in0=n.gap[0:p, u, 0:t], scalar=D / 4.0,
                             in1=n.gap[0:p, u, 0:t], op0=ALU.mult, op1=ALU.mult).then_inc(n.gap_ready, 1)


def norm_spread(dve, n, p, t, u, g):
    dve.wait_ge(n.gap_ready, 2 * g + 2)
    dve.wait_ge(n.both_ready, g + 1)
    dve.scalar_tensor_tensor(out=n.spread[0:p, u, 0:t], in0=n.both[0:p, u, 0:t, 1], scalar=D * LN_EPS,
                             in1=n.gap2[0:p, u, 0:t], op0=ALU.add, op1=ALU.add).then_inc(n.spread_ready, 1)


def norm_root(pool, n, p, t, u, g, half, root_d):
    pool.wait_ge(n.spread_ready, g + 1)
    pool.tensor_tensor(n.root[0:p, u, 0:t], n.spread[0:p, u, 0:t], half[0:p, 0:t], ALU.pow)\
        .then_inc(n.root_ready, 1)
    pool.wait_ge(n.both_ready, g + 1)
    pool.tensor_tensor(n.mean[0:p, u, 0:t], n.both[0:p, u, 0:t, 0], half[0:p, 0:t], ALU.mult)\
        .then_inc(n.mean_ready, 1)
    pool.wait_ge(n.root_ready, g + 1)
    pool.tensor_tensor(n.rstd[0:p, u, 0:t], n.root[0:p, u, 0:t], root_d[0:p, 0:t], ALU.mult)\
        .then_inc(n.rstd_ready, 1)


def norm_shift(pool, n, p, t, u, g):
    pool.wait_ge(n.rstd_ready, g + 1)
    pool.wait_ge(n.mean_ready, g + 1)
    pool.tensor_tensor(n.shift[0:p, u, 0:t], n.mean[0:p, u, 0:t], n.rstd[0:p, u, 0:t], ALU.mult)\
        .then_inc(n.shift_ready, 1)


def norm_apply_act(act, n, to, y, p, t, u, g, ready):
    act.wait_ge(n.shift_ready, g + 1)
    for c in range(t - 1):
        last = act.activation(to[0:p, c, :], y[0:p, c, :], ACT.Identity, bias=n.shift[0:p, u, c:c + 1],
                              scale=n.rstd[0:p, u, c:c + 1])
    last.then_inc(ready, 1)


class Norms:

    def __init__(self, part, nc, sem, name, kinds):
        def sb(what, last):
            return part.enter_context(nc.sbuf_tensor(f"{name}_{what}", [P, U, kinds, T] + last, F32))

        self.kinds = kinds
        self.stat, self.both = sb("stat", [6]), sb("both", [2])
        self.gap, self.gap2, self.spread = sb("gap", []), sb("gap2", []), sb("spread", [])
        self.root, self.mean, self.rstd, self.shift = sb("root", []), sb("mean", []), sb("rstd", []), sb("shift", [])
        self.set, self.stat_ready, self.gap_ready = sem(f"{name}_set"), sem(f"{name}_stat_ready"), sem(f"{name}_gap_ready")
        self.spread_ready, self.root_ready, self.ready = sem(f"{name}_spread_ready"), sem(f"{name}_root_ready"), sem(f"{name}_ready")
        self.rstd_ready = sem(f"{name}_rstd_ready")


def norms_stat(dve, n, kind, y, p, t, u):
    for c in range(t):
        last = dve.bn_stats(n.stat[0:p, u, kind, c, :], y[0:p, c, :])
    last.then_inc(n.stat_ready, 1)


def norms_spread(dve, n, u, k, stats):
    s = n.stat[:, u]
    dve.wait_ge(n.stat_ready, stats)
    dve.tensor_tensor(n.gap[:, u], s[:, :, :, 1], s[:, :, :, 4], ALU.subtract).then_inc(n.gap_ready, 1)
    dve.tensor_tensor(n.both[:, u], s[:, :, :, 1:3], s[:, :, :, 4:6], ALU.add).then_inc(n.gap_ready, 1)
    dve.wait_ge(n.gap_ready, 3 * k + 1)
    dve.scalar_tensor_tensor(out=n.gap2[:, u], in0=n.gap[:, u], scalar=D / 4.0, in1=n.gap[:, u],
                             op0=ALU.mult, op1=ALU.mult).then_inc(n.gap_ready, 1)
    dve.wait_ge(n.gap_ready, 3 * k + 3)
    dve.scalar_tensor_tensor(out=n.spread[:, u], in0=n.both[:, u, :, :, 1], scalar=D * LN_EPS, in1=n.gap2[:, u],
                             op0=ALU.add, op1=ALU.add).then_inc(n.spread_ready, 1)


def norms_root(pool, n, u, k, half, root_d):
    def by_kind(v):
        return v[:].rearrange("p (k t) -> p k t", t=T)

    pool.wait_ge(n.spread_ready, k + 1)
    pool.tensor_tensor(n.root[:, u], n.spread[:, u], by_kind(half), ALU.pow).then_inc(n.root_ready, 1)
    pool.tensor_tensor(n.mean[:, u], n.both[:, u, :, :, 0], by_kind(half), ALU.mult).then_inc(n.root_ready, 1)
    pool.wait_ge(n.root_ready, 2 * k + 1)
    pool.tensor_tensor(n.rstd[:, u], n.root[:, u], by_kind(root_d), ALU.mult).then_inc(n.rstd_ready, 1)
    pool.wait_ge(n.rstd_ready, k + 1)
    pool.wait_ge(n.root_ready, 2 * k + 2)
    pool.tensor_tensor(n.shift[:, u], n.mean[:, u], n.rstd[:, u], ALU.mult).then_inc(n.ready, 1)


def norms_apply_act(act, n, kind, to, y, p, t, j, u, ready):
    jb, ub, k = back(j, u, 1)
    act.wait_ge(n.ready, k + 1)
    for c in range(t):
        last = act.activation(to[0:p, c, :], y[0:p, c, :], ACT.Identity, bias=n.shift[0:p, ub, kind, c:c + 1],
                              scale=n.rstd[0:p, ub, kind, c:c + 1])
    last.then_inc(ready, 1)


def norm_scale_last(pool, n, y, p, t, u):
    pool.tensor_tensor(n.scaled[0:p, u], y[0:p, t - 1, :], n.rstd[0:p, u, t - 1:t].to_broadcast([p, D]), ALU.mult)\
        .then_inc(n.scaled_ready, 1)


def norm_shift_last(pool, n, to, p, t, u, g, ready):
    pool.wait_ge(n.scaled_ready, g + 1)
    pool.tensor_tensor(to[0:p, t - 1, :], n.scaled[0:p, u], n.shift[0:p, u, t - 1:t].to_broadcast([p, D]), ALU.add)\
        .then_inc(ready, 1)


def nodes0(nc, sem, NG, group, geometry, x, agg, x1, eps1, half, root_d, ident, W1T, W2T, bn_scale, bn_shift,
           onesB, b2_3):
    with ExitStack() as part:
        def sb(name, shape, dt=F32):
            return part.enter_context(nc.sbuf_tensor(name, shape, dt))

        def ps(name):
            return part.enter_context(nc.psum_tensor(name, [P, 2, T * P], F32))

        xs = sb("n0_x", [P, U, T, D])
        ags = sb("n0_agg", [P, U, T, D])
        h = sb("n0_h", [P, S, T, D])
        hT = sb("n0_hT", [D, S, T * P])
        rT = sb("n0_rT", [D, S, T * P])
        y = sb("n0_y", [P, S, T, D])
        o = sb("n0_o", [P, S, T, D])
        turned, lin1, lin2 = ps("n0_turned"), ps("n0_lin1"), ps("n0_lin2")
        n1 = Norm(part, nc, sem, "n0_norm")

        rows_in = [sem(f"n0_rows_in{u}") for u in range(U)]
        x1_out = [sem(f"n0_x1_out{s}") for s in range(S)]
        h_ready, turned_ready, hT_ready = sem("n0_h_ready"), sem("n0_turned_ready"), sem("n0_hT_ready")
        lin1_ready, rT_ready, lin2_ready = sem("n0_lin1_ready"), sem("n0_rT_ready"), sem("n0_lin2_ready")
        y_ready, o_ready, o_last_ready = sem("n0_y_ready"), sem("n0_o_ready"), sem("n0_o_last_ready")

        with nc.Block() as block:
            @block.sync
            def _(sp):
                def body(j, u):
                    g = j * U + u
                    if works(g, NG):
                        p, t = geometry(g)
                        if late(j):
                            sp.wait_ge(y_ready, g - U + 1)
                        sp.dma_start(xs[0:p, u, 0:t], group(x, g)).then_inc(rows_in[u], 16)
                        sp.dma_start(ags[0:p, u, 0:t], group(agg, g)).then_inc(rows_in[u], 16)

                walk(sp, NG, 0, body)

            @block.vector
            def _(dve):
                def body(j, u):
                    g = j * U + u
                    jb, ub, gb = back(j, u, 4)
                    jc, uc, gc = back(j, u, 5)
                    if works(g, NG):
                        p, t = geometry(g)
                        r, s = turn_of(j, u)
                        dve.wait_ge(rows_in[u], (j + 1) * 32)
                        if late(r):
                            dve.wait_ge(turned_ready, g - S + 1)
                        dve.scalar_tensor_tensor(out=h[0:p, s, 0:t], in0=xs[0:p, u, 0:t], scalar=eps1[0:p],
                                                 in1=ags[0:p, u, 0:t], op0=ALU.mult, op1=ALU.add)\
                           .then_inc(h_ready, 1)
                    if works(gb, NG):
                        pb, tb = geometry(gb)
                        r, s = turn_of(jb, ub)
                        dve.wait_ge(lin2_ready, gb + 1)
                        if late(r):
                            dve.wait_ge(o_ready, gb - S + 1)
                            dve.wait_ge(o_last_ready, gb - S + 1)
                        dve.tensor_tensor(y[0:pb, s, 0:tb], lin2[0:pb, ub % 2, 0:tb * D].rearrange(
                            "p (t d) -> p t d", d=D), xs[0:pb, ub, 0:tb], ALU.add).then_inc(y_ready, 1)
                    if works(gc, NG):
                        pc, tc = geometry(gc)
                        norm_sums(dve, n1, pc, tc, uc, gc)
                    if works(gb, NG):
                        dve.wait_ge(y_ready, gb + 1)
                        norm_stats(dve, n1, y[:, s], pb, range(tb // 2), ub)
                    if works(gc, NG):
                        norm_gap2(dve, n1, pc, tc, uc, gc)
                    if works(gb, NG):
                        norm_stats(dve, n1, y[:, s], pb, range(tb // 2, tb), ub)
                    if works(gc, NG):
                        norm_spread(dve, n1, pc, tc, uc, gc)

                walk(dve, NG, 5, body)

            @block.gpsimd
            def _(pool):
                def body(j, u):
                    g = j * U + u
                    jb, ub, gb = back(j, u, 1)
                    if works(g, NG):
                        p, t = geometry(g)
                        norm_root(pool, n1, p, t, u, g, half, root_d)
                    if works(gb, NG):
                        pb, tb = geometry(gb)
                        r, s = turn_of(jb, ub)
                        pool.wait_ge(n1.shift_ready, gb + 1)
                        norm_scale_last(pool, n1, y[:, s], pb, tb, ub)
                    if works(g, NG):
                        norm_shift(pool, n1, p, t, u, g)
                    if works(gb, NG):
                        if late(r):
                            pool.wait_ge(x1_out[s], r * 16)
                        norm_shift_last(pool, n1, o[:, s], pb, tb, ub, gb, o_last_ready)

                walk(pool, NG, 1, body)

            @block.scalar
            def _(act):
                def body(j, u):
                    j, u, g = back(j, u, 1)
                    if works(g, NG):
                        p, t = geometry(g)
                        act.wait_ge(turned_ready, g + 1)
                        r, s = turn_of(j, u)
                        if late(r):
                            act.wait_ge(lin1_ready, g - S + 1)
                        act.activation(hT[:, s, 0:t * p], turned[:, u % 2, 0:t * p], ACT.Copy)\
                           .then_inc(hT_ready, 1)
                    jb, ub, gb = back(j, u, 5)
                    if works(gb, NG):
                        p, t = geometry(gb)
                        r, s = turn_of(jb, ub)
                        if late(r):
                            act.wait_ge(x1_out[s], r * 16)
                        norm_apply_act(act, n1, o[:, s], y[:, s], p, t, ub, gb, o_ready)
                    jb, ub, gb = back(j, u, 1)
                    if works(gb, NG):
                        p, t = geometry(gb)
                        act.wait_ge(lin1_ready, gb + 1)
                        r, s = turn_of(jb, ub)
                        if late(r):
                            act.wait_ge(lin2_ready, gb - S + 1)
                        act.activation(rT[:, s, 0:t * p], lin1[:, ub % 2, 0:t * p], ACT.Relu,
                                       bias=bn_shift[:], scale=bn_scale[:]).then_inc(rT_ready, 1)
                    jb, ub, gb = back(j, u, 6)
                    if works(gb, NG):
                        p, t = geometry(gb)
                        act.wait_ge(o_ready, gb + 1)
                        act.wait_ge(o_last_ready, gb + 1)
                        act.dma_start(group(x1, gb), o[0:p, ub % S, 0:t]).then_inc(x1_out[ub % S], 16)

                walk(act, NG, 7, body)
                for s in range(S):
                    act.wait_ge(x1_out[s], len(range(s, NG, S)) * 16)

            @block.tensor
            def _(pe):
                def body(j, u):
                    j, u, g = back(j, u, 1)
                    if works(g, NG):
                        p, t = geometry(g)
                        pe.wait_ge(h_ready, g + 1)
                        if not isinstance(g, int) or g >= 2:
                            pe.wait_ge(hT_ready, g - 1)
                        for c in range(t):
                            mm = pe.transpose(turned[:, u % 2, c * p:(c + 1) * p], h[0:p, u % S, c, :], ident[0:p, 0:p])
                        mm.then_inc(turned_ready, 1)
                    jb, ub, gb = back(j, u, 1)
                    if works(gb, NG):
                        p, t = geometry(gb)
                        pe.wait_ge(hT_ready, gb + 1)
                        if not isinstance(gb, int) or gb >= 2:
                            pe.wait_ge(rT_ready, gb - 1)
                        pe.matmul(lin1[:, ub % 2, 0:t * p], W1T[:], hT[:, ub % S, 0:t * p],
                                  start=True, stop=True).then_inc(lin1_ready, 1)
                    jb, ub, gb = back(j, u, 2)
                    if works(gb, NG):
                        p, t = geometry(gb)
                        pe.wait_ge(rT_ready, gb + 1)
                        if not isinstance(gb, int) or gb >= 2:
                            pe.wait_ge(y_ready, gb - 1)
                        add_bias(pe, lin2[0:p, ub % 2, 0:t * D], onesB, b2_3, p, t)
                        for c in range(t):
                            mm = pe.matmul(lin2[0:p, ub % 2, c * D:(c + 1) * D],
                                           rT[:, ub % S, c * p:(c + 1) * p], W2T[:], start=False, stop=(c == t - 1))
                        mm.then_inc(lin2_ready, 1)

                walk(pe, NG, 3, body)


def add_bias(pe, to, onesB, bias_3, p, t):
    pe.matmul(to, onesB[:, 0:p], bias_3[:, 0:t].rearrange("r t d -> r (t d)"), start=True, stop=False)


def edges1(nc, sem, NB, E_LAST, N, x1, agg, edge_attr, side, soft_side, breaks, ident, idx_cols, dst_cols,
           Wq_s, Wk_s, Wv_s, We_s, onesB, bq_3, NG, group, geometry, skipped, Wskip_s, bskip_3):
    TH = T * H
    R = -(-NG // NB)
    assert R <= 2, "two PSUM banks are free for a moment in each step"
    with ExitStack() as part:
        def sb(name, shape, dt=F32):
            return part.enter_context(nc.sbuf_tensor(name, shape, dt))

        def ps(name, shape):
            return part.enter_context(nc.psum_tensor(name, shape, F32))

        idx = sb("e1_idx", [P, U, 3, T], I32)
        dst_f = sb("e1_dst_f", [P, U, T])
        xs = sb("e1_xs", [P, S, T, D])
        xd = sb("e1_xd", [P, S, T, D])
        ea = sb("e1_ea", [P, S, T, DE + 1])
        brk = sb("e1_brk", [TH, S, P + 1])
        xsT = sb("e1_xsT", [D, 2, T, P])
        xdT = sb("e1_xdT", [D, 2, T, P])
        eaT = sb("e1_eaT", [DE + 1, 2, T, P])
        q = sb("e1_q", [P, T * D])
        qk = sb("e1_qk", [P, T * D])
        logit = sb("e1_logit", [P, TH])
        run = sb("e1_run", [TH, P])
        top = sb("e1_top", [TH, P])
        diff = sb("e1_diff", [P, TH])
        ex = sb("e1_ex", [P, TH])
        exv = sb("e1_exv", [P, T, D])
        same = sb("e1_same", [P, T, P])
        rden = sb("e1_rden", [P, TH])
        att = sb("e1_att", [P, S, T, D])
        soft = sb("e1_soft", [P, S, T, 2 * H])
        x1_rows = sb("e1_x1_rows", [P, S, R, T, D])
        x1_T = sb("e1_x1_T", [D, R, T * P])
        skip = sb("e1_skip", [P, S, R, T, D])
        xsT_p, xdT_p, eaT_full = ps("e1_xsT_p", [D, T, P]), ps("e1_xdT_p", [D, T, P]), ps("e1_eaT_p", [P, T, P])
        eaT_p = eaT_full[0:DE + 1]
        x1_T_p = (xsT_p, xdT_p)
        skip_p = (eaT_full, xsT_p)
        k_p, v_p, q_p = ps("e1_k_p", [P, T * D]), ps("e1_v_p", [P, T * D]), ps("e1_q_p", [P, T * D])
        wide = ps("e1_wide", [P, T, P])
        misc = ps("e1_misc", [P, 512])
        logitT_p = misc[0:TH, 0:P]
        top_p = misc[:, P:P + TH]
        den_p = misc[:, 2 * P:2 * P + TH]

        idx_ready, dstf_ready = sem("e1_idx_ready"), sem("e1_dstf_ready")
        rows_in = [sem(f"e1_rows_in{s}") for s in range(S)]
        ea_in = [sem(f"e1_ea_in{s}") for s in range(S)]
        brk_in = [sem(f"e1_brk_in{s}") for s in range(S)]
        scattered = [sem(f"e1_scattered{s}") for s in range(S)]
        sided = [sem(f"e1_sided{s}") for s in range(S)]
        begun = sem("e1_begun")
        ea_set, turned_ready, xT_ready = sem("e1_ea_set"), sem("e1_turned_ready"), sem("e1_xT_ready")
        kq_ready, v_ready, q_ready, qk_ready, logit_ready = sem("e1_kq_ready"), sem("e1_v_ready"), sem("e1_q_ready"), sem("e1_qk_ready"), sem("e1_logit_ready")
        logitT_ready, run_ready, top_ready = sem("e1_logitT_ready"), sem("e1_run_ready"), sem("e1_top_ready")
        topT_ready, diff_ready, ex_ready = sem("e1_topT_ready"), sem("e1_diff_ready"), sem("e1_ex_ready")
        top_kept, spread_ready, same_ready = sem("e1_top_kept"), sem("e1_spread_ready"), sem("e1_same_ready")
        exv_ready, sums_ready, rden_ready, att_ready = sem("e1_exv_ready"), sem("e1_sums_ready"), sem("e1_rden_ready"), sem("e1_att_ready")
        den_kept = sem("e1_den_kept")
        x1_in = [sem(f"e1_x1_in{s}") for s in range(S)]
        skip_out = [sem(f"e1_skip_out{s}") for s in range(S)]
        x1_T_p_ready, x1_T_ready = sem("e1_x1_T_p_ready"), sem("e1_x1_T_ready")
        skip_p_ready, skip_ready = sem("e1_skip_p_ready"), sem("e1_skip_ready")

        def groups(i):
            return [(r, i * R + r) for r in range(R) if works(i * R + r, NG) and works(i, NB)]

        def passed(s, r):
            return sum(len(groups(s + m * S)) for m in range(r)) if isinstance(r, int) else r * R

        with nc.Block() as block:
            @block.gpsimd
            def _(pool):
                last_row = pool.to_reg(N - 1)
                pool.wait_ge(begun, 1)

                def body(j, u):
                    i = j * U + u
                    if works(i, NB):
                        now, free = ready_values(pool, i + 1, i - S + 1)
                        r, s = turn_of(j, u)
                        pool.wait_ge(begun, 1)
                        pool.wait_ge(idx_ready, now)
                        if late(r):
                            pool.wait_ge(turned_ready, free)
                        for t in range(T):
                            gather_rows(pool, xs[:, s, t, :], x1, idx[:, u, 0, t:t + 1].bitcast(U32), last_row)\
                                .then_inc(rows_in[s], 16)
                            gather_dst(pool, xd[:, s, t, :], x1, idx[:, u, 1, t:t + 1].bitcast(U32), last_row)\
                                .then_inc(rows_in[s], 16)
                    jb, ub, ib = back(j, u, AHEAD + 3)
                    if works(ib, NB):
                        (now,) = ready_values(pool, ib + 1)
                        pool.wait_ge(begun, 1)
                        pool.wait_ge(att_ready, now)
                        s = ub % S
                        for t in range(T):
                            scatter_rows(pool, agg, idx[:, ub, 2, t:t + 1].bitcast(U32), att[:, s, t, :], last_row)\
                                .then_inc(scattered[s], 16)

                walk(pool, NB, AHEAD + 3, body)
                for s in range(S):
                    pool.wait_ge(scattered[s], len(range(s, NB, S)) * T * 16)

            @block.sync
            def _(sp):
                sp.wait_ge(ea_set, 1)

                def body(j, u):
                    i = j * U + u
                    if works(i, NB):
                        r, s = turn_of(j, u)
                        if late(r):
                            sp.wait_ge(turned_ready, i - S + 1)
                        if isinstance(i, int) and i == NB - 1:
                            full, rest = E_LAST // P, E_LAST % P
                            if full:
                                sp.dma_start(ea[:, s, 0:full, 0:DE],
                                             edge_attr[i * B:i * B + full * P].rearrange("(t p) d -> p t d", p=P))\
                                  .then_inc(ea_in[s], 16)
                            if rest:
                                sp.dma_start(ea[0:rest, s, full, 0:DE],
                                             edge_attr[i * B + full * P:i * B + E_LAST]).then_inc(ea_in[s], 16)
                        else:
                            sp.dma_start(ea[:, s, :, 0:DE],
                                         edge_attr[bass.ds(i * B, B)].rearrange("(t p) d -> p t d", p=P))\
                              .then_inc(ea_in[s], 16)
                    jb, ub, ib = back(j, u, AHEAD)
                    if works(ib, NB):
                        r, s = turn_of(jb, ub)
                        if late(r):
                            sp.wait_ge(x1_T_p_ready, ib - S + 1)
                        for n, g in groups(ib):
                            p, t = geometry(g)
                            sp.dma_start(x1_rows[0:p, s, n, 0:t], group(x1, g)).then_inc(x1_in[s], 16)
                        if late(r):
                            sp.wait_ge(top_ready, ib - S + 1)
                        sp.dma_start(brk[:, s], breaks[bass.ds(ib, 1)].rearrange("b t h e -> (b t h) e"))\
                          .then_inc(brk_in[s], 16)
                    jb, ub, ib = back(j, u, AHEAD + 3)
                    if works(ib, NB):
                        s = ub % S
                        sp.wait_ge(skip_ready, ib + 1)
                        for n, g in groups(ib):
                            p, t = geometry(g)
                            sp.dma_start(group(skipped, g), skip[0:p, s, n, 0:t]).then_inc(skip_out[s], 16)
                        sp.wait_ge(att_ready, ib + 1)
                        sp.wait_ge(den_kept, ib + 1)
                        sp.wait_ge(top_kept, ib + 1)
                        for end, p in enumerate((0, P - 1)):
                            sp.dma_start(side_rows(side, ib, end), att[p:p + 1, s]).then_inc(sided[s], 16)
                            sp.dma_start(side_rows(soft_side, ib, end), soft[p:p + 1, s]).then_inc(sided[s], 16)

                walk(sp, NB, AHEAD + 3, body)
                for s in range(S):
                    sp.wait_ge(sided[s], len(range(s, NB, S)) * 64)
                    sp.wait_ge(skip_out[s], passed(s, len(range(s, NB, S))) * 16)

            @block.scalar
            def _(act):
                def body(j, u):
                    j, u, i = back(j, u, AHEAD)
                    jb, ub, ib = back(j, u, 1)
                    if works(ib, NB):
                        r, s = turn_of(jb, ub)
                        act.wait_ge(skip_p_ready, ib + 1)
                        if late(r) and groups(ib):
                            act.wait_ge(skip_out[s], passed(s, r) * 16)
                        for n, g in groups(ib):
                            p, t = geometry(g)
                            last = act.activation(skip[0:p, s, n, 0:t].rearrange("p t d -> p (t d)"),
                                                  skip_p[n][0:p, 0:t].rearrange("p t d -> p (t d)"), ACT.Copy)
                        if groups(ib):
                            last.then_inc(skip_ready, 1)
                        else:
                            act.sem_inc(skip_ready, 1)
                        act.wait_ge(kq_ready, ib + 1)
                        if not isinstance(ib, int) or ib >= 1:
                            act.wait_ge(qk_ready, ib)
                        act.activation(q[:], q_p[:], ACT.Copy).then_inc(q_ready, 1)
                    jb, ub, ib = back(j, u, 2)
                    if works(ib, NB):
                        act.wait_ge(diff_ready, ib + 1)
                        if not isinstance(ib, int) or ib >= 1:
                            act.wait_ge(sums_ready, ib)
                        act.activation(ex[:], diff[:], ACT.Exp, scale=float(C) ** -0.5).then_inc(ex_ready, 1)
                    if works(i, NB):
                        act.wait_ge(turned_ready, i + 1)
                        if not isinstance(i, int) or i >= 2:
                            act.wait_ge(v_ready, i - 1)
                        act.activation(xsT[:, u % 2], xsT_p[:], ACT.Copy)
                        act.activation(xdT[:, u % 2], xdT_p[:], ACT.Copy)
                        act.activation(eaT[:, u % 2], eaT_p[:], ACT.Copy).then_inc(xT_ready, 1)
                        act.wait_ge(x1_T_p_ready, i + 1)
                        for n, g in groups(i):
                            p, t = geometry(g)
                            last = act.activation(x1_T[:, n, 0:t * p], flat(x1_T_p[n])[:, 0:t * p], ACT.Copy)
                        if groups(i):
                            last.then_inc(x1_T_ready, 1)
                        else:
                            act.sem_inc(x1_T_ready, 1)

                walk(act, NB, AHEAD + 2, body)

            @block.vector
            def _(dve):
                dve.memset(ea[:, :, :, DE:DE + 1], 1.0).then_inc(ea_set, 1)
                dve.memset(xd[:], 0.0).then_inc(begun, 1)

                def body(j, u):
                    i = j * U + u
                    if works(i, NB):
                        if late(j):
                            r, s = turn_of(j, u)
                            dve.wait_ge(scattered[s], (r - 1) * T * 16)
                        prepare_batch(dve, i, u, idx, dst_f, idx_cols, dst_cols, idx_ready, dstf_ready)
                    j, u, i = back(j, u, AHEAD)
                    jb, ub, ib = back(j, u, 2)
                    if works(ib, NB):
                        r, s = turn_of(jb, ub)
                        dve.wait_ge(logitT_ready, ib + 1)
                        dve.wait_ge(brk_in[s], (r + 1) * 16)
                        dve.tensor_tensor_scan(run[:], brk[:, s, 0:P], logitT_p, LOW, ALU.add, ALU.max)\
                           .then_inc(run_ready, 1)
                        dve.wait_ge(run_ready, ib + 1)
                        dve.tensor_tensor_scan(top[:, ::-1], brk[:, s, 1:P + 1][:, ::-1], run[:, ::-1], LOW,
                                               ALU.add, ALU.max).then_inc(top_ready, 1)
                        dve.wait_ge(spread_ready, ib + 1)
                        dve.wait_ge(dstf_ready, ib + 1)
                        dve.tensor_tensor(same[:], wide[:], dst_f[:, ub].unsqueeze(2).to_broadcast([P, T, P]),
                                          ALU.is_equal).then_inc(same_ready, 1)
                        dve.wait_ge(topT_ready, ib + 1)
                        dve.tensor_tensor(diff[:], logit[:], top_p, ALU.subtract).then_inc(diff_ready, 1)
                        if late(r):
                            dve.wait_ge(sided[s], r * 64)
                        dve.tensor_copy(soft[:, s, :, 0:H], top_p.rearrange("p (t h) -> p t h", h=H))\
                           .then_inc(top_kept, 1)
                        dve.wait_ge(ex_ready, ib + 1)
                        dve.wait_ge(v_ready, ib + 1)
                        dve.tensor_tensor(exv[:].rearrange("p t (h c) -> p (t h) c", c=C),
                                          v_p[:].rearrange("p (n c) -> p n c", c=C),
                                          ex[:].unsqueeze(2).to_broadcast([P, TH, C]), ALU.mult)\
                           .then_inc(exv_ready, 1)
                    jb, ub, ib = back(j, u, 1)
                    if works(ib, NB):
                        dve.wait_ge(q_ready, ib + 1)
                        dve.tensor_tensor(qk[:], k_p[:], q[:], ALU.mult).then_inc(qk_ready, 1)
                        dve.wait_ge(qk_ready, ib + 1)
                        if not isinstance(ib, int) or ib >= 1:
                            dve.wait_ge(diff_ready, ib)
                        dve.tensor_reduce(logit[:], qk[:].rearrange("p (n c) -> p n c", c=C),
                                          mybir.AxisListType.X, ALU.add).then_inc(logit_ready, 1)
                    jb, ub, ib = back(j, u, 2)
                    if works(ib, NB):
                        r, s = turn_of(jb, ub)
                        dve.wait_ge(sums_ready, ib + 1)
                        dve.reciprocal(rden[:], den_p).then_inc(rden_ready, 1)
                        if late(r):
                            dve.wait_ge(scattered[s], r * T * 16)
                        dve.tensor_copy(soft[:, s, :, H:2 * H], den_p.rearrange("p (t h) -> p t h", h=H))\
                           .then_inc(den_kept, 1)
                        dve.wait_ge(rden_ready, ib + 1)
                        dve.tensor_tensor(att[:, s].rearrange("p t (h c) -> p (t h) c", c=C),
                                          wide[:].rearrange("p t (h c) -> p (t h) c", c=C),
                                          rden[:].unsqueeze(2).to_broadcast([P, TH, C]), ALU.mult)\
                           .then_inc(att_ready, 1)

                walk(dve, NB, AHEAD + 2, body)

            @block.tensor
            def _(pe):
                def body(j, u):
                    j, u, i = back(j, u, AHEAD)
                    jb, ub, ib = back(j, u, 2)
                    if works(ib, NB):
                        pe.wait_ge(logit_ready, ib + 1)
                        if not isinstance(ib, int) or ib >= 1:
                            pe.wait_ge(den_kept, ib)
                        pe.transpose(logitT_p, logit[:], ident[:]).then_inc(logitT_ready, 1)
                    jb, ub, ib = back(j, u, 1)
                    if works(ib, NB):
                        pe.wait_ge(x1_T_ready, ib + 1)
                        for n, g in groups(ib):
                            p, t = geometry(g)
                            to = flat(skip_p[n])
                            add_bias(pe, to[0:p, 0:t * D], onesB, bskip_3, p, t)
                            for c in range(t):
                                mm = pe.matmul(to[0:p, c * D:(c + 1) * D], x1_T[:, n, c * p:(c + 1) * p], Wskip_s[:],
                                               start=False, stop=(c == t - 1))
                        if groups(ib):
                            mm.then_inc(skip_p_ready, 1)
                        else:
                            pe.sem_inc(skip_p_ready, 1)
                    if works(ib, NB):
                        pe.wait_ge(xT_ready, ib + 1)
                        if not isinstance(ib, int) or ib >= 1:
                            pe.wait_ge(qk_ready, ib)
                        add_bias(pe, q_p[:], onesB, bq_3, P, T)
                        for t in range(T):
                            pe.matmul(q_p[:, t * D:(t + 1) * D], xdT[:, ub % 2, t], Wq_s[:], start=False,
                                      stop=(t == T - 1))
                        for t in range(T):
                            pe.matmul(k_p[:, t * D:(t + 1) * D], xsT[:, ub % 2, t], Wk_s[:], start=True, stop=False)
                            mm = pe.matmul(k_p[:, t * D:(t + 1) * D], eaT[:, ub % 2, t], We_s[:, 0, :],
                                           start=False, stop=True)
                        mm.then_inc(kq_ready, 1)
                    jb, ub, ib = back(j, u, 2)
                    if works(ib, NB):
                        pe.wait_ge(top_ready, ib + 1)
                        pe.wait_ge(dstf_ready, ib + 1)
                        if not isinstance(ib, int) or ib >= 1:
                            pe.wait_ge(att_ready, ib)
                        for t in range(T):
                            mm = pe.transpose(wide[:, t, :], dst_f[:, ub, t:t + 1].to_broadcast([P, P]), ident[:])
                        mm.then_inc(spread_ready, 1)
                        pe.transpose(top_p, top[:], ident[0:TH, 0:TH]).then_inc(topT_ready, 1)
                    if works(i, NB):
                        r, s = turn_of(j, u)
                        pe.wait_ge(rows_in[s], (r + 1) * 2 * T * 16)
                        split = 2 if isinstance(i, int) and i == NB - 1 and E_LAST >= P and E_LAST % P else 1
                        pe.wait_ge(ea_in[s], (r + split) * 16)
                        if not isinstance(i, int) or i >= 1:
                            pe.wait_ge(skip_ready, i)
                        for t in range(T):
                            pe.transpose(xsT_p[:, t], xs[:, s, t], ident[:])
                            pe.transpose(xdT_p[:, t], xd[:, s, t], ident[:])
                            mm = pe.transpose(eaT_p[:, t], ea[:, s, t], ident[:])
                        mm.then_inc(turned_ready, 1)
                    if works(ib, NB):
                        pe.wait_ge(exv_ready, ib + 1)
                        for t in range(T):
                            pe.matmul(wide[:, t, :], same[:, t, :], exv[:, t, :], start=True, stop=True)
                            mm = pe.matmul(den_p[:, t * H:(t + 1) * H], same[:, t, :], ex[:, t * H:(t + 1) * H],
                                           start=True, stop=True)
                        mm.then_inc(sums_ready, 1)
                    if works(i, NB):
                        r, s = turn_of(j, u)
                        pe.wait_ge(xT_ready, i + 1)
                        if groups(i):
                            pe.wait_ge(x1_in[s], passed(s, r) * 16 + len(groups(i)) * 16)
                        for n, g in groups(i):
                            p, t = geometry(g)
                            for c in range(t):
                                mm = pe.transpose(flat(x1_T_p[n])[:, c * p:(c + 1) * p], x1_rows[0:p, s, n, c],
                                                  ident[0:p, 0:p])
                        if groups(i):
                            mm.then_inc(x1_T_p_ready, 1)
                        else:
                            pe.sem_inc(x1_T_p_ready, 1)
                    jb, ub, ib = back(j, u, 1)
                    if works(ib, NB):
                        if not isinstance(ib, int) or ib >= 1:
                            pe.wait_ge(exv_ready, ib)
                        for t in range(T):
                            pe.matmul(v_p[:, t * D:(t + 1) * D], xsT[:, ub % 2, t], Wv_s[:], start=True, stop=False)
                            mm = pe.matmul(v_p[:, t * D:(t + 1) * D], eaT[:, ub % 2, t], We_s[:, 1, :],
                                           start=False, stop=True)
                        mm.then_inc(v_ready, 1)

                walk(pe, NB, AHEAD + 2, body)



def gather_dst(pool, rows, dram, index, last_row):
    return pool.indirect_dma_start(rows, None, dram, bass.IndirectOffsetOnAxis(index, 0), bounds_check=last_row,
                                   oob_is_err=False)


def joins1(nc, sem, NI, CI, PI, side, soft_side, agg, ident, same_item, count_item, row_item, head_of, N):
    with ExitStack() as part:
        def sb(name, shape, dt=F32):
            return part.enter_context(nc.sbuf_tensor(name, shape, dt))

        items = sb("j1_items", [PI, CI, D])
        soft = sb("j1_soft", [PI, CI, 2 * H])
        av = sb("j1_av", [D, NI])
        brk = sb("j1_brk", [H, NI + 1])
        top = sb("j1_top", [H, NI])
        run = sb("j1_run", [H, NI])
        whole = sb("j1_whole", [H, NI])
        den = sb("j1_den", [H, NI])
        w = sb("j1_w", [H, NI])
        num_run = sb("j1_num_run", [D, NI])
        den_run = sb("j1_den_run", [D, NI])
        W8 = -(-CI // 2)
        turn = part.enter_context(nc.psum_tensor("j1_turn", [P, 2, 2, 512], F32))
        s_in, s_turn, s_v, s_p = sem("j1_in"), sem("j1_turned"), sem("j1_vector_steps"), sem("j1_product_steps")
        s_a, s_rows, s_out, s_rt = sem("j1_act_steps"), sem("j1_rows"), sem("j1_out"), sem("j1_rows_turned")
        s_rt2 = sem("j1_scans")
        chunks = [(c * PI, min(CI, c + W8) * PI) for c in range(0, CI, W8)]
        assert all(b - a <= 512 for a, b in chunks) and H <= 32

        with nc.Block() as block:
            @block.sync
            def _(sp):
                sp.dma_start(items[:], side.rearrange("(c p) d -> p c d", p=PI)).then_inc(s_in, 16)
                sp.dma_start(soft[:], soft_side.rearrange("(c p) d -> p c d", p=PI)).then_inc(s_in, 16)

            @block.tensor
            def _(pe):
                def col(n, c):
                    k, r = divmod(c, W8)
                    return turn[:, n, k, r * PI:(r + 1) * PI]

                pe.wait_ge(s_in, 32)
                for c in range(CI):
                    pe.transpose(col(0, c)[0:H], soft[:, c, 0:H], ident[0:PI, 0:PI])
                    mm = pe.transpose(col(1, c)[0:H], soft[:, c, H:2 * H], ident[0:PI, 0:PI])
                mm.then_inc(s_turn, 1)
                pe.wait_ge(s_v, 2)
                for c in range(CI):
                    mm = pe.transpose(col(0, c), items[:, c, :], ident[0:PI, 0:PI])
                mm.then_inc(s_turn, 1)
                pe.wait_ge(s_v, 8)
                for k, (a, b) in enumerate(chunks):
                    mm = pe.matmul(turn[:, 1, k, 0:b - a], head_of[:], w[:, a:b], start=True, stop=True)
                mm.then_inc(s_p, 1)
                for c in range(CI):
                    if c == 0:
                        pe.wait_ge(s_v, 14)
                    elif c % 4 == 0:
                        pe.wait_ge(s_rows, c // 4)
                    mm = pe.transpose(turn[0:PI, 0, 0, (c % 4) * P:(c % 4 + 1) * P],
                                      av[:, c * PI:(c + 1) * PI], ident[:])
                    if c % 4 == 3 or c == CI - 1:
                        mm.then_inc(s_rt, 1)

            @block.scalar
            def _(act):
                act.wait_ge(s_v, 6)
                act.activation(w[:], w[:], ACT.Exp, scale=float(C) ** -0.5).then_inc(s_a, 1)

            @block.vector
            def _(dve):
                def halves(to, n, rows):
                    for k, (a, b) in enumerate(chunks):
                        last = dve.tensor_copy(to[:, a:b], turn[0:rows, n, k, 0:b - a])
                    return last

                dve.wait_ge(s_turn, 1)
                halves(top, 0, H).then_inc(s_v, 1)
                halves(den, 1, H).then_inc(s_v, 1)
                dve.memset(brk[:], LOW).then_inc(s_v, 1)
                dve.wait_ge(s_v, 3)
                dve.tensor_scalar(brk[:, 0:NI], same_item[0:H], -1.0, -LOW, ALU.add, ALU.mult).then_inc(s_v, 1)
                dve.wait_ge(s_v, 4)
                dve.tensor_tensor_scan(run[:], brk[:, 0:NI], top[:], LOW, ALU.add, ALU.max).then_inc(s_v, 1)
                dve.wait_ge(s_v, 5)
                dve.tensor_tensor_scan(whole[:, ::-1], brk[:, 1:NI + 1][:, ::-1], run[:, ::-1], LOW,
                                       ALU.add, ALU.max).then_inc(s_rt2, 1)
                dve.wait_ge(s_rt2, 1)
                dve.tensor_tensor(w[:], top[:], whole[:], ALU.subtract).then_inc(s_v, 1)
                dve.wait_ge(s_a, 1)
                dve.tensor_tensor(w[:], w[:], den[:], ALU.mult).then_inc(s_v, 1)
                dve.wait_ge(s_v, 7)
                dve.tensor_tensor(w[:], w[:], count_item[0:H], ALU.mult).then_inc(s_v, 1)
                dve.wait_ge(s_turn, 2)
                halves(av, 0, D).then_inc(s_v, 1)
                dve.wait_ge(s_p, 1)
                halves(den_run, 1, D).then_inc(s_v, 1)
                dve.wait_ge(s_v, 10)
                dve.tensor_tensor(av[:], av[:], den_run[:], ALU.mult).then_inc(s_v, 1)
                dve.wait_ge(s_v, 11)
                dve.tensor_tensor_scan(num_run[:], same_item[:], av[:], 0.0, ALU.mult, ALU.add).then_inc(s_v, 1)
                dve.wait_ge(s_v, 12)
                dve.tensor_tensor_scan(av[:], same_item[:], den_run[:], 0.0, ALU.mult, ALU.add).then_inc(s_rt2, 1)
                dve.wait_ge(s_rt2, 2)
                dve.reciprocal(den_run[:], av[:]).then_inc(s_v, 1)
                dve.wait_ge(s_v, 13)
                dve.tensor_tensor(av[:], num_run[:], den_run[:], ALU.mult).then_inc(s_v, 1)
                for c in range(0, CI, 4):
                    n = min(4, CI - c)
                    dve.wait_ge(s_rt, c // 4 + 1)
                    dve.tensor_copy(items[:, c:c + n, :].rearrange("p c d -> p (c d)"), turn[0:PI, 0, 0, 0:n * P])\
                       .then_inc(s_rows, 1)

            @block.gpsimd
            def _(pool):
                for c in range(CI):
                    if c % 4 == 0:
                        pool.wait_ge(s_rows, c // 4 + 1)
                    scatter_rows(pool, agg, row_item[:, c:c + 1].bitcast(U32), items[:, c, :], N - 1)\
                        .then_inc(s_out, 16)
                pool.wait_ge(s_out, CI * 16)


def nodes1(nc, sem, NG, group, geometry, x1, skipped, agg, out, half, root_d, ident, Wf1_s, Wf2_s, onesB,
           bf2_3, g1_col, b1_col, bf1_col, g1_row, g2_row, b2n_row):
    F = FF // D
    with ExitStack() as part:
        def sb(name, shape, dt=F32):
            return part.enter_context(nc.sbuf_tensor(name, shape, dt))

        def ps(name, shape):
            return part.enter_context(nc.psum_tensor(name, shape, F32))

        xs, ags = sb("n1_x", [P, U, T, D]), sb("n1_agg", [P, U, T, D])
        skips = sb("n1_skip", [P, U, T, D])
        y, z = sb("n1_y", [P, 2, T, D]), sb("n1_z", [P, S, T, D])
        zg = sb("n1_zg", [P, S, T, D])
        xb = sb("n1_xb", [P, U, T, D])
        hT = sb("n1_hT", [D, 2, T * P])
        act_T = sb("n1_act_T", [D, 2, F, T * P])
        w, wn = sb("n1_w", [P, 2, T, D]), sb("n1_wn", [P, 2, T, D])
        wg = sb("n1_wg", [P, 2, T, D])
        res, o = sb("n1_res", [P, S, T, D]), sb("n1_o", [P, S, T, D])
        zT_p, lin2_p = ps("n1_zT_p", [D, T * P]), ps("n1_lin2_p", [P, 2, T * D])
        lin1_p = ps("n1_lin1_p", [D, F, T * P])
        norms = Norms(part, nc, sem, "n1_norms", 3)

        rows_in = [sem(f"n1_rows_in{u}") for u in range(U)]
        stored = [sem(f"n1_stored{s}") for s in range(S)]
        y_ready, z_ready, zT_p_ready = sem("n1_y_ready"), sem("n1_z_ready"), sem("n1_zT_p_ready")
        hT_ready, lin1_ready, gelu_ready = sem("n1_hT_ready"), sem("n1_lin1_ready"), sem("n1_gelu_ready")
        lin2_ready, w_ready, wn_ready = sem("n1_lin2_ready"), sem("n1_w_ready"), sem("n1_wn_ready")
        zg_ready, wg_ready, xb_ready = sem("n1_zg_ready"), sem("n1_wg_ready"), sem("n1_xb_ready")
        r_ready, o_ready = sem("n1_r_ready"), sem("n1_o_ready")

        def rows(psum, p, t):
            return psum[0:p, 0:t * D].rearrange("p (t d) -> p t d", d=D)

        with nc.Block() as block:
            @block.sync
            def _(sp):
                def body(j, u):
                    g = j * U + u
                    if works(g, NG):
                        p, t = geometry(g)
                        if late(j):
                            sp.wait_ge(xb_ready, g - U + 1)
                            sp.wait_ge(y_ready, g - U + 1)
                        sp.dma_start(xs[0:p, u, 0:t], group(x1, g)).then_inc(rows_in[u], 16)
                        sp.dma_start(skips[0:p, u, 0:t], group(skipped, g)).then_inc(rows_in[u], 16)
                        sp.dma_start(ags[0:p, u, 0:t], group(agg, g)).then_inc(rows_in[u], 16)
                    jb, ub, gb = back(j, u, 9)
                    if works(gb, NG):
                        p, t = geometry(gb)
                        sp.wait_ge(o_ready, gb + 1)
                        sp.dma_start(group(out, gb), o[0:p, ub % S, 0:t]).then_inc(stored[ub % S], 16)

                walk(sp, NG, 9, body)
                for s in range(S):
                    sp.wait_ge(stored[s], len(range(s, NG, S)) * 16)

            @block.tensor
            def _(pe):
                def body(j, u):
                    jb, ub, gb = back(j, u, 2)
                    if works(gb, NG):
                        p, t = geometry(gb)
                        pe.wait_ge(z_ready, gb + 1)
                        if not isinstance(gb, int) or gb >= 1:
                            pe.wait_ge(hT_ready, gb)
                        for c in range(t):
                            mm = pe.transpose(zT_p[:, c * p:(c + 1) * p], z[0:p, ub % S, c, :], ident[0:p, 0:p])
                        mm.then_inc(zT_p_ready, 1)
                    jb, ub, gb = back(j, u, 4)
                    if works(gb, NG):
                        p, t = geometry(gb)
                        pe.wait_ge(gelu_ready, F * gb + F)
                        if not isinstance(gb, int) or gb >= 2:
                            pe.wait_ge(w_ready, gb - 1)
                        add_bias(pe, lin2_p[0:p, ub % 2, 0:t * D], onesB, bf2_3, p, t)
                        for c in range(t):
                            for f in range(F):
                                mm = pe.matmul(lin2_p[0:p, ub % 2, c * D:(c + 1) * D],
                                               act_T[:, ub % 2, f, c * p:(c + 1) * p], Wf2_s[:, f, :],
                                               start=False, stop=(c == t - 1 and f == F - 1))
                        mm.then_inc(lin2_ready, 1)
                    jb, ub, gb = back(j, u, 2)
                    if works(gb, NG):
                        p, t = geometry(gb)
                        pe.wait_ge(hT_ready, gb + 1)
                        for f in range(F):
                            if not isinstance(gb, int) or gb >= 1:
                                pe.wait_ge(gelu_ready, F * gb - F + f + 1)
                            pe.matmul(lin1_p[:, f, 0:t * p], Wf1_s[:, f * D:(f + 1) * D], hT[:, ub % 2, 0:t * p],
                                      start=True, stop=True).then_inc(lin1_ready, 1)

                walk(pe, NG, 4, body)

            @block.scalar
            def _(act):
                def body(j, u):
                    jb, ub, gb = back(j, u, 6)
                    if works(gb, NG):
                        p, t = geometry(gb)
                        if not isinstance(gb, int) or gb >= 2:
                            act.wait_ge(wg_ready, gb - 1)
                        norms_apply_act(act, norms, 1, wn[:, ub % 2], w[:, ub % 2], p, t, j, u, wn_ready)
                    jb, ub, gb = back(j, u, 2)
                    if works(gb, NG):
                        p, t = geometry(gb)
                        act.wait_ge(zT_p_ready, gb + 1)
                        if not isinstance(gb, int) or gb >= 2:
                            act.wait_ge(lin1_ready, F * gb - F)
                        act.activation(hT[:, ub % 2, 0:t * p], zT_p[:, 0:t * p], ACT.Identity, bias=b1_col[:],
                                       scale=g1_col[:]).then_inc(hT_ready, 1)
                    jo, uo, go = back(j, u, 8)
                    if works(go, NG):
                        po, to = geometry(go)
                        r, s = turn_of(jo, uo)
                        if late(r):
                            act.wait_ge(stored[s], r * 16)
                        norms_apply_act(act, norms, 2, o[:, s], res[:, s], po, to, j, u, o_ready)
                    if works(gb, NG):
                        if not isinstance(gb, int) or gb >= 2:
                            act.wait_ge(lin2_ready, gb - 1)
                        for f in range(F):
                            act.wait_ge(lin1_ready, F * gb + f + 1)
                            act.activation(act_T[:, ub % 2, f, 0:t * p], lin1_p[:, f, 0:t * p], ACT.Gelu,
                                           bias=bf1_col[:, f:f + 1]).then_inc(gelu_ready, 1)

                walk(act, NG, 8, body)

            @block.vector
            def _(dve):
                dve.memset(norms.stat[:], 1.0).then_inc(norms.set, 1)
                dve.wait_ge(norms.set, 1)

                def body(j, u):
                    g = j * U + u
                    jc, uc, gc = back(j, u, 7)
                    if works(gc, NG):
                        pc, tc = geometry(gc)
                        r, s = turn_of(jc, uc)
                        dve.wait_ge(wg_ready, gc + 1)
                        dve.wait_ge(xb_ready, gc + 1)
                        if late(r):
                            dve.wait_ge(o_ready, gc - S + 1)
                        dve.tensor_tensor(res[0:pc, s, 0:tc], wg[0:pc, uc % 2, 0:tc], xb[0:pc, uc, 0:tc], ALU.add)\
                           .then_inc(r_ready, 1)
                    jb, ub, gb = back(j, u, 5)
                    if works(gb, NG):
                        pb, tb = geometry(gb)
                        dve.wait_ge(lin2_ready, gb + 1)
                        dve.wait_ge(zg_ready, gb + 1)
                        if not isinstance(gb, int) or gb >= 2:
                            dve.wait_ge(wn_ready, gb - 1)
                        dve.tensor_tensor(w[0:pb, ub % 2, 0:tb], rows(lin2_p[:, ub % 2], pb, tb), zg[0:pb, ub % S, 0:tb],
                                          ALU.add).then_inc(w_ready, 1)
                    if works(g, NG):
                        p, t = geometry(g)
                        dve.wait_ge(rows_in[u], (j + 1) * 48)
                        dve.tensor_tensor(y[0:p, u % 2, 0:t], skips[0:p, u, 0:t], ags[0:p, u, 0:t], ALU.add)\
                           .then_inc(y_ready, 1)
                    if works(gc, NG):
                        dve.wait_ge(r_ready, gc + 1)
                        norms_stat(dve, norms, 2, res[:, uc % S], pc, tc, u)
                    if works(gb, NG):
                        dve.wait_ge(w_ready, gb + 1)
                        norms_stat(dve, norms, 1, w[:, ub % 2], pb, tb, u)
                    ja, ua, ga = back(j, u, 1)
                    if works(ga, NG):
                        pa, ta = geometry(ga)
                        r, s = turn_of(ja, ua)
                        if late(r):
                            dve.wait_ge(zT_p_ready, ga - S + 1)
                            dve.wait_ge(zg_ready, ga - S + 1)
                        dve.wait_ge(norms.ready, ga + 1)
                        for c in range(ta):
                            last = dve.tensor_scalar(z[0:pa, s, c, :], y[0:pa, ua % 2, c, :],
                                                     norms.rstd[0:pa, ua, 0, c:c + 1],
                                                     norms.shift[0:pa, ua, 0, c:c + 1], ALU.mult, ALU.add)
                        last.then_inc(z_ready, 1)
                    if works(g, NG):
                        dve.wait_ge(y_ready, g + 1)
                        norms_stat(dve, norms, 0, y[:, u % 2], p, t, u)
                    if isinstance(g, int):
                        norms_spread(dve, norms, u, g, sum(max(0, min(k + 1, NG)) for k in (g, g - 5, g - 7)))
                    else:
                        norms_spread(dve, norms, u, g, 3 * g + 3 - 5 - 7)

                walk(dve, NG, 7, body)

            @block.gpsimd
            def _(pool):
                def body(j, u):
                    g = j * U + u
                    if works(g, NG):
                        p, t = geometry(g)
                        if late(j):
                            pool.wait_ge(r_ready, g - U + 1)
                        pool.wait_ge(rows_in[u], (j + 1) * 48)
                        pool.tensor_tensor(xb[0:p, u, 0:t], xs[0:p, u, 0:t], b2n_row[0:p, 0:t], ALU.add)\
                            .then_inc(xb_ready, 1)
                    jb, ub, gb = back(j, u, 6)
                    if works(gb, NG):
                        p, t = geometry(gb)
                        pool.wait_ge(wn_ready, gb + 1)
                        if not isinstance(gb, int) or gb >= 2:
                            pool.wait_ge(r_ready, gb - 1)
                        pool.tensor_tensor(wg[0:p, ub % 2, 0:t], wn[0:p, ub % 2, 0:t], g2_row[0:p, 0:t],
                                           ALU.mult).then_inc(wg_ready, 1)
                    jb, ub, gb = back(j, u, 1)
                    if works(gb, NG):
                        p, t = geometry(gb)
                        r, s = turn_of(jb, ub)
                        pool.wait_ge(z_ready, gb + 1)
                        if late(r):
                            pool.wait_ge(w_ready, gb - S + 1)
                        pool.tensor_tensor(zg[0:p, s, 0:t], z[0:p, s, 0:t], g1_row[0:p, 0:t], ALU.mult)\
                            .then_inc(zg_ready, 1)
                    norms_root(pool, norms, u, j * U + u, half, root_d)

                walk(pool, NG, 7, body)



_INS = ['x', 'src', 'dst', 'edge_attr_64', 'L0_gnn_W1', 'L0_gnn_gamma', 'L0_gnn_beta', 'L0_gnn_W2', 'L0_gnn_b2',
        'L0_gnn_eps', 'L1_gnn_Wq', 'L1_gnn_bq', 'L1_gnn_Wk', 'L1_gnn_bk', 'L1_gnn_Wv', 'L1_gnn_bv', 'L1_gnn_We',
        'L1_gnn_Wskip', 'L1_gnn_bskip', 'L1_gnn_g1', 'L1_gnn_b1', 'L1_gnn_g2', 'L1_gnn_b2', 'L1_gnn_Wf1',
        'L1_gnn_bf1', 'L1_gnn_Wf2', 'L1_gnn_bf2']


def kernel(**inputs):
    import numpy as _np
    import concourse.bacc as _bacc
    from concourse.bass_utils import run_bass_kernel_spmd as _run

    nc = _bacc.Bacc("TRN2", target_bir_lowering=False, num_devices=1)
    arrays, args = {}, []
    for name in _INS:
        a = _np.ascontiguousarray(inputs[name])
        if a.ndim == 0:
            a = a.reshape(1)
        arrays[f"in_{name}"] = a
        args.append(nc.dram_tensor(f"in_{name}", a.shape, mybir.dt.from_np(a.dtype), kind="ExternalInput").ap())
    n = inputs['x'].shape[0]
    args.append(nc.dram_tensor("out_0", (n, D), F32, kind="ExternalOutput").ap())
    build(nc, *args)
    r = _run(nc, [arrays], core_ids=[0])
    return r.results[0]["out_0"]
```
